# Optimizing a Trainium2 kernel written in Bass

```python
import numpy as np
import jax
import jax.numpy as jnp

def _softmax(x, axis=-1):
    return jax.nn.softmax(x, axis=axis)

def _gelu(x):
    return jax.nn.gelu(x, approximate=True)

def _silu(x):
    return jax.nn.silu(x)

def _sigmoid(x):
    return jax.nn.sigmoid(x)

def _layernorm(x, axis=-1, eps=1e-05):
    m = jnp.mean(x, axis=axis, keepdims=True)
    v = jnp.var(x, axis=axis, keepdims=True)
    return (x - m) / jnp.sqrt(v + eps)

def _scatter_add(tgt, idx, src, axis=0):
    return tgt.at[idx].add(src)

def _segment_sum(src, seg, n):
    return jax.ops.segment_sum(src, seg, n)
kernel_name = 'mk_xattn_seq_d4_seqx_r8_5ddb6a'

def setup_inputs(seed: int=0):
    np.random.seed(seed)
    _w = jnp.asarray

    def _rec_inputs():
        import jax
        import jax.numpy as jnp
        _rk = jax.random.key(seed)
        x = -0.0002928 + 1 * jax.random.normal(jax.random.fold_in(_rk, 1), (16, 128, 256), jnp.float32)
        _lenS = 128 - jax.random.randint(jax.random.fold_in(_rk, 7), (16,), 0, max(1, 128 // 4) + 1, jnp.int32)
        _lenS2 = 128 - jax.random.randint(jax.random.fold_in(_rk, 8), (16,), 0, max(1, 128 // 4) + 1, jnp.int32)
        _ctx_2048P = jax.random.normal(jax.random.fold_in(_rk, 11), (16, 16, 256), jnp.float32)
        _ctx_2048c = jax.random.dirichlet(jax.random.fold_in(_rk, 511), 0.3 * jnp.ones((16,), jnp.float32), (16, 128))
        _ctx_2048t = jnp.einsum('bsk,bkd->bsd', _ctx_2048c, _ctx_2048P)
        _ctx_2048t = _ctx_2048t * jax.lax.rsqrt(jnp.mean(jnp.square(_ctx_2048t)) + 1e-12) * 0.953939
        ctx_2048 = -1.39393e-06 + 0.999914 * (_ctx_2048t + 0.3 * jax.random.normal(jax.random.fold_in(_rk, 611), (16, 128, 256), jnp.float32))
        _validS = jnp.arange(128)[None, :] < _lenS[:, None]
        _validS2 = jnp.arange(128)[None, :] < _lenS2[:, None]
        _causal = jnp.tril(jnp.ones((128, 128), dtype=bool))
        mask_BxS2_ik0 = jnp.where(jnp.broadcast_to(_validS2[:, :], (16, 128)), 0, 1).astype(jnp.int32)
        mask_1x1xSxS2_fc1 = jnp.where(jnp.broadcast_to(_validS2[0:1, None, None, :], (1, 1, 128, 128)), 1.0, 0.0).astype(jnp.float32)
        mask_Bx1xSxS2_ff1 = jnp.where(jnp.ones((16, 1, 128, 128), dtype=bool), 1.0, 0.0).astype(jnp.float32)
        return (x, ctx_2048, mask_BxS2_ik0, mask_1x1xSxS2_fc1, mask_Bx1xSxS2_ff1)
    x, ctx_2048, mask_BxS2_ik0, mask_1x1xSxS2_fc1, mask_Bx1xSxS2_ff1 = _rec_inputs()

    def _L0_xattn_setup():
        import math
        import jax, jax.numpy as jnp
        import numpy as np
        C = 128
        H = 16
        DH = C // H
        EPS = 1e-05

        def pos_enc(c, T, dtype):
            pos = jnp.arange(T, dtype=jnp.float32)[:, None]
            div = jnp.exp(jnp.arange(0, c, 2, dtype=jnp.float32) * (-math.log(10000.0) / c))
            ang = pos * div
            pe = jnp.zeros((T, c), dtype=jnp.float32)
            pe = pe.at[:, 0::2].set(jnp.sin(ang)).at[:, 1::2].set(jnp.cos(ang))
            return pe.T.astype(dtype)

        def layer_norm(x, g, b):
            mu = jnp.mean(x, axis=-1, keepdims=True)
            var = jnp.mean(jnp.square(x - mu), axis=-1, keepdims=True)
            return (x - mu) * jax.lax.rsqrt(var + EPS) * g + b
        key = jax.random.key(seed)
        ks = jax.random.split(key, 16)
        s = 1.0 / math.sqrt(C)
        inp = {'zt_prev': jax.random.normal(ks[0], (2, C, 256), jnp.float32), 'za': jax.random.normal(ks[1], (2, C, 256), jnp.float32), 'Wq': jax.random.normal(ks[2], (C, C), jnp.float32) * s, 'Wk': jax.random.normal(ks[3], (C, C), jnp.float32) * s, 'Wv': jax.random.normal(ks[4], (C, C), jnp.float32) * s, 'Wo': jax.random.normal(ks[5], (C, C), jnp.float32) * s, 'ln_q_g': jnp.ones((C,), jnp.float32), 'ln_q_b': jnp.zeros((C,), jnp.float32), 'ln_kv_g': jnp.ones((C,), jnp.float32), 'ln_kv_b': jnp.zeros((C,), jnp.float32), 'ffn_ln_g': jnp.ones((C,), jnp.float32), 'ffn_ln_b': jnp.zeros((C,), jnp.float32), 'W1': jax.random.normal(ks[6], (C, 2 * C), jnp.float32) * s, 'b1': jnp.zeros((2 * C,), jnp.float32), 'W2': jax.random.normal(ks[7], (2 * C, C), jnp.float32) * (1.0 / math.sqrt(2 * C)), 'b2': jnp.zeros((C,), jnp.float32)}
        return inp
    _L0_xattn_all = _L0_xattn_setup()
    _L0_xattn_in = {k: v for k, v in _L0_xattn_all.items() if k in ('Wq', 'Wk', 'Wv', 'Wo', 'ln_q_g', 'ln_q_b', 'ln_kv_g', 'ln_kv_b', 'ffn_ln_g', 'ffn_ln_b', 'W1', 'b1', 'W2', 'b2')}
    del _L0_xattn_all

    def _L1_xattn_setup():
        import jax, jax.numpy as jnp
        import numpy as np
        B, P, K, H, NH = (4, 256, 32, 256, 16)
        DH = H // NH
        EPS = 1e-06

        def rmsnorm(x, w):
            var = jnp.mean(jnp.square(x), axis=-1, keepdims=True)
            return x * jax.lax.rsqrt(var + EPS) * w
        key = jax.random.key(seed)
        ks = jax.random.split(key, 12)
        s = 0.02
        return {'x': jax.random.normal(ks[0], (B, P, H), jnp.float32), 'latents': jax.random.normal(ks[1], (B, K, H), jnp.float32), 'attention_mask': jax.random.randint(ks[2], (B, P), 0, 2, jnp.int32), 'q_w': s * jax.random.normal(ks[3], (H, H), jnp.float32), 'q_b': jnp.zeros((H,), jnp.float32), 'kv_w': s * jax.random.normal(ks[4], (H, 2 * H), jnp.float32), 'kv_b': jnp.zeros((2 * H,), jnp.float32), 'out_w': s * jax.random.normal(ks[5], (H, H), jnp.float32), 'out_b': jnp.zeros((H,), jnp.float32), 'postnorm_w': jnp.ones((H,), jnp.float32), 'mlp_w1': s * jax.random.normal(ks[6], (H, 4 * H), jnp.float32), 'mlp_b1': jnp.zeros((4 * H,), jnp.float32), 'mlp_w2': s * jax.random.normal(ks[7], (4 * H, H), jnp.float32), 'mlp_b2': jnp.zeros((H,), jnp.float32)}
    _L1_xattn_all = _L1_xattn_setup()
    _L1_xattn_in = {k: v for k, v in _L1_xattn_all.items() if k in ('q_w', 'q_b', 'kv_w', 'kv_b', 'out_w', 'out_b', 'postnorm_w', 'mlp_w1', 'mlp_b1', 'mlp_w2', 'mlp_b2')}
    del _L1_xattn_all

    def _L2_xattn_setup():
        import jax, jax.numpy as jnp
        import numpy as np
        B, Q, S1, S2 = (4, 32, 256, 256)
        D, H, K, F = (256, 16, 128, 1024)
        LN_EPS = 1e-05

        def _layer_norm(x, scale, offset):
            mu = jnp.mean(x, axis=-1, keepdims=True)
            var = jnp.var(x, axis=-1, keepdims=True)
            return (x - mu) * jax.lax.rsqrt(var + LN_EPS) * scale + offset

        def _cross_attention(q_in, kv_in, wq, bq, wk, bk, wv, bv, wo, bo, bias_k, bias_v):
            b, q_len, _ = q_in.shape
            t = kv_in.shape[1]
            qh = (q_in @ wq + bq).reshape(b, q_len, H, K)
            kh = (kv_in @ wk + bk).reshape(b, t, H, K)
            vh = (kv_in @ wv + bv).reshape(b, t, H, K)
            kh = jnp.concatenate([kh, jnp.broadcast_to(bias_k, (b, 1, H, K))], axis=1)
            vh = jnp.concatenate([vh, jnp.broadcast_to(bias_v, (b, 1, H, K))], axis=1)
            scale = jnp.sqrt(jnp.asarray(K, q_in.dtype))
            logits = jnp.einsum('bqhk,bthk->bhqt', qh, kh) / scale
            weights = jax.nn.softmax(logits, axis=-1)
            ctx = jnp.einsum('bhqt,bthk->bqhk', weights, vh).reshape(b, q_len, H * K)
            return ctx @ wo + bo

        def _forward(x, xf_1, xf_2, ln1_scale, ln1_offset, wq1, bq1, wk1, bk1, wv1, bv1, wo1, bo1, bias_k1, bias_v1, ln2_scale, ln2_offset, wq2, bq2, wk2, bk2, wv2, bv2, wo2, bo2, bias_k2, bias_v2, ln_mlp_scale, ln_mlp_offset, w_fc1, b_fc1, w_fc2, b_fc2):
            res = x
            h = _layer_norm(x, ln1_scale, ln1_offset)
            x = res + _cross_attention(h, xf_1, wq1, bq1, wk1, bk1, wv1, bv1, wo1, bo1, bias_k1, bias_v1)
            res = x
            h = _layer_norm(x, ln2_scale, ln2_offset)
            x = res + _cross_attention(h, xf_2, wq2, bq2, wk2, bk2, wv2, bv2, wo2, bo2, bias_k2, bias_v2)
            h = _layer_norm(x, ln_mlp_scale, ln_mlp_offset)
            h = jax.nn.gelu(h @ w_fc1 + b_fc1, approximate=False) @ w_fc2 + b_fc2
            return x + h
        key = jax.random.key(seed)
        ks = iter(jax.random.split(key, 64))

        def rn(shape, s=0.02):
            return jax.random.normal(next(ks), shape, jnp.float32) * s
        inp = {'x': rn((B, Q, D), 1.0), 'xf_1': rn((B, S1, D), 1.0), 'xf_2': rn((B, S2, D), 1.0)}
        for i in (1, 2):
            inp[f'ln{i}_scale'] = jnp.ones((D,), jnp.float32)
            inp[f'ln{i}_offset'] = jnp.zeros((D,), jnp.float32)
            inp[f'wq{i}'] = rn((D, H * K))
            inp[f'bq{i}'] = jnp.zeros((H * K,), jnp.float32)
            inp[f'wk{i}'] = rn((D, H * K))
            inp[f'bk{i}'] = jnp.zeros((H * K,), jnp.float32)
            inp[f'wv{i}'] = rn((D, H * K))
            inp[f'bv{i}'] = jnp.zeros((H * K,), jnp.float32)
            inp[f'wo{i}'] = rn((H * K, D))
            inp[f'bo{i}'] = jnp.zeros((D,), jnp.float32)
            inp[f'bias_k{i}'] = rn((1, 1, H, K))
            inp[f'bias_v{i}'] = rn((1, 1, H, K))
        inp['ln_mlp_scale'] = jnp.ones((D,), jnp.float32)
        inp['ln_mlp_offset'] = jnp.zeros((D,), jnp.float32)
        inp['w_fc1'] = rn((D, F))
        inp['b_fc1'] = jnp.zeros((F,), jnp.float32)
        inp['w_fc2'] = rn((F, D))
        inp['b_fc2'] = jnp.zeros((D,), jnp.float32)
        return inp
    _L2_xattn_all = _L2_xattn_setup()
    _L2_xattn_in = {k: v for k, v in _L2_xattn_all.items() if k in ('ln1_scale', 'ln1_offset', 'wq1', 'bq1', 'wk1', 'bk1', 'wv1', 'bv1', 'wo1', 'bo1', 'bias_k1', 'bias_v1', 'ln2_scale', 'ln2_offset', 'wq2', 'bq2', 'wk2', 'bk2', 'wv2', 'bv2', 'wo2', 'bo2', 'bias_k2', 'bias_v2', 'ln_mlp_scale', 'ln_mlp_offset', 'w_fc1', 'b_fc1', 'w_fc2', 'b_fc2')}
    del _L2_xattn_all

    def _L3_xattn_setup():
        import jax, jax.numpy as jnp
        import numpy as np
        H = 256
        NH = 16
        HD = H // NH
        EPS = 1e-05

        def gelu(x):
            return 0.5 * x * (1.0 + jnp.tanh(0.7978845608028654 * x * (1.0 + 0.044715 * x * x)))

        def layernorm(x, scale, bias):
            m = jnp.mean(x, axis=-1, keepdims=True)
            v = jnp.mean(jnp.square(x - m), axis=-1, keepdims=True)
            return (x - m) * jax.lax.rsqrt(v + EPS) * scale + bias

        def split_heads(x):
            b, s, _ = x.shape
            return x.reshape(b, s, NH, HD).transpose(0, 2, 1, 3)

        def merge_heads(x):
            b, nh, s, hd = x.shape
            return x.transpose(0, 2, 1, 3).reshape(b, s, nh * hd)

        def attention(q, k, v, mask):
            scores = jnp.einsum('bhqd,bhkd->bhqk', q, k) / jnp.sqrt(jnp.float32(HD))
            scores = scores * mask - 10000.0 * (1.0 - mask)
            probs = jax.nn.softmax(scores, axis=-1)
            return jnp.einsum('bhqk,bhkd->bhqd', probs, v)
        key = jax.random.key(seed)
        ks = jax.random.split(key, 16)
        b, s, t = (2, 128, 128)
        w = lambda k, i, o: jax.random.normal(k, (i, o), jnp.float32) * 0.02
        inp = {'hidden_states': jax.random.normal(ks[0], (b, s, H), jnp.float32), 'encoder_states': jax.random.normal(ks[1], (b, t, H), jnp.float32), 'ltor_mask': jnp.tril(jnp.ones((1, 1, s, s), jnp.float32)), 'cross_mask': jnp.ones((b, 1, s, t), jnp.float32), 'ln1_s': jnp.ones((H,), jnp.float32), 'ln1_b': jnp.zeros((H,), jnp.float32), 'w_qkv': w(ks[2], H, 3 * H), 'b_qkv': jnp.zeros((3 * H,), jnp.float32), 'w_ao': w(ks[3], H, H), 'b_ao': jnp.zeros((H,), jnp.float32), 'ln2_s': jnp.ones((H,), jnp.float32), 'ln2_b': jnp.zeros((H,), jnp.float32), 'w_q': w(ks[4], H, H), 'b_q': jnp.zeros((H,), jnp.float32), 'w_kv': w(ks[5], H, 2 * H), 'b_kv': jnp.zeros((2 * H,), jnp.float32), 'w_co': w(ks[6], H, H), 'b_co': jnp.zeros((H,), jnp.float32), 'ln3_s': jnp.ones((H,), jnp.float32), 'ln3_b': jnp.zeros((H,), jnp.float32), 'w1': w(ks[7], H, 4 * H), 'b1': jnp.zeros((4 * H,), jnp.float32), 'w2': w(ks[8], 4 * H, H), 'b2': jnp.zeros((H,), jnp.float32)}
        return inp
    _L3_xattn_all = _L3_xattn_setup()
    _L3_xattn_in = {k: v for k, v in _L3_xattn_all.items() if k in ('ln1_s', 'ln1_b', 'w_qkv', 'b_qkv', 'w_ao', 'b_ao', 'ln2_s', 'ln2_b', 'w_q', 'b_q', 'w_kv', 'b_kv', 'w_co', 'b_co', 'ln3_s', 'ln3_b', 'w1', 'b1', 'w2', 'b2')}
    del _L3_xattn_all
    return {'x': x, 'ctx_2048': ctx_2048, 'mask_BxS2_ik0': mask_BxS2_ik0, 'mask_1x1xSxS2_fc1': mask_1x1xSxS2_fc1, 'mask_Bx1xSxS2_ff1': mask_Bx1xSxS2_ff1, 'L0_xattn_Wq': _L0_xattn_in['Wq'], 'L0_xattn_Wk': _L0_xattn_in['Wk'], 'L0_xattn_Wv': _L0_xattn_in['Wv'], 'L0_xattn_Wo': _L0_xattn_in['Wo'], 'L0_xattn_ln_q_g': _L0_xattn_in['ln_q_g'], 'L0_xattn_ln_q_b': _L0_xattn_in['ln_q_b'], 'L0_xattn_ln_kv_g': _L0_xattn_in['ln_kv_g'], 'L0_xattn_ln_kv_b': _L0_xattn_in['ln_kv_b'], 'L0_xattn_ffn_ln_g': _L0_xattn_in['ffn_ln_g'], 'L0_xattn_ffn_ln_b': _L0_xattn_in['ffn_ln_b'], 'L0_xattn_W1': _L0_xattn_in['W1'], 'L0_xattn_b1': _L0_xattn_in['b1'], 'L0_xattn_W2': _L0_xattn_in['W2'], 'L0_xattn_b2': _L0_xattn_in['b2'], 'L1_xattn_q_w': _L1_xattn_in['q_w'], 'L1_xattn_q_b': _L1_xattn_in['q_b'], 'L1_xattn_kv_w': _L1_xattn_in['kv_w'], 'L1_xattn_kv_b': _L1_xattn_in['kv_b'], 'L1_xattn_out_w': _L1_xattn_in['out_w'], 'L1_xattn_out_b': _L1_xattn_in['out_b'], 'L1_xattn_postnorm_w': _L1_xattn_in['postnorm_w'], 'L1_xattn_mlp_w1': _L1_xattn_in['mlp_w1'], 'L1_xattn_mlp_b1': _L1_xattn_in['mlp_b1'], 'L1_xattn_mlp_w2': _L1_xattn_in['mlp_w2'], 'L1_xattn_mlp_b2': _L1_xattn_in['mlp_b2'], 'L2_xattn_ln1_scale': _L2_xattn_in['ln1_scale'], 'L2_xattn_ln1_offset': _L2_xattn_in['ln1_offset'], 'L2_xattn_wq1': _L2_xattn_in['wq1'], 'L2_xattn_bq1': _L2_xattn_in['bq1'], 'L2_xattn_wk1': _L2_xattn_in['wk1'], 'L2_xattn_bk1': _L2_xattn_in['bk1'], 'L2_xattn_wv1': _L2_xattn_in['wv1'], 'L2_xattn_bv1': _L2_xattn_in['bv1'], 'L2_xattn_wo1': _L2_xattn_in['wo1'], 'L2_xattn_bo1': _L2_xattn_in['bo1'], 'L2_xattn_bias_k1': _L2_xattn_in['bias_k1'], 'L2_xattn_bias_v1': _L2_xattn_in['bias_v1'], 'L2_xattn_ln2_scale': _L2_xattn_in['ln2_scale'], 'L2_xattn_ln2_offset': _L2_xattn_in['ln2_offset'], 'L2_xattn_wq2': _L2_xattn_in['wq2'], 'L2_xattn_bq2': _L2_xattn_in['bq2'], 'L2_xattn_wk2': _L2_xattn_in['wk2'], 'L2_xattn_bk2': _L2_xattn_in['bk2'], 'L2_xattn_wv2': _L2_xattn_in['wv2'], 'L2_xattn_bv2': _L2_xattn_in['bv2'], 'L2_xattn_wo2': _L2_xattn_in['wo2'], 'L2_xattn_bo2': _L2_xattn_in['bo2'], 'L2_xattn_bias_k2': _L2_xattn_in['bias_k2'], 'L2_xattn_bias_v2': _L2_xattn_in['bias_v2'], 'L2_xattn_ln_mlp_scale': _L2_xattn_in['ln_mlp_scale'], 'L2_xattn_ln_mlp_offset': _L2_xattn_in['ln_mlp_offset'], 'L2_xattn_w_fc1': _L2_xattn_in['w_fc1'], 'L2_xattn_b_fc1': _L2_xattn_in['b_fc1'], 'L2_xattn_w_fc2': _L2_xattn_in['w_fc2'], 'L2_xattn_b_fc2': _L2_xattn_in['b_fc2'], 'L3_xattn_ln1_s': _L3_xattn_in['ln1_s'], 'L3_xattn_ln1_b': _L3_xattn_in['ln1_b'], 'L3_xattn_w_qkv': _L3_xattn_in['w_qkv'], 'L3_xattn_b_qkv': _L3_xattn_in['b_qkv'], 'L3_xattn_w_ao': _L3_xattn_in['w_ao'], 'L3_xattn_b_ao': _L3_xattn_in['b_ao'], 'L3_xattn_ln2_s': _L3_xattn_in['ln2_s'], 'L3_xattn_ln2_b': _L3_xattn_in['ln2_b'], 'L3_xattn_w_q': _L3_xattn_in['w_q'], 'L3_xattn_b_q': _L3_xattn_in['b_q'], 'L3_xattn_w_kv': _L3_xattn_in['w_kv'], 'L3_xattn_b_kv': _L3_xattn_in['b_kv'], 'L3_xattn_w_co': _L3_xattn_in['w_co'], 'L3_xattn_b_co': _L3_xattn_in['b_co'], 'L3_xattn_ln3_s': _L3_xattn_in['ln3_s'], 'L3_xattn_ln3_b': _L3_xattn_in['ln3_b'], 'L3_xattn_w1': _L3_xattn_in['w1'], 'L3_xattn_b1': _L3_xattn_in['b1'], 'L3_xattn_w2': _L3_xattn_in['w2'], 'L3_xattn_b2': _L3_xattn_in['b2']}

def reference(x, ctx_2048, mask_BxS2_ik0, mask_1x1xSxS2_fc1, mask_Bx1xSxS2_ff1, L0_xattn_Wq, L0_xattn_Wk, L0_xattn_Wv, L0_xattn_Wo, L0_xattn_ln_q_g, L0_xattn_ln_q_b, L0_xattn_ln_kv_g, L0_xattn_ln_kv_b, L0_xattn_ffn_ln_g, L0_xattn_ffn_ln_b, L0_xattn_W1, L0_xattn_b1, L0_xattn_W2, L0_xattn_b2, L1_xattn_q_w, L1_xattn_q_b, L1_xattn_kv_w, L1_xattn_kv_b, L1_xattn_out_w, L1_xattn_out_b, L1_xattn_postnorm_w, L1_xattn_mlp_w1, L1_xattn_mlp_b1, L1_xattn_mlp_w2, L1_xattn_mlp_b2, L2_xattn_ln1_scale, L2_xattn_ln1_offset, L2_xattn_wq1, L2_xattn_bq1, L2_xattn_wk1, L2_xattn_bk1, L2_xattn_wv1, L2_xattn_bv1, L2_xattn_wo1, L2_xattn_bo1, L2_xattn_bias_k1, L2_xattn_bias_v1, L2_xattn_ln2_scale, L2_xattn_ln2_offset, L2_xattn_wq2, L2_xattn_bq2, L2_xattn_wk2, L2_xattn_bk2, L2_xattn_wv2, L2_xattn_bv2, L2_xattn_wo2, L2_xattn_bo2, L2_xattn_bias_k2, L2_xattn_bias_v2, L2_xattn_ln_mlp_scale, L2_xattn_ln_mlp_offset, L2_xattn_w_fc1, L2_xattn_b_fc1, L2_xattn_w_fc2, L2_xattn_b_fc2, L3_xattn_ln1_s, L3_xattn_ln1_b, L3_xattn_w_qkv, L3_xattn_b_qkv, L3_xattn_w_ao, L3_xattn_b_ao, L3_xattn_ln2_s, L3_xattn_ln2_b, L3_xattn_w_q, L3_xattn_b_q, L3_xattn_w_kv, L3_xattn_b_kv, L3_xattn_w_co, L3_xattn_b_co, L3_xattn_ln3_s, L3_xattn_ln3_b, L3_xattn_w1, L3_xattn_b1, L3_xattn_w2, L3_xattn_b2):
    import jax
    import jax.numpy as jnp

    def _L0_xattn_ref(zt_prev, za, Wq, Wk, Wv, Wo, ln_q_g, ln_q_b, ln_kv_g, ln_kv_b, ffn_ln_g, ffn_ln_b, W1, b1, W2, b2):
        import math
        import jax, jax.numpy as jnp
        import numpy as np
        C = 128
        H = 16
        DH = C // H
        EPS = 1e-05

        def pos_enc(c, T, dtype):
            pos = jnp.arange(T, dtype=jnp.float32)[:, None]
            div = jnp.exp(jnp.arange(0, c, 2, dtype=jnp.float32) * (-math.log(10000.0) / c))
            ang = pos * div
            pe = jnp.zeros((T, c), dtype=jnp.float32)
            pe = pe.at[:, 0::2].set(jnp.sin(ang)).at[:, 1::2].set(jnp.cos(ang))
            return pe.T.astype(dtype)

        def layer_norm(x, g, b):
            mu = jnp.mean(x, axis=-1, keepdims=True)
            var = jnp.mean(jnp.square(x - mu), axis=-1, keepdims=True)
            return (x - mu) * jax.lax.rsqrt(var + EPS) * g + b
        B, _, Tq = zt_prev.shape
        Tk = za.shape[-1]
        q = jnp.transpose(zt_prev + pos_enc(C, Tq, zt_prev.dtype)[None], (0, 2, 1))
        kv = jnp.transpose(za + pos_enc(C, Tk, za.dtype)[None], (0, 2, 1))
        q = layer_norm(q, ln_q_g, ln_q_b)
        kv = layer_norm(kv, ln_kv_g, ln_kv_b)

        def split(x):
            Bt, T, _ = x.shape
            return jnp.transpose(x.reshape(Bt, T, H, DH), (0, 2, 1, 3))
        Q = split(q @ Wq)
        K = split(kv @ Wk)
        V = split(kv @ Wv)
        attn = jnp.einsum('bhqd,bhkd->bhqk', Q, K) / math.sqrt(DH)
        ctx = jnp.einsum('bhqk,bhkd->bhqd', jax.nn.softmax(attn, axis=-1), V)
        ctx = jnp.transpose(ctx, (0, 2, 1, 3)).reshape(B, Tq, C)
        y = ctx @ Wo
        r = y + q
        h = layer_norm(r, ffn_ln_g, ffn_ln_b)
        h = jax.nn.gelu(h @ W1 + b1, approximate=False) @ W2 + b2
        out = h + r
        return jnp.transpose(out, (0, 2, 1))

    def _L1_xattn_ref(x, latents, attention_mask, q_w, q_b, kv_w, kv_b, out_w, out_b, postnorm_w, mlp_w1, mlp_b1, mlp_w2, mlp_b2):
        import jax, jax.numpy as jnp
        import numpy as np
        B, P, K, H, NH = (4, 256, 32, 256, 16)
        DH = H // NH
        EPS = 1e-06

        def rmsnorm(x, w):
            var = jnp.mean(jnp.square(x), axis=-1, keepdims=True)
            return x * jax.lax.rsqrt(var + EPS) * w
        b, p, _ = x.shape
        k_len = latents.shape[1]
        residual = latents
        h = jnp.concatenate([x, latents], axis=1)
        q = (latents @ q_w + q_b).reshape(b, k_len, NH, DH)
        kv = (h @ kv_w + kv_b).reshape(b, p + k_len, NH, DH, 2)
        kmat, v = (kv[..., 0], kv[..., 1])
        attn = jnp.einsum('bkhd,bnhd->bhkn', q, kmat) / DH
        full_mask = jnp.concatenate([attention_mask.astype(bool), jnp.ones((b, k_len), bool)], axis=-1)
        attn = jnp.where(full_mask[:, None, None, :], attn, -jnp.inf)
        attn = jax.nn.softmax(attn.astype(jnp.float32), axis=-1).astype(q.dtype)
        attn_out = jnp.einsum('bhkn,bnhd->bkhd', attn, v).reshape(b, k_len, H)
        attn_out = attn_out @ out_w + out_b + residual
        out = rmsnorm(attn_out, postnorm_w)
        out = jax.nn.gelu(out @ mlp_w1 + mlp_b1) @ mlp_w2 + mlp_b2
        return out + residual

    def _L2_xattn_ref(x, xf_1, xf_2, ln1_scale, ln1_offset, wq1, bq1, wk1, bk1, wv1, bv1, wo1, bo1, bias_k1, bias_v1, ln2_scale, ln2_offset, wq2, bq2, wk2, bk2, wv2, bv2, wo2, bo2, bias_k2, bias_v2, ln_mlp_scale, ln_mlp_offset, w_fc1, b_fc1, w_fc2, b_fc2):
        import jax, jax.numpy as jnp
        import numpy as np
        B, Q, S1, S2 = (4, 32, 256, 256)
        D, H, K, F = (256, 16, 128, 1024)
        LN_EPS = 1e-05

        def _layer_norm(x, scale, offset):
            mu = jnp.mean(x, axis=-1, keepdims=True)
            var = jnp.var(x, axis=-1, keepdims=True)
            return (x - mu) * jax.lax.rsqrt(var + LN_EPS) * scale + offset

        def _cross_attention(q_in, kv_in, wq, bq, wk, bk, wv, bv, wo, bo, bias_k, bias_v):
            b, q_len, _ = q_in.shape
            t = kv_in.shape[1]
            qh = (q_in @ wq + bq).reshape(b, q_len, H, K)
            kh = (kv_in @ wk + bk).reshape(b, t, H, K)
            vh = (kv_in @ wv + bv).reshape(b, t, H, K)
            kh = jnp.concatenate([kh, jnp.broadcast_to(bias_k, (b, 1, H, K))], axis=1)
            vh = jnp.concatenate([vh, jnp.broadcast_to(bias_v, (b, 1, H, K))], axis=1)
            scale = jnp.sqrt(jnp.asarray(K, q_in.dtype))
            logits = jnp.einsum('bqhk,bthk->bhqt', qh, kh) / scale
            weights = jax.nn.softmax(logits, axis=-1)
            ctx = jnp.einsum('bhqt,bthk->bqhk', weights, vh).reshape(b, q_len, H * K)
            return ctx @ wo + bo

        def _forward(x, xf_1, xf_2, ln1_scale, ln1_offset, wq1, bq1, wk1, bk1, wv1, bv1, wo1, bo1, bias_k1, bias_v1, ln2_scale, ln2_offset, wq2, bq2, wk2, bk2, wv2, bv2, wo2, bo2, bias_k2, bias_v2, ln_mlp_scale, ln_mlp_offset, w_fc1, b_fc1, w_fc2, b_fc2):
            res = x
            h = _layer_norm(x, ln1_scale, ln1_offset)
            x = res + _cross_attention(h, xf_1, wq1, bq1, wk1, bk1, wv1, bv1, wo1, bo1, bias_k1, bias_v1)
            res = x
            h = _layer_norm(x, ln2_scale, ln2_offset)
            x = res + _cross_attention(h, xf_2, wq2, bq2, wk2, bk2, wv2, bv2, wo2, bo2, bias_k2, bias_v2)
            h = _layer_norm(x, ln_mlp_scale, ln_mlp_offset)
            h = jax.nn.gelu(h @ w_fc1 + b_fc1, approximate=False) @ w_fc2 + b_fc2
            return x + h
        return _forward(x, xf_1, xf_2, ln1_scale, ln1_offset, wq1, bq1, wk1, bk1, wv1, bv1, wo1, bo1, bias_k1, bias_v1, ln2_scale, ln2_offset, wq2, bq2, wk2, bk2, wv2, bv2, wo2, bo2, bias_k2, bias_v2, ln_mlp_scale, ln_mlp_offset, w_fc1, b_fc1, w_fc2, b_fc2)

    def _L3_xattn_ref(hidden_states, encoder_states, ltor_mask, cross_mask, ln1_s, ln1_b, w_qkv, b_qkv, w_ao, b_ao, ln2_s, ln2_b, w_q, b_q, w_kv, b_kv, w_co, b_co, ln3_s, ln3_b, w1, b1, w2, b2):
        import jax, jax.numpy as jnp
        import numpy as np
        H = 256
        NH = 16
        HD = H // NH
        EPS = 1e-05

        def gelu(x):
            return 0.5 * x * (1.0 + jnp.tanh(0.7978845608028654 * x * (1.0 + 0.044715 * x * x)))

        def layernorm(x, scale, bias):
            m = jnp.mean(x, axis=-1, keepdims=True)
            v = jnp.mean(jnp.square(x - m), axis=-1, keepdims=True)
            return (x - m) * jax.lax.rsqrt(v + EPS) * scale + bias

        def split_heads(x):
            b, s, _ = x.shape
            return x.reshape(b, s, NH, HD).transpose(0, 2, 1, 3)

        def merge_heads(x):
            b, nh, s, hd = x.shape
            return x.transpose(0, 2, 1, 3).reshape(b, s, nh * hd)

        def attention(q, k, v, mask):
            scores = jnp.einsum('bhqd,bhkd->bhqk', q, k) / jnp.sqrt(jnp.float32(HD))
            scores = scores * mask - 10000.0 * (1.0 - mask)
            probs = jax.nn.softmax(scores, axis=-1)
            return jnp.einsum('bhqk,bhkd->bhqd', probs, v)
        ln_out = layernorm(hidden_states, ln1_s, ln1_b)
        qkv = ln_out @ w_qkv + b_qkv
        q, k, v = jnp.split(qkv, 3, axis=-1)
        ctx = merge_heads(attention(split_heads(q), split_heads(k), split_heads(v), ltor_mask))
        attn_out = ctx @ w_ao + b_ao
        x = hidden_states + attn_out
        ln_out = layernorm(x, ln2_s, ln2_b)
        q = ln_out @ w_q + b_q
        kv = encoder_states @ w_kv + b_kv
        k, v = jnp.split(kv, 2, axis=-1)
        ctx = merge_heads(attention(split_heads(q), split_heads(k), split_heads(v), cross_mask))
        cross_out = ctx @ w_co + b_co
        x = x + cross_out
        ln_out = layernorm(x, ln3_s, ln3_b)
        mlp_out = gelu(ln_out @ w1 + b1) @ w2 + b2
        return x + mlp_out
    x = _L0_xattn_ref(x, ctx_2048, L0_xattn_Wq, L0_xattn_Wk, L0_xattn_Wv, L0_xattn_Wo, L0_xattn_ln_q_g, L0_xattn_ln_q_b, L0_xattn_ln_kv_g, L0_xattn_ln_kv_b, L0_xattn_ffn_ln_g, L0_xattn_ffn_ln_b, L0_xattn_W1, L0_xattn_b1, L0_xattn_W2, L0_xattn_b2)
    x = _L1_xattn_ref(ctx_2048, x, mask_BxS2_ik0, L1_xattn_q_w, L1_xattn_q_b, L1_xattn_kv_w, L1_xattn_kv_b, L1_xattn_out_w, L1_xattn_out_b, L1_xattn_postnorm_w, L1_xattn_mlp_w1, L1_xattn_mlp_b1, L1_xattn_mlp_w2, L1_xattn_mlp_b2)
    x = _L2_xattn_ref(x, ctx_2048, ctx_2048, L2_xattn_ln1_scale, L2_xattn_ln1_offset, L2_xattn_wq1, L2_xattn_bq1, L2_xattn_wk1, L2_xattn_bk1, L2_xattn_wv1, L2_xattn_bv1, L2_xattn_wo1, L2_xattn_bo1, L2_xattn_bias_k1, L2_xattn_bias_v1, L2_xattn_ln2_scale, L2_xattn_ln2_offset, L2_xattn_wq2, L2_xattn_bq2, L2_xattn_wk2, L2_xattn_bk2, L2_xattn_wv2, L2_xattn_bv2, L2_xattn_wo2, L2_xattn_bo2, L2_xattn_bias_k2, L2_xattn_bias_v2, L2_xattn_ln_mlp_scale, L2_xattn_ln_mlp_offset, L2_xattn_w_fc1, L2_xattn_b_fc1, L2_xattn_w_fc2, L2_xattn_b_fc2)
    x = _L3_xattn_ref(x, ctx_2048, mask_1x1xSxS2_fc1, mask_Bx1xSxS2_ff1, L3_xattn_ln1_s, L3_xattn_ln1_b, L3_xattn_w_qkv, L3_xattn_b_qkv, L3_xattn_w_ao, L3_xattn_b_ao, L3_xattn_ln2_s, L3_xattn_ln2_b, L3_xattn_w_q, L3_xattn_b_q, L3_xattn_w_kv, L3_xattn_b_kv, L3_xattn_w_co, L3_xattn_b_co, L3_xattn_ln3_s, L3_xattn_ln3_b, L3_xattn_w1, L3_xattn_b1, L3_xattn_w2, L3_xattn_b2)
    return x

_drawn_inputs = setup_inputs


def setup_inputs(seed=0):
    import zlib

    import numpy as np

    out = dict(_drawn_inputs(seed))
    spreads = {'L0_xattn_ln_q_g': (1.0, 0.2),
     'L0_xattn_ln_q_b': (0.0, 0.1),
     'L0_xattn_ln_kv_g': (1.0, 0.2),
     'L0_xattn_ln_kv_b': (0.0, 0.1),
     'L0_xattn_ffn_ln_g': (1.0, 0.2),
     'L0_xattn_ffn_ln_b': (0.0, 0.1),
     'L0_xattn_b1': (0.0, 0.1),
     'L0_xattn_b2': (0.0, 0.1),
     'L1_xattn_q_b': (0.0, 0.8),
     'L1_xattn_kv_b': (0.0, 0.8),
     'L1_xattn_out_b': (0.0, 2.0),
     'L1_xattn_postnorm_w': (1.0, 0.6),
     'L1_xattn_mlp_b1': (0.0, 0.306),
     'L1_xattn_mlp_b2': (0.0, 0.1),
     'L2_xattn_ln1_scale': (1.0, 0.6),
     'L2_xattn_ln1_offset': (0.0, 0.8),
     'L2_xattn_bq1': (0.0, 0.8),
     'L2_xattn_bk1': (0.0, 2.0),
     'L2_xattn_bv1': (0.0, 0.1),
     'L2_xattn_bo1': (0.0, 0.1),
     'L2_xattn_ln2_scale': (1.0, 0.6),
     'L2_xattn_ln2_offset': (0.0, 0.8),
     'L2_xattn_bq2': (0.0, 0.8),
     'L2_xattn_bk2': (0.0, 2.0),
     'L2_xattn_bv2': (0.0, 0.1),
     'L2_xattn_bo2': (0.0, 0.1),
     'L2_xattn_ln_mlp_scale': (1.0, 0.6),
     'L2_xattn_ln_mlp_offset': (0.0, 0.8),
     'L2_xattn_b_fc1': (0.0, 0.3),
     'L2_xattn_b_fc2': (0.0, 0.1),
     'L3_xattn_ln1_s': (1.0, 0.6),
     'L3_xattn_ln1_b': (0.0, 0.8),
     'L3_xattn_b_qkv': (0.0, 0.346),
     'L3_xattn_b_ao': (0.0, 0.1),
     'L3_xattn_ln2_s': (1.0, 0.6),
     'L3_xattn_ln2_b': (0.0, 2.0),
     'L3_xattn_b_q': (0.0, 2.0),
     'L3_xattn_b_kv': (0.0, 0.354),
     'L3_xattn_b_co': (0.0, 0.1),
     'L3_xattn_ln3_s': (1.0, 0.6),
     'L3_xattn_ln3_b': (0.0, 0.8),
     'L3_xattn_b1': (0.0, 0.301),
     'L3_xattn_b2': (0.0, 0.1)}
    factors = {'L1_xattn_q_w': 8.0,
     'L1_xattn_kv_w': 8.0,
     'L1_xattn_out_w': 8.0,
     'L2_xattn_wq1': 8.0,
     'L2_xattn_wk1': 8.0,
     'L2_xattn_bias_k1': 64.0,
     'L2_xattn_bias_v1': 64.0,
     'L2_xattn_wq2': 8.0,
     'L2_xattn_wk2': 8.0,
     'L2_xattn_bias_k2': 64.0,
     'L2_xattn_bias_v2': 64.0,
     'L3_xattn_w_q': 22.847}
    for name, (base, spread) in spreads.items():
        noise = np.random.default_rng([zlib.crc32(name.encode()), seed]).standard_normal(out[name].shape)
        drawn = base * np.exp(spread * noise) if base else spread * noise
        out[name] = jnp.asarray(drawn.astype(out[name].dtype))
    for name, factor in factors.items():
        out[name] = (out[name] * factor).astype(out[name].dtype)
    return out
```

```python
from contextlib import ExitStack

import numpy as np

import concourse.bass as bass
from concourse import mybir

F32 = mybir.dt.float32
BF16 = mybir.dt.bfloat16
I32 = mybir.dt.int32
ALU = mybir.AluOpType
ACT = mybir.ActivationFunctionType
AX = mybir.AxisListType.X

P = 128
B = 16
D = 256
S = 128
H = 16
BANK = 512
SLOT = 32
FF = 1024
NEG = -1.0e30

COLUMNS = [
    ("l0_ffn_g", 1), ("l0_ffn_b", 1), ("l0_b1", 2), ("l0_b2", 1),
    ("l1_q_b", 2), ("l1_k_b", 2), ("l1_v_b", 2), ("l1_post", 2), ("l1_b1", 8),
    ("l2_ln1_g", 2), ("l2_ln1_b", 2), ("l2_bq1", 16), ("l2_bk1", 16), ("l2_bias_k1", 16), ("l2_bias_v1", 16),
    ("l2_bo1", 2),
    ("l2_ln2_g", 2), ("l2_ln2_b", 2), ("l2_bq2", 16), ("l2_bk2", 16), ("l2_bias_k2", 16), ("l2_bias_v2", 16),
    ("l2_bo2", 2),
    ("l2_lnm_g", 2), ("l2_lnm_b", 2), ("l2_b1", 8),
    ("l3_ln1_g", 2), ("l3_ln1_b", 2), ("l3_q_b1", 2), ("l3_k_b1", 2), ("l3_v_b1", 2),
    ("l3_ln2_g", 2), ("l3_ln2_b", 2), ("l3_q_b2", 2), ("l3_k_b2", 2), ("l3_v_b2", 2),
    ("l3_ln3_g", 2), ("l3_ln3_b", 2), ("l3_b1", 8),
]
COL_AT = {}
for _name, _n in COLUMNS:
    COL_AT[_name] = (sum(n for _, n in COLUMNS[:len(COL_AT)]), _n)
N_COLS = sum(n for _, n in COLUMNS)
ROWS = ["l0_q_g", "l0_kv_g", "l0_q_b", "l0_kv_b", "l1_out_b", "l1_b2", "l2_b2", "l3_ao_b", "l3_co_b", "l3_b2"]
ROW_LEN = {n: (S if n.startswith("l0") else D) for n in ROWS}
ROW_AT = {n: sum(ROW_LEN[m] for m in ROWS[:i]) for i, n in enumerate(ROWS)}
N_ROWS = sum(ROW_LEN.values())


class Bank:

    def __init__(self, ap, full, free, jobs):
        self.ap, self.full, self.free, self.jobs = ap, full, free, jobs

    def nth(self, step, job):
        return step * self.jobs + job + 1


class Step:

    def __init__(self, i, k, per):
        self.i, self.k, self.per = i, k, per
        self.n = i * per + k

    def times(self, count, more):
        return self.n * count + more


def pipelined(eng, steps, per, both):
    both(Step(0, 0, per), None)
    rounds = steps // per
    if rounds > 1:
        with eng.Fori(0, rounds - 1) as i:
            for k in range(per):
                both(Step(i, k + 1, per), Step(i, k, per))
    for k in range(per):
        both(Step(rounds - 1, k + 1, per) if k < per - 1 else None, Step(rounds - 1, k, per))


class Chip:
    pass


def clear_semaphores(nc, sems):
    for s in sems:
        nc.gpsimd.sem_clear(s)
    nc.all_engine_barrier()


def load_constants(c, l1_loaded):
    nc = c.nc
    loaded, made, shapes_loaded = (c.lasting(n) for n in ("constants_loaded", "constants_made", "shapes_loaded"))
    with nc.Block() as block:

        @block.sync
        def _(sync):
            sync.dma_start(c.shapes[:, :], c.dram["shapes"]).then_inc(shapes_loaded, 16)
            sync.dma_start(c.cols[:, :], c.dram["cols"]).then_inc(loaded, 16)
            sync.dma_start(c.rows[:, :], c.dram["rows"].rearrange("(a n) -> a n", a=1).to_broadcast([P, N_ROWS]))\
                .then_inc(loaded, 16)
            mine = [n for n in WEIGHTS_01 if n.startswith("l0")]
            for name in mine:
                sync.dma_start(c.w[name][:, :, :], c.dram[name]).then_inc(loaded, 16)
            for name in WEIGHTS_01:
                if name not in mine:
                    sync.dma_start(c.w[name][:, :, :], c.dram[name]).then_inc(l1_loaded, 16)
            sync.wait_ge(loaded, 16 * (2 + len(mine)))
            sync.wait_ge(l1_loaded, 16 * (len(WEIGHTS_01) - len(mine)))

        @block.gpsimd
        def _(pool):
            pool.memset(c.ident[:, :], 0.0).then_inc(made, 1)
            pool.memset(c.ident_bf[:, :], 0.0).then_inc(made, 1)
            pool.memset(c.ones_bf[:, :], 1.0).then_inc(made, 1)
            pool.memset(c.minus_half[:, :], -0.5).then_inc(made, 1)
            pool.memset(c.epsilons[:, 0:1], 1e-5).then_inc(made, 1)
            pool.memset(c.epsilons[:, 1:2], 1e-6).then_inc(made, 1)
            pool.memset(c.quarter[:, :], 0.25).then_inc(made, 1)
            pool.wait_ge(made, 7)
            for m in (c.ident, c.ident_bf):
                pool.affine_select(out=m[:, :], in_=m[:, :], compare_op=ALU.not_equal, fill=1.0, base=0,
                                   pattern=[[-1, P]], channel_multiplier=1).then_inc(made, 1)
            pool.wait_ge(shapes_loaded, 16)
            pool.tensor_copy(c.select[:, :], c.shapes[:, 2 * H:]).then_inc(made, 1)
            pool.wait_ge(made, 10)


def inverse_root(pool, c, chain, at, value, out, eps, n):
    small = c.epsilons[:, 0 if eps == 1e-5 else 1:1 if eps == 1e-5 else 2].unsqueeze(1).to_broadcast([P, n, 1])
    pool.tensor_tensor(out=out, in0=value, in1=small, op=ALU.add).then_inc(chain, 1)
    pool.wait_ge(chain, at + 1)
    return pool.tensor_tensor(out=out, in0=out, in1=c.minus_half[:, 0:n].unsqueeze(2), op=ALU.pow)


def carry_wait(act, c):
    c.carried = (c.carried + 1) % 8
    act.activation(c.waiter_act[:, c.carried:c.carried + 1], c.minus_half[:, 0:1], ACT.Copy)


def norm_transposed(c, name, gamma, beta, add=False):
    nc = c.nc
    with ExitStack() as ctx:
        def sb(n, shape, dt=F32):
            return ctx.enter_context(nc.sbuf_tensor(f"{name}_{n}", shape, dt))

        sems = []

        def sem(n):
            sems.append(ctx.enter_context(nc.semaphore(f"{name}_{n}")))
            return sems[-1]

        staged = sb("staged", [P, 2, 2, S])
        stats = sb("stats", [P, 2, 6])
        mean_var = sb("mean_var", [P, 2, 2])
        rstd = sb("rstd", [P, 2, 1])
        xn = sb("xn", [P, 2, D])
        psum = [ctx.enter_context(nc.psum_tensor(f"{name}_psum{i}", [P, BANK], F32)) for i in range(4)]
        added = [Bank(psum[i], sem(f"added_full{i}"), sem(f"added_free{i}"), 1) for i in range(2)]
        turned = [Bank(psum[2 + i], sem(f"turned_full{i}"), sem(f"turned_free{i}"), 1) for i in range(2)]
        acc_staged = sem("acc_staged")
        stats_done = sem("stats_done")
        var_done = sem("var_done")
        rstd_done = sem("rstd_done")
        pool_chain = sem("pool_chain")
        xn_done = sem("xn_done")
        ctx.callback(clear_semaphores, nc, sems)
        block = ctx.enter_context(nc.Block())

        def steps(eng, one):
            with eng.Fori(0, B // 2) as i:
                for p in range(2):
                    one(i, p, i * 2 + p)

        @block.sync
        def _(sync):
            for bank in added + turned:
                sync.sem_inc(bank.free, 1)

        @block.gpsimd
        def _(pool):
            def one(i, p, b):
                pool.wait_ge(var_done, b + 1)
                inverse_root(pool, c, pool_chain, b, mean_var[:, p:p + 1, 1:2], rstd[:, p:p + 1, :], 1e-5, 1)\
                    .then_inc(rstd_done, 1)
            steps(pool, one)

        @block.tensor
        def _(pe):
            def one(i, p, b):
                if add:
                    pe.wait_ge(acc_staged, b + 1)
                    pe.wait_ge(added[p].free, i + 1)
                    for t in range(2):
                        last = pe.transpose(added[p].ap[:, t * S:(t + 1) * S], staged[:, p, t, :], c.ident[:, :])
                    last.then_inc(added[p].full, 1)
                pe.wait_ge(xn_done, b + 1)
                pe.wait_ge(turned[p].free, i + 1)
                for t in range(2):
                    last = pe.transpose(turned[p].ap[:, t * S:(t + 1) * S], xn[:, p, t * P:(t + 1) * P], c.ident[:, :])
                last.then_inc(turned[p].full, 1)
            steps(pe, one)

        @block.vector
        def _(dve):
            def one(i, p, b):
                x = c.x[:, b, :]
                if add:
                    dve.wait_ge(added[p].full, i + 1)
                    dve.tensor_tensor(out=x, in0=x, in1=added[p].ap[:, 0:D], op=ALU.add).then_inc(added[p].free, 1)
                    dve.wait_ge(added[p].free, i + 2)
                    dve.memset(c.waiter[:, :], 0.0)
                dve.bn_stats(stats[:, p, :], x).then_inc(stats_done, 1)
                dve.wait_ge(stats_done, b + 1)
                dve.memset(c.waiter[:, :], 0.0)
                dve.bn_aggr(mean_var[:, p, :], stats[:, p, :]).then_inc(var_done, 1)
                dve.wait_ge(rstd_done, b + 1)
                dve.wait_ge(turned[p].free, i + 1)
                dve.tensor_scalar(out=xn[:, p, :], in0=x, scalar1=mean_var[:, p, 0:1], scalar2=rstd[:, p, :],
                                  op0=ALU.subtract, op1=ALU.mult).then_inc(xn_done, 1)
            steps(dve, one)

        @block.scalar
        def _(act):
            def one(i, p, b):
                if add:
                    act.wait_ge(added[p].free, i + 1)
                    carry_wait(act, c)
                    act.activation(staged[:, p, :, :], c.acc[:, :, b, :], ACT.Copy).then_inc(acc_staged, 1)
                act.wait_ge(turned[p].full, i + 1)
                carry_wait(act, c)
                for t in range(2):
                    last = act.activation(c.nT[:, t, b, :], turned[p].ap[:, t * S:(t + 1) * S], ACT.Identity,
                                          bias=c.col(beta, t), scale=c.col(gamma, t))
                last.then_inc(turned[p].free, 1)
            steps(act, one)


def mlp(c, name, w1, b1, w2, func, width, hidden, finish):
    nc = c.nc
    kt, ft = width // P, hidden // P
    channels = finish == "channels"
    groups = 8 if channels else 4
    store = name == "l3_mlp"
    with ExitStack() as ctx:
        def sb(n, shape, dt=F32):
            return ctx.enter_context(nc.sbuf_tensor(f"{name}_{n}", shape, dt))

        sems = []

        def sem(n):
            sems.append(ctx.enter_context(nc.semaphore(f"{name}_{n}")))
            return sems[-1]

        hT = sb("hT", [P, 2, ft, BANK])
        psum = [ctx.enter_context(nc.psum_tensor(f"{name}_psum{i}", [P, BANK], F32)) for i in range(8)]
        ups = min(ft, 4)
        up = [Bank(psum[i], sem(f"up_full{i}"), sem(f"up_free{i}"), ft // ups) for i in range(ups)]
        down = [Bank(psum[4 + i], sem(f"down_full{i}"), sem(f"down_free{i}"), 1) for i in range(4)]
        bias_added = sem("bias_added")
        stored = sem("stored")
        ctx.callback(clear_semaphores, nc, sems)
        block = ctx.enter_context(nc.Block())

        def source(t, g):
            if width == P:
                return c.nT_flat[:, bass.ds(g * BANK, BANK)]
            return c.nT[:, t, bass.ds(g * 4, 4), :]

        @block.sync
        def _(sync):
            for bank in up + down:
                sync.sem_inc(bank.free, 1)
            if store:
                with sync.Fori(0, groups) as g:
                    for bank in down:
                        sync.wait_ge(bank.free, g + 2)
                    sync.dma_start(c.out[bass.ds(g * 4, 4), :, :].rearrange("b p d -> p b d"),
                                   c.x[:, bass.ds(g * 4, 4), :]).then_inc(stored, 16)
                sync.wait_ge(stored, 16 * groups)

        @block.gpsimd
        def _(pool):
            if not channels:
                with pool.Fori(0, B) as b:
                    pool.tensor_tensor(out=c.x[:, b, :], in0=c.x[:, b, :], in1=c.row(finish), op=ALU.add)\
                        .then_inc(bias_added, 1)

        @block.tensor
        def _(pe):
            with pe.Fori(0, groups // 2) as i:
                for p in range(2):
                    g = i * 2 + p
                    for f in range(ft):
                        bank = up[f % ups]
                        pe.wait_ge(bank.free, bank.nth(g, f // ups))
                        for t in range(kt):
                            last = pe.matmul(bank.ap[:, :], w1[:, t, f * P:(f + 1) * P], source(t, g),
                                             start=(t == 0), stop=(t == kt - 1))
                        last.then_inc(bank.full, 1)
                    for bank in up:
                        pe.wait_ge(bank.free, bank.nth(g, bank.jobs - 1) + 1)
                    if channels:
                        bank = down[p]
                        pe.wait_ge(bank.free, i + 1)
                        for f in range(ft):
                            last = pe.matmul(bank.ap[:, :], w2[:, f, :], hT[:, p, f, :],
                                             start=(f == 0), stop=(f == ft - 1))
                        last.then_inc(bank.full, 1)
                    else:
                        for n in range(4):
                            bank = down[n]
                            pe.wait_ge(bank.free, g + 1)
                            for f in range(ft):
                                last = pe.matmul(bank.ap[:, 0:D], hT[:, p, f, n * P:(n + 1) * P], w2[:, f, :],
                                                 start=(f == 0), stop=(f == ft - 1))
                            last.then_inc(bank.full, 1)

        @block.scalar
        def _(act):
            with act.Fori(0, groups // 2) as i:
                for p in range(2):
                    g = i * 2 + p
                    for f in range(ft):
                        bank = up[f % ups]
                        act.wait_ge(bank.full, bank.nth(g, f // ups))
                        act.activation(hT[:, p, f, :], bank.ap[:, :], func, bias=c.col(b1, f), scale=1.0)\
                            .then_inc(bank.free, 1)

        @block.vector
        def _(dve):
            with dve.Fori(0, groups // 2) as i:
                for p in range(2):
                    g = i * 2 + p
                    if channels:
                        bank = down[p]
                        dve.wait_ge(bank.full, i + 1)
                        dve.scalar_tensor_tensor(out=c.x_flat[:, bass.ds(g * BANK, BANK)], in0=bank.ap[:, :],
                                                 scalar=c.col("l0_b2", 0), in1=c.acc_flat[:, bass.ds(g * BANK, BANK)],
                                                 op0=ALU.add, op1=ALU.add).then_inc(bank.free, 1)
                    else:
                        for n in range(4):
                            bank = down[n]
                            b = g * 4 + n
                            dve.wait_ge(bias_added, b + 1)
                            dve.wait_ge(bank.full, g + 1)
                            dve.tensor_tensor(out=c.x[:, b, :], in0=c.x[:, b, :], in1=bank.ap[:, 0:D], op=ALU.add)\
                                .then_inc(bank.free, 1)


class Narrow:

    def __init__(self, name, channel_tiles, queries, keys, head_dim, scale, front_jobs, back_jobs):
        self.name = name
        self.ct = channel_tiles
        self.nq, self.nk, self.dh = queries, keys, head_dim
        self.scale = scale
        self.qt, self.kt = queries // P, keys // P
        self.heads_a_tile = H // channel_tiles
        self.hq, self.hk = BANK // queries, BANK // keys
        self.score_jobs = self.qt * H // self.hk
        self.turned_jobs = self.kt * H // self.hq
        self.front_jobs = front_jobs + self.score_jobs
        self.back_jobs = back_jobs


LAYER0 = Narrow("l0", 1, 256, 256, 8, 8.0 ** -0.5, 4, 6)
LAYER1 = Narrow("l1", 2, 128, 256, 16, 1.0 / 16, 6, 4)
LAYER3_SELF = Narrow("l3s", 2, 128, 128, 16, 1.0, 4, 4)
LAYER3_CROSS = Narrow("l3c", 2, 128, 128, 16, 1.0, 4, 4)


def narrow_attention(c, z):
    nc = c.nc
    l0, l1 = z is LAYER0, z is LAYER1
    masked = z.name.startswith("l3")
    cross = z is LAYER3_CROSS
    with ExitStack() as ctx:
        def sb(n, shape, dt=F32):
            return ctx.enter_context(nc.sbuf_tensor(f"{z.name}_{n}", shape, dt))

        sems = []

        def sem(n):
            sems.append(ctx.enter_context(nc.semaphore(f"{z.name}_{n}")))
            return sems[-1]

        QK = sb("QK", [P, 2, z.ct * (z.nq + z.nk)])
        QT = [QK[:, p, 0:z.ct * z.nq].rearrange("p (t q) -> p t q", t=z.ct) for p in range(2)]
        KT = [QK[:, p, z.ct * z.nq:].rearrange("p (t k) -> p t k", t=z.ct) for p in range(2)]
        q_blocks = sb("q_blocks", [P, 2, H, z.nq])
        V = sb("V", [P, 2, z.kt, H, SLOT])
        neg_max_T = sb("neg_max_T", [P, 2, z.nq], BF16)
        width = z.ct * P
        q_bf = sb("q_bf", [P, z.ct, z.nq], BF16)
        k_blocks = sb("k_blocks", [P, H, z.nk], BF16)
        neg_max = sb("neg_max", [P, z.qt, H])
        neg_max_bf = sb("neg_max_bf", [P, z.qt, P], BF16)
        PT = sb("PT", [P, 3, BANK])
        ctx_den = sb("ctx_den", [P, 4, z.nq])
        rden = sb("rden", [P, z.qt, H, 1])
        ctx_q = sb("ctx_q", [P, z.qt, H, z.dh])
        ctx_T = sb("ctx_T", [P, z.ct, z.nq])
        x_T = sb("x_T", [P, 4 * P])
        if l0:
            x_in = sb("x_in", [P, 2, 4, P])
        else:
            res = sb("res", [P, 2, D])
        if l1:
            x_in = sb("x_in", [P, 2, D])
            mask_col = sb("mask_col", [P, B])
            mask_step = sb("mask_step", [P, 1])
            mask_row = sb("mask_row", [P, B, z.nk], BF16)
            mask_int = sb("mask_int", [P, B], I32)
            mask_row_int = sb("mask_row_int", [1, B, S], I32)
        else:
            stats = sb("stats", [P, 4, 6])
            mean_var = sb("mean_var", [P, 4, 2])
            rstd = sb("rstd", [P, 4, 1])
            xn = sb("xn", [P, 4, P])
        if l0 or l1:
            r = sb("r", [P, z.qt, width])
            rn = sb("rn", [P, z.qt, width])
            stats_b = sb("stats_b", [P, 2, 6])
            mean_var_b = sb("mean_var_b", [P, 2, 2])
            rstd_b = sb("rstd_b", [P, 2, 1])
        if l1 or cross:
            ctx_in = sb("ctx_in", [P, 2, 2, S])
        if masked:
            mask_in = sb("mask_in", [P, 2, 2, S])
            mask_mul = sb("mask_mul", [P, 2, 2, S])
            mask_add = sb("mask_add", [P, 2, 2, S])
            s_masked = sb("s_masked", [P, 2, BANK])
            s_biased = sb("s_biased", [P, 2, BANK])
            t_masked = sb("t_masked", [P, 2, BANK])
            t_biased = sb("t_biased", [P, 2, BANK])
            t_shifted = sb("t_shifted", [P, 2, BANK])

        banks = [ctx.enter_context(nc.psum_tensor(f"{z.name}_psum{i}", [P, BANK], F32)) for i in range(8)]

        def bank(n, what, jobs):
            return Bank(banks[n], sem(f"{what}_full"), sem(f"{what}_free"), jobs)

        front = [bank(i, f"front{i}", z.front_jobs // 2) for i in range(2)]
        turned = [bank(2 + i, f"turned{i}", z.turned_jobs // (1 if masked else 2)) for i in range(2)]
        context = [bank(4 + i, f"context{i}", 1) for i in range(2 if l0 else 1)]
        back = [bank(6 + i, f"back{i}", z.back_jobs // 2) for i in range(2)]

        loaded = sem("loaded")
        set_up = sem("set_up")
        x_loaded = [sem(f"x_loaded{p}") for p in range(2)]
        mask_loaded = [sem(f"mask_loaded{p}") for p in range(2)]
        mask_made = sem("mask_made")
        mask_copied = sem("mask_copied")
        x_ready = sem("x_ready")
        stats_done = sem("stats_done")
        var_done = sem("var_done")
        rstd_done = sem("rstd_done")
        rstd_part = sem("rstd_part")
        xn_done = sem("xn_done")
        scaled = sem("scaled")
        ln_done = sem("ln_done")
        res_ready = sem("res_ready")
        blocks_ready = sem("blocks_ready")
        q_blocks_ready = sem("q_blocks_ready")
        s_ready = sem("s_ready")
        t_ready = sem("t_ready")
        max_done = sem("max_done")
        probs_ready = sem("probs_ready")
        rden_done = sem("rden_done")
        stats_b_done = sem("stats_b_done")
        var_b_done = sem("var_b_done")
        rstd_b_part = sem("rstd_b_part")
        rstd_b_done = sem("rstd_b_done")
        rn_done = sem("rn_done")
        ctx.callback(clear_semaphores, nc, sems)
        block = ctx.enter_context(nc.Block())

        lag = 2 if masked else 1
        pieces = z.turned_jobs + lag
        n_pre = z.front_jobs - z.score_jobs - 1
        pre_at = [8, 10, 12] if l0 else [1, 2, 3, 4, 5] if l1 else [2, 3, 4]
        share = -(-z.score_jobs // z.back_jobs)

        def F(f):
            return front[f % 2], f // 2

        def order(fr, bk, pre, stream, score, tail, last):
            for n in range(pieces):
                if bk is not None:
                    stream(bk, n)
                if fr is not None:
                    for f in range(n_pre):
                        if pre_at[f] == n:
                            pre(fr, f)
            for m in range(z.back_jobs):
                if fr is not None:
                    for j in range(m * share, min((m + 1) * share, z.score_jobs)):
                        score(fr, j)
                if bk is not None:
                    tail(bk, m)
            if fr is not None:
                last(fr)

        T, Q_JOB, K_JOB, V_JOBS = 0, (2 if l1 else 1), 1, ([3, 4] if l1 else [2])
        N_JOB = z.front_jobs - 1
        TURN = list(range(z.qt))
        CTX_T = [z.qt] if not masked else [1, 2]
        OUT = CTX_T[-1] + 1
        TAIL = list(range(OUT + 1, z.back_jobs))

        def by_head(ap):
            return ap.rearrange("p (h s) -> p h s", h=4)

        def all_heads(ap):
            return ap.unsqueeze(1).to_broadcast([P, 4, S])

        def out_evacuated(b):
            bk = back[OUT % 2]
            return bk.free, bk.nth(b, OUT // 2) + 1

        @block.sync
        def _(sync):
            for bk in front + turned + context + back:
                sync.sem_inc(bk.free, 1)
            if l1:
                sync.dma_start(mask_int[:, :], c.dram["mask_T"]).then_inc(loaded, 16)
                sync.dma_start(mask_row_int[:, :, :], c.dram["mask"].rearrange("(a b) s -> a b s", a=1))\
                    .then_inc(loaded, 16)
            if masked and not cross:
                sync.dma_start(mask_in[:, 0, :, :], c.dram["self_mask"].rearrange("w p s -> p w s"))\
                    .then_inc(loaded, 16)

            def load(b, p):
                if l0:
                    sync.dma_start(x_in[:, p, 0:2, :], c.dram["x_T"][b].rearrange("(t p) s -> p t s", p=P))\
                        .then_inc(x_loaded[p], 16)
                    sync.dma_start(x_in[:, p, 2:4, :], c.dram["ctx_T"][b].rearrange("(t p) s -> p t s", p=P))\
                        .then_inc(x_loaded[p], 16)
                if l1 or cross:
                    sync.dma_start(ctx_in[:, p, :, :], c.dram["ctx_T"][b].rearrange("(t p) s -> p t s", p=P))\
                        .then_inc(x_loaded[p], 16)
                if cross:
                    sync.dma_start(mask_in[:, p, :, :], c.dram["cross_mask"][b].rearrange("w p s -> p w s"))\
                        .then_inc(mask_loaded[p], 16)

            if l0 or l1 or cross:
                for p in range(2):
                    load(p, p)
                with sync.Fori(1, B // 2) as i:
                    for p in range(2):
                        before = (i - 1) * 2 + p
                        if l0:
                            sync.wait_ge(*out_evacuated(before))
                        else:
                            bk, k = F(V_JOBS[-1])
                            sync.wait_ge(bk.full, bk.nth(before, k))
                        if cross:
                            sync.wait_ge(mask_made, (before + 1) * 2)
                        load(i * 2 + p, p)

        @block.gpsimd
        def _(pool):
            pool.memset(neg_max_bf[:, :, :], 0.0).then_inc(set_up, 1)
            pool.memset(V[:, :, :, :, :], 0.0).then_inc(set_up, 1)
            pool.wait_ge(set_up, 2)
            pool.memset(V[:, :, :, :, z.dh:z.dh + 1], 1.0).then_inc(set_up, 1)
            if l1:
                pool.memset(mask_row[:, :, :], 0.0).then_inc(set_up, 1)
                pool.wait_ge(set_up, 4)
                pool.wait_ge(loaded, 32)
                pool.tensor_scalar(out=mask_col[:, :], in0=mask_int[:, :], scalar1=0.0, scalar2=NEG,
                                   op0=ALU.is_equal, op1=ALU.mult).then_inc(set_up, 1)
                pool.tensor_scalar(out=mask_row[0:1, :, 0:S], in0=mask_row_int[:, :, :], scalar1=0.0, scalar2=NEG,
                                   op0=ALU.is_equal, op1=ALU.mult).then_inc(set_up, 1)
                pool.wait_ge(set_up, 6)

            def make_masks(p):
                pool.tensor_tensor(out=mask_mul[:, p, :, :], in0=mask_in[:, p, :, :],
                                   in1=c.quarter[:, :].unsqueeze(2).to_broadcast([P, 2, S]), op=ALU.mult)\
                    .then_inc(mask_made, 1)
                pool.tensor_scalar(out=mask_add[:, p, :, :], in0=mask_in[:, p, :, :], scalar1=10000.0,
                                   scalar2=-10000.0, op0=ALU.mult, op1=ALU.add).then_inc(mask_made, 1)

            if masked and not cross:
                pool.wait_ge(loaded, 16)
                make_masks(0)
                pool.wait_ge(mask_made, 2)

            def begin(b, first):
                p = b.k % 2
                if l0:
                    pool.wait_ge(x_loaded[p], (b.n - p) * 16 + 32)
                    x = x_in[:, p, :, :]
                    pool.tensor_tensor(out=x, in0=x, in1=c.pos[:, :, :], op=ALU.add).then_inc(x_ready, 1)
                else:
                    if not first:
                        bk = back[OUT % 2]
                        pool.wait_ge(bk.free, b.times(bk.jobs, OUT // 2 + 2 - 2 * bk.jobs))
                    x = c.x[:, b.n, :]
                    pool.tensor_tensor(out=res[:, p, :], in0=x, in1=c.row(
                        "l1_out_b" if l1 else "l3_co_b" if cross else "l3_ao_b"), op=ALU.add).then_inc(res_ready, 1)
                    if l1:
                        pool.tensor_copy(x_in[:, p, :], x).then_inc(x_ready, 1)
                    if cross:
                        pool.wait_ge(mask_loaded[p], (b.n - p) * 8 + 16)
                        if not first:
                            pool.wait_ge(turned[0].free, b.times(4, 1 - 4))
                        make_masks(p)
                if not l1:
                    pool.wait_ge(var_done, b.n + 1)
                    n = 4 if l0 else 1
                    inverse_root(pool, c, rstd_part, b.n, mean_var[:, 0:n, 1:2], rstd[:, 0:n, :], 1e-5, n)\
                        .then_inc(rstd_done, 1)
                if l0:
                    x = x_in[:, p, :, :].rearrange("p (s t) c -> p s t c", s=2)
                    n = xn[:, :, :].rearrange("p (s t) c -> p s t c", s=2)
                    pool.wait_ge(xn_done, b.n + 1)
                    pool.tensor_tensor(out=x, in0=n, in1=c.pair("l0_q_g"), op=ALU.mult).then_inc(scaled, 1)
                    pool.wait_ge(scaled, b.n + 1)
                    pool.tensor_tensor(out=x, in0=x, in1=c.pair("l0_q_b"), op=ALU.add).then_inc(ln_done, 1)

            def pre(b, f):
                p = b.k % 2
                if f == 0:
                    return
                if f == V_JOBS[0]:
                    for job in {Q_JOB, K_JOB}:
                        bk, k = F(job)
                        pool.wait_ge(bk.free, bk.nth(b.n, k) + 1)
                    for t in range(z.ct):
                        heads = slice(t * z.heads_a_tile, (t + 1) * z.heads_a_tile)
                        shape = [P, z.heads_a_tile, z.nk]
                        pool.tensor_tensor(out=k_blocks[:, heads, :],
                                           in0=KT[p][:, t, :].unsqueeze(1).to_broadcast(shape),
                                           in1=c.head_mask(z.dh)[:, heads].unsqueeze(2).to_broadcast(shape),
                                           op=ALU.mult).then_inc(blocks_ready, 1)
                    pool.tensor_copy(q_bf[:, :, :], QT[p]).then_inc(blocks_ready, 1)

            def stream(b, n):
                if masked and n < z.turned_jobs:
                    pool.wait_ge(turned[0].free, turned[0].nth(b.n, n) + 1)
                    p = b.k % 2 if cross else 0
                    pool.tensor_tensor(out=by_head(t_biased[:, n % 2, :]), in0=by_head(t_masked[:, n % 2, :]),
                                       in1=all_heads(mask_add[:, p, 1, :]), op=ALU.add).then_inc(t_ready, 1)

            def score(b, j):
                if masked:
                    bk, k = F(n_pre + j)
                    pool.wait_ge(bk.free, bk.nth(b.n, k) + 1)
                    p = b.k % 2 if cross else 0
                    pool.tensor_tensor(out=by_head(s_biased[:, j % 2, :]), in0=by_head(s_masked[:, j % 2, :]),
                                       in1=all_heads(mask_add[:, p, 0, :]), op=ALU.add).then_inc(s_ready, 1)

            def tail(b, m):
                if TAIL and m == OUT:
                    pool.wait_ge(var_b_done, b.n + 1)
                    n = z.qt
                    inverse_root(pool, c, rstd_b_part, b.n, mean_var_b[:, 0:n, 1:2], rstd_b[:, 0:n, :],
                                 1e-5 if l0 else 1e-6, n).then_inc(rstd_b_done, 1)

            def both(fr, bk):
                if fr is not None:
                    begin(fr, bk is None)
                order(fr, bk, pre, stream, score, tail, lambda b: None)

            pipelined(pool, B, 2, both)

        @block.tensor
        def _(pe):
            pe.wait_ge(set_up, 6 if l1 else 3)

            def pre(b, f):
                p = b.k % 2
                bk, k = F(f)
                out = bk.ap
                if f == T:
                    if l1:
                        pe.wait_ge(x_ready, b.n + 1)
                    elif l0:
                        pe.wait_ge(ln_done, b.n + 1)
                    else:
                        pe.wait_ge(xn_done, b.n + 1)
                    pe.wait_ge(bk.free, bk.nth(b.n, k))
                    for t in range(4 if l0 else 2):
                        src = x_in[:, p, t, :] if l0 else x_in[:, p, t * P:(t + 1) * P] if l1 else xn[:, t, :]
                        last = pe.transpose(out[:, t * P:(t + 1) * P], src, c.ident[:, :])
                    last.then_inc(bk.full, 1)
                    return
                tk, t0 = F(T)
                pe.wait_ge(tk.free, tk.nth(b.n, t0) + 1)
                if l1 or cross:
                    pe.wait_ge(x_loaded[p], (b.n - p) * 8 + 16)
                pe.wait_ge(bk.free, bk.nth(b.n, k))
                own = x_T[:, 0:2 * P].rearrange("p (t s) -> p t s", t=2)
                w = c.w
                if l0:
                    if f == K_JOB:
                        pe.matmul(out[:, 0:256], w["l0_wq"][:, 0, :], x_T[:, 0:256], start=True, stop=True)
                        last = pe.matmul(out[:, 256:512], w["l0_wk"][:, 0, :], x_T[:, 256:512], start=True, stop=True)
                    else:
                        for t in range(2):
                            last = pe.matmul(out[:, t * P:(t + 1) * P], x_T[:, (2 + t) * P:(3 + t) * P],
                                             w["l0_wv"][:, 0, :], start=True, stop=True)
                elif l1:
                    other = ctx_in[:, p, :, :]
                    if f == K_JOB:
                        for m in range(2):
                            for half, src in enumerate((other, own)):
                                for t in range(2):
                                    last = pe.matmul(out[:, m * 256 + half * P:m * 256 + (half + 1) * P],
                                                     w["l1_wk"][:, t, m * P:(m + 1) * P], src[:, t, :],
                                                     start=(t == 0), stop=(t == 1))
                    elif f == Q_JOB:
                        for m in range(2):
                            for t in range(2):
                                last = pe.matmul(out[:, m * P:(m + 1) * P], w["l1_wq"][:, t, m * P:(m + 1) * P],
                                                 own[:, t, :], start=(t == 0), stop=(t == 1))
                    else:
                        src = (other, own)[f - V_JOBS[0]]
                        for t in range(2):
                            last = pe.matmul(out[:, 0:D], src[:, t, :], w["l1_wv"][:, t, :],
                                             start=(t == 0), stop=(t == 1))
                else:
                    other = ctx_in[:, p, :, :] if cross else own
                    wq, wk, wv = (w["l3_wqc"], w["l3_wkc"], w["l3_wvc"]) if cross else (w["l3_wq"], w["l3_wk"], w["l3_wv"])
                    if f == K_JOB:
                        for j, (wt, src) in enumerate(((wq, own), (wk, other))):
                            for m in range(2):
                                for t in range(2):
                                    last = pe.matmul(out[:, (2 * j + m) * P:(2 * j + m + 1) * P],
                                                     wt[:, t, m * P:(m + 1) * P], src[:, t, :],
                                                     start=(t == 0), stop=(t == 1))
                    else:
                        for t in range(2):
                            last = pe.matmul(out[:, 0:D], other[:, t, :], wv[:, t, :], start=(t == 0), stop=(t == 1))
                last.then_inc(bk.full, 1)

            def score(b, j):
                per_tile = H // z.hk
                q, h = j // per_tile, j % per_tile * z.hk
                if j == 0:
                    pe.wait_ge(blocks_ready, b.times(1 + z.ct, 1 + z.ct))
                bk, k = F(n_pre + j)
                pe.wait_ge(bk.free, bk.nth(b.n, k))
                t = h // z.heads_a_tile
                last = pe.matmul(bk.ap[:, :], q_bf[:, t, q * P:(q + 1) * P], k_blocks[:, h:h + z.hk, :],
                                 start=True, stop=not l1)
                if l1:
                    last = pe.matmul(bk.ap[:, :], c.ones_bf[:, :],
                                     mask_row[:, b.n, :].unsqueeze(1).to_broadcast([P, z.hk, z.nk]),
                                     start=False, stop=True)
                last.then_inc(bk.full, 1)

            def last_front(b):
                bk, k = F(N_JOB)
                pe.wait_ge(max_done, b.times(3, 3))
                pe.wait_ge(bk.free, bk.nth(b.n, k))
                for q in range(z.qt):
                    last = pe.transpose(bk.ap[:, :].bitcast(BF16)[:, q * P:(q + 1) * P], neg_max_bf[:, q, :],
                                        c.ident_bf[:, :])
                last.then_inc(bk.full, 1)

            def stream(b, n):
                p = b.k % 2
                if n == 0:
                    bk, k = F(N_JOB)
                    pe.wait_ge(bk.free, bk.nth(b.n, k) + 1)
                    for job in V_JOBS:
                        bk, k = F(job)
                        pe.wait_ge(bk.free, bk.nth(b.n, k) + 1)
                    pe.wait_ge(q_blocks_ready, b.times(z.ct, z.ct))
                if n < z.turned_jobs:
                    chunk, kt = n // z.kt, n % z.kt
                    h = chunk * z.hq
                    t = h // z.heads_a_tile
                    bk, k = (turned[0], n) if masked else (turned[n % 2], n // 2)
                    pe.wait_ge(bk.free, bk.nth(b.n, k))
                    last = pe.matmul(bk.ap[:, :], KT[p][:, t, kt * P:(kt + 1) * P], q_blocks[:, p, h:h + z.hq, :],
                                     start=True, stop=True)
                    if masked:
                        last.then_inc(bk.full, 1)
                        bk = turned[1]
                        pe.wait_ge(bk.free, bk.nth(b.n, n))
                    for i in range(z.hq):
                        last = pe.matmul(bk.ap[:, i * z.nq:(i + 1) * z.nq],
                                         c.select16[:, h + i:h + i + 1].to_broadcast([P, P]), neg_max_T[:, p, :],
                                         start=masked, stop=True, skip_group_check=not masked)
                    last.then_inc(bk.full, 1)
                if n >= lag:
                    m = n - lag
                    chunk, kt = m // z.kt, m % z.kt
                    pe.wait_ge(probs_ready, b.times(z.turned_jobs, m + 1))
                    for i in range(z.hq):
                        h = chunk * z.hq + i
                        g, j = h // 4, h % 4
                        cb, at = g * z.nq // BANK, g * z.nq % BANK
                        if kt == 0 and j == 0 and at == 0:
                            pe.wait_ge(context[cb].free, b.n + 1)
                        last = pe.matmul(context[cb].ap[j * SLOT:(j + 1) * SLOT, at:at + z.nq], V[:, p, kt, h, :],
                                         PT[:, m % 3, i * z.nq:(i + 1) * z.nq],
                                         start=(kt == 0), stop=(kt == z.kt - 1))
                    if kt == z.kt - 1 and (h + 1) * z.nq % (4 * BANK) == 0:
                        last.then_inc(context[cb].full, 1)

            def tail(b, m):
                bk, k = back[m % 2], m // 2
                out = bk.ap
                if m in TURN:
                    if m == 0:
                        for cb in context:
                            pe.wait_ge(cb.free, b.n + 2)
                    pe.wait_ge(bk.free, bk.nth(b.n, k))
                    for g in range(4):
                        last = pe.transpose(out[:, g * P:(g + 1) * P], ctx_den[:, g, m * P:(m + 1) * P], c.ident[:, :])
                elif m in CTX_T:
                    for j in TURN:
                        pe.wait_ge(back[j % 2].free, back[j % 2].nth(b.n, j // 2) + 1)
                    pe.wait_ge(bk.free, bk.nth(b.n, k))
                    flat = ctx_q[:, :, :, :].rearrange("p q h d -> p q (h d)")
                    for i in range(2 if not masked else 1):
                        src = flat[:, i, :] if l0 else flat[:, 0, (m - 1 + i) * P:(m + i) * P]
                        last = pe.transpose(out[:, i * P:(i + 1) * P], src, c.ident[:, :])
                elif m == OUT:
                    for j in CTX_T:
                        pe.wait_ge(back[j % 2].free, back[j % 2].nth(b.n, j // 2) + 1)
                    pe.wait_ge(bk.free, bk.nth(b.n, k))
                    wo = c.w["l0_wo" if l0 else "l1_wo" if l1 else "l3_wco" if cross else "l3_wao"]
                    for q in range(z.qt):
                        for t in range(z.ct):
                            last = pe.matmul(out[:, q * width:(q + 1) * width], ctx_T[:, t, q * P:(q + 1) * P],
                                             wo[:, t, :], start=(t == 0), stop=(t == z.ct - 1))
                else:
                    src = r
                    if m == TAIL[0]:
                        pe.wait_ge(rn_done, b.n + 1)
                        src = rn
                    pe.wait_ge(bk.free, bk.nth(b.n, k))
                    flat = src[:, :, :].rearrange("p q c -> p (q c)")
                    for i in range(2):
                        last = pe.transpose(out[:, i * P:(i + 1) * P], flat[:, i * P:(i + 1) * P], c.ident[:, :])
                last.then_inc(bk.full, 1)

            pipelined(pe, B, 2, lambda fr, bk: order(fr, bk, pre, stream, score, tail, last_front))

        @block.scalar
        def _(act):
            act.wait_ge(set_up, 6 if l1 else 3)

            def pre(b, f):
                p = b.k % 2
                bk, k = F(f)
                if f in V_JOBS:
                    return
                act.wait_ge(bk.full, bk.nth(b.n, k))
                if f == T:
                    if masked:
                        g, be = ("l3_ln2_g", "l3_ln2_b") if cross else ("l3_ln1_g", "l3_ln1_b")
                        for t in range(2):
                            last = act.activation(x_T[:, t * P:(t + 1) * P], bk.ap[:, t * P:(t + 1) * P], ACT.Identity,
                                                  bias=c.col(be, t), scale=c.col(g, t))
                    else:
                        n = 4 if l0 else 2
                        last = act.activation(x_T[:, 0:n * P], bk.ap[:, 0:n * P], ACT.Copy)
                elif l0:
                    last = act.activation(QK[:, p, :], bk.ap[:, :], ACT.Copy)
                elif l1:
                    dst, name = (QT[p], "l1_q_b") if f == Q_JOB else (KT[p], "l1_k_b")
                    n = z.nq if f == Q_JOB else z.nk
                    for t in range(2):
                        last = act.activation(dst[:, t, :], bk.ap[:, t * n:(t + 1) * n], ACT.Identity,
                                              bias=c.col(name, t), scale=1.0)
                else:
                    for j, (dst, name) in enumerate(((QT[p], "l3_q_b"), (KT[p], "l3_k_b"))):
                        for t in range(2):
                            last = act.activation(dst[:, t, :], bk.ap[:, (2 * j + t) * P:(2 * j + t + 1) * P],
                                                  ACT.Identity, bias=c.col(name + ("2" if cross else "1"), t), scale=1.0)
                last.then_inc(bk.free, 1)

            def stream(b, n):
                if n >= z.turned_jobs:
                    return
                if l1 and n == 0:
                    act.activation(mask_step[:, :], mask_col[:, bass.ds(b.n, 1)], ACT.Copy).then_inc(mask_copied, 1)
                    act.wait_ge(mask_copied, b.n + 1)
                if masked:
                    act.wait_ge(turned[1].free, turned[1].nth(b.n, n) + 1)
                    act.activation(PT[:, n % 3, :], t_shifted[:, n % 2, :], ACT.Exp).then_inc(probs_ready, 1)
                    return
                bk, k = turned[n % 2], n // 2
                act.wait_ge(bk.full, bk.nth(b.n, k))
                bias = mask_step[:, :] if l1 and n % z.kt == 0 else 0.0
                act.activation(PT[:, n % 3, :], bk.ap[:, :], ACT.Exp, bias=bias, scale=z.scale).then_inc(probs_ready, 1)
                act.wait_ge(probs_ready, b.times(z.turned_jobs, n + 1))
                act.sem_inc(bk.free, 1)

            def tail(b, m):
                bk, k = back[m % 2], m // 2
                if m in TURN or m == OUT:
                    return
                act.wait_ge(bk.full, bk.nth(b.n, k))
                if m in CTX_T:
                    if l0:
                        last = act.activation(ctx_T[:, 0, :], bk.ap[:, 0:z.nq], ACT.Copy)
                    else:
                        name = "l1_v_b" if l1 else "l3_v_b2" if cross else "l3_v_b1"
                        for i in range(2 if not masked else 1):
                            t = m - 1 + i
                            last = act.activation(ctx_T[:, t, :], bk.ap[:, i * P:(i + 1) * P], ACT.Identity,
                                                  bias=c.col(name, t), scale=1.0)
                elif l0:
                    carry_wait(act, c)
                    if m == TAIL[0]:
                        last = act.activation(c.nT_flat[:, bass.ds(b.n * 256, 256)], bk.ap[:, 0:256], ACT.Identity,
                                              bias=c.col("l0_ffn_b", 0), scale=c.col("l0_ffn_g", 0))
                    else:
                        last = act.activation(c.acc_flat[:, bass.ds(b.n * 256, 256)], bk.ap[:, 0:256], ACT.Copy)
                else:
                    carry_wait(act, c)
                    for t in range(2):
                        last = act.activation(c.nT[:, t, b.n, :], bk.ap[:, t * P:(t + 1) * P], ACT.Copy,
                                              scale=c.col("l1_post", t))
                last.then_inc(bk.free, 1)

            nothing = lambda b, j: None
            pipelined(act, B, 2, lambda fr, bk: order(fr, bk, pre, stream, nothing, tail, lambda b: None))

        @block.vector
        def _(dve):
            dve.wait_ge(set_up, 6 if l1 else 3)

            def begin(b):
                p = b.k % 2
                tiles = [x_in[:, p, t, :] for t in range(4)] if l0 else [c.x[:, b.n, :]]
                if l0:
                    dve.wait_ge(x_ready, b.n + 1)
                for t, x in enumerate(tiles):
                    last = dve.bn_stats(stats[:, t, :], x)
                last.then_inc(stats_done, 1)
                dve.wait_ge(stats_done, b.n + 1)
                dve.memset(c.waiter[:, :], 0.0)
                for t in range(len(tiles)):
                    last = dve.bn_aggr(mean_var[:, t, :], stats[:, t, :])
                last.then_inc(var_done, 1)
                dve.wait_ge(rstd_done, b.n + 1)
                for t, x in enumerate(tiles):
                    out = xn[:, t, :] if l0 else xn[:, 0:2, :].rearrange("p t c -> p (t c)")
                    last = dve.tensor_scalar(out=out, in0=x, scalar1=mean_var[:, t, 0:1], scalar2=rstd[:, t, :],
                                             op0=ALU.subtract, op1=ALU.mult)
                last.then_inc(xn_done, 1)

            def pre(b, f):
                p = b.k % 2
                if f not in V_JOBS:
                    return
                bk, k = F(f)
                dve.wait_ge(bk.full, bk.nth(b.n, k))
                for t in range(2 if l0 else 1):
                    kt = t if l0 else f - V_JOBS[0]
                    src = bk.ap[:, t * width:(t + 1) * width].rearrange("p (h d) -> p h d", h=H)
                    last = dve.tensor_copy(V[:, p, kt, :, 0:z.dh], src)
                last.then_inc(bk.free, 1)
                if f == V_JOBS[0]:
                    bk, k = F(Q_JOB)
                    dve.wait_ge(bk.free, bk.nth(b.n, k) + 1)
                    for t in range(z.ct):
                        heads = slice(t * z.heads_a_tile, (t + 1) * z.heads_a_tile)
                        shape = [P, z.heads_a_tile, z.nq]
                        dve.tensor_tensor(out=q_blocks[:, p, heads, :],
                                          in0=QT[p][:, t, :].unsqueeze(1).to_broadcast(shape),
                                          in1=c.head_mask(z.dh)[:, heads].unsqueeze(2).to_broadcast(shape),
                                          op=ALU.mult).then_inc(q_blocks_ready, 1)

            def maximum(b, j, src):
                per_tile = H // z.hk
                q, h = j // per_tile, j % per_tile * z.hk
                return dve.tensor_reduce(neg_max[:, q, h:h + z.hk], src.rearrange("p (h k) -> p h k", h=z.hk), AX,
                                         ALU.max, negate=True)

            def score(b, j):
                bk, k = F(n_pre + j)
                dve.wait_ge(bk.full, bk.nth(b.n, k))
                if not masked:
                    maximum(b, j, bk.ap[:, :]).then_inc(bk.free, 1)
                    return
                p = b.k % 2 if cross else 0
                if cross:
                    dve.wait_ge(mask_made, b.times(2, 2))
                dve.tensor_tensor(out=by_head(s_masked[:, j % 2, :]), in0=by_head(bk.ap[:, :]),
                                  in1=all_heads(mask_mul[:, p, 0, :]), op=ALU.mult).then_inc(bk.free, 1)
                if j > 0:
                    dve.wait_ge(s_ready, b.times(4, j))
                    maximum(b, j - 1, s_biased[:, (j - 1) % 2, :])

            def last_front(b):
                if masked:
                    dve.wait_ge(s_ready, b.times(4, 4))
                    maximum(b, 3, s_biased[:, 1, :]).then_inc(max_done, 1)
                    dve.wait_ge(max_done, b.times(3, 1))
                else:
                    for j in (z.score_jobs - 2, z.score_jobs - 1):
                        bk, k = F(n_pre + j)
                        dve.wait_ge(bk.free, bk.nth(b.n, k) + 1)
                    dve.sem_inc(max_done, 1)
                dve.tensor_copy(neg_max_bf[:, :, 0:H], neg_max[:, :, :]).then_inc(max_done, 1)
                dve.wait_ge(max_done, b.times(3, 2))
                dve.tensor_tensor(out=neg_max_bf[:, :, H:2 * H], in0=neg_max[:, :, :], in1=neg_max_bf[:, :, 0:H],
                                  op=ALU.subtract).then_inc(max_done, 1)
                bk, k = F(N_JOB)
                dve.wait_ge(bk.full, bk.nth(b.n, k))
                dve.tensor_copy(neg_max_T[:, b.k % 2, :], bk.ap[:, :].bitcast(BF16)[:, 0:z.nq]).then_inc(bk.free, 1)

            def shift(b, n):
                dve.wait_ge(turned[1].full, turned[1].nth(b.n, n))
                dve.wait_ge(t_ready, b.times(4, n + 1))
                if n >= 2:
                    dve.wait_ge(probs_ready, b.times(4, n - 1))
                dve.tensor_tensor(out=t_shifted[:, n % 2, :], in0=t_biased[:, n % 2, :], in1=turned[1].ap[:, :],
                                  op=ALU.add).then_inc(turned[1].free, 1)

            def stream(b, n):
                if masked:
                    if n < z.turned_jobs:
                        p = b.k % 2 if cross else 0
                        dve.wait_ge(turned[0].full, turned[0].nth(b.n, n))
                        dve.tensor_tensor(out=by_head(t_masked[:, n % 2, :]), in0=by_head(turned[0].ap[:, :]),
                                          in1=all_heads(mask_mul[:, p, 1, :]), op=ALU.mult).then_inc(turned[0].free, 1)
                    if 1 <= n <= z.turned_jobs:
                        shift(b, n - 1)
                for i, cb in enumerate(context):
                    if n == (z.turned_jobs * (i + 1)) // len(context) + lag - 1:
                        dve.wait_ge(cb.full, b.n + 1)
                        per = 4 // len(context)
                        dve.tensor_copy(ctx_den[:, i * per:(i + 1) * per, :].rearrange("p g q -> p (g q)"),
                                        cb.ap[:, 0:per * z.nq]).then_inc(cb.free, 1)

            def tail(b, m):
                p = b.k % 2
                bk, k = back[m % 2], m // 2
                if m in TURN:
                    dve.wait_ge(bk.full, bk.nth(b.n, k))
                    slots = bk.ap[:, :].rearrange("p (h s) -> p h s", h=H)
                    dve.reciprocal(rden[:, m, :, :], slots[:, :, z.dh:z.dh + 1]).then_inc(rden_done, 1)
                    dve.wait_ge(rden_done, b.times(z.qt, m + 1))
                    dve.tensor_tensor(out=ctx_q[:, m, :, :], in0=slots[:, :, 0:z.dh],
                                      in1=rden[:, m, :, :].to_broadcast([P, H, z.dh]), op=ALU.mult).then_inc(bk.free, 1)
                elif m == OUT:
                    dve.wait_ge(bk.full, bk.nth(b.n, k))
                    if masked:
                        dve.tensor_tensor(out=c.x[:, b.n, :], in0=res[:, p, :], in1=bk.ap[:, 0:D], op=ALU.add)\
                            .then_inc(bk.free, 1)
                        return
                    flat = r[:, :, :].rearrange("p q c -> p (q c)")
                    src = x_in[:, p, 0:2, :].rearrange("p t c -> p (t c)") if l0 else res[:, p, :]
                    dve.tensor_tensor(out=flat, in0=src, in1=bk.ap[:, 0:256], op=ALU.add).then_inc(bk.free, 1)
                    dve.wait_ge(bk.free, bk.nth(b.n, k) + 1)
                    if l0:
                        for q in range(z.qt):
                            last = dve.bn_stats(stats_b[:, q, :], r[:, q, :])
                        last.then_inc(stats_b_done, 1)
                        dve.wait_ge(stats_b_done, b.n + 1)
                        dve.memset(c.waiter[:, :], 0.0)
                        for q in range(z.qt):
                            last = dve.bn_aggr(mean_var_b[:, q, :], stats_b[:, q, :])
                        last.then_inc(var_b_done, 1)
                        dve.wait_ge(rstd_b_done, b.n + 1)
                        for q in range(z.qt):
                            last = dve.tensor_scalar(out=rn[:, q, :], in0=r[:, q, :], scalar1=mean_var_b[:, q, 0:1],
                                                     scalar2=rstd_b[:, q, :], op0=ALU.subtract, op1=ALU.mult)
                        last.then_inc(rn_done, 1)
                    else:
                        dve.tensor_tensor_reduce(out=rn[:, 0, :], in0=r[:, 0, :], in1=r[:, 0, :], scale=1.0 / D,
                                                 scalar=0.0, op0=ALU.mult, op1=ALU.add,
                                                 accum_out=mean_var_b[:, 0, 1:2]).then_inc(var_b_done, 1)
                        dve.wait_ge(rstd_b_done, b.n + 1)
                        dve.tensor_scalar(out=rn[:, 0, :], in0=r[:, 0, :], scalar1=rstd_b[:, 0, :], scalar2=None,
                                          op0=ALU.mult).then_inc(rn_done, 1)

            def both(fr, bk):
                if fr is not None and not l1:
                    begin(fr)
                order(fr, bk, pre, stream, score, tail, last_front)

            pipelined(dve, B, 2, both)


def extra_scores(c, a):
    nc = c.nc
    with ExitStack() as ctx:
        def sb(n, shape, dt=F32):
            return ctx.enter_context(nc.sbuf_tensor(f"l2x{a}_{n}", shape, dt))

        sems = []

        def sem(n):
            sems.append(ctx.enter_context(nc.semaphore(f"l2x{a}_{n}")))
            return sems[-1]

        W = H * P
        wq = sb("wq", [P, 2, W])
        vectors = sb("vectors", [P, 4, W])
        U = sb("U", [P, 2, H])
        offset = sb("offset", [P, H])
        psum = ctx.enter_context(nc.psum_tensor(f"l2x{a}_psum", [P, BANK], F32))
        loaded, multiplied, summed, scored, done = (sem(n) for n in ("loaded", "multiplied", "summed", "scored", "done"))
        ctx.callback(clear_semaphores, nc, sems)
        block = ctx.enter_context(nc.Block())

        @block.sync
        def _(sync):
            sync.dma_start(wq[:, :, :], c.dram[f"l2_wq{a}"].rearrange("(t p) n -> p t n", p=P)).then_inc(loaded, 16)
            sync.dma_start(vectors[:, :, :], c.dram[f"l2_rows{a}"].rearrange("(a v) n -> a v n", a=1)
                           .to_broadcast([P, 4, W])).then_inc(loaded, 16)

        @block.gpsimd
        def _(pool):
            pool.wait_ge(loaded, 32)
            pool.tensor_tensor(out=c.value_bias[:, :], in0=vectors[:, 2, :], in1=vectors[:, 3, :], op=ALU.subtract)\
                .then_inc(done, 1)
            for t in range(2):
                pool.tensor_copy(c.acc[:, t, :, :].rearrange("p b s -> p (b s)"),
                                 c.col(f"l2_bo{a}", t).to_broadcast([P, B * S])).then_inc(done, 1)

        @block.vector
        def _(dve):
            dve.wait_ge(loaded, 32)
            for t in range(2):
                dve.tensor_tensor(out=wq[:, t, :], in0=wq[:, t, :], in1=vectors[:, 1, :], op=ALU.mult)\
                    .then_inc(multiplied, 1)
            dve.tensor_tensor(out=vectors[:, 0, :], in0=vectors[:, 0, :], in1=vectors[:, 1, :], op=ALU.mult)\
                .then_inc(multiplied, 1)
            dve.wait_ge(multiplied, 3)
            for t in range(2):
                dve.tensor_reduce(U[:, t, :], wq[:, t, :].rearrange("p (h d) -> p h d", h=H), AX, ALU.add)\
                    .then_inc(summed, 1)
            dve.tensor_reduce(offset[:, :], vectors[:, 0, :].rearrange("p (h d) -> p h d", h=H), AX, ALU.add)\
                .then_inc(summed, 1)
            dve.wait_ge(summed, 3)
            dve.wait_ge(scored, 1)
            dve.tensor_tensor(out=c.extra[:, :, :], in0=psum[:, 0:B * H].rearrange("p (b h) -> p h b", h=H),
                              in1=offset[:, :].unsqueeze(2).to_broadcast([P, H, B]), op=ALU.add).then_inc(done, 1)

        @block.tensor
        def _(pe):
            pe.wait_ge(summed, 2)
            for b in range(B):
                for t in range(2):
                    last = pe.matmul(psum[:, b * H:(b + 1) * H], c.nT[:, t, b, :], U[:, t, :],
                                     start=(t == 0), stop=(t == 1))
            last.then_inc(scored, 1)


def wide_heads(c, a):
    nc = c.nc
    G = 4
    T = G * S
    scale = float(P) ** -0.5
    steps = H * G
    with ExitStack() as ctx:
        def sb(n, shape, dt=F32):
            return ctx.enter_context(nc.sbuf_tensor(f"l2h{a}_{n}", shape, dt))

        sems = []

        def sem(n):
            sems.append(ctx.enter_context(nc.semaphore(f"l2h{a}_{n}")))
            return sems[-1]

        weights = sb("weights", [P, 2, 4, D])
        QT = sb("QT", [P, 2, T])
        KT = sb("KT", [P, 2, T])
        q_bf = sb("q_bf", [P, T], BF16)
        k_bf = sb("k_bf", [P, T], BF16)
        V = sb("V", [P, 2, G, P + 1])
        max_s = sb("max_s", [P, G])
        max_all = sb("max_all", [P, G])
        shift = sb("shift", [P, P], BF16)
        extra_arg = sb("extra_arg", [P, 2, G])
        extra_prob = sb("extra_prob", [P, 2, G])
        shift_T = sb("shift_T", [P, 2, P], BF16)
        PT = sb("PT", [P, T])
        den = sb("den", [P, G])
        rden = sb("rden", [P, G])
        ctx_q = sb("ctx_q", [P, G, P])
        ctx_T = sb("ctx_T", [P, T])
        head_vectors = sb("head_vectors", [P, 2, 4, 1])
        banks = [ctx.enter_context(nc.psum_tensor(f"l2h{a}_psum{i}", [P, BANK], F32)) for i in range(8)]

        def bank(n, what, jobs):
            return Bank(banks[n], sem(f"{what}_full"), sem(f"{what}_free"), jobs)

        q_bank = bank(0, "q", 1)
        k_bank = bank(1, "k", 1)
        v_bank = bank(2, "v", 1)
        s_bank = bank(3, "s", 2)
        t_bank = bank(4, "t", 2)
        pv_bank = [bank(5, "pv0", 1), bank(6, "pv1", 1)]
        o_bank = bank(7, "o", 2)

        weights_loaded = [sem(f"weights_loaded{p}") for p in range(2)]
        set_up = sem("set_up")
        copied = sem("copied")
        max_done = sem("max_done")
        extra_ready = sem("extra_ready")
        vectors_ready = sem("vectors_ready")
        probs_ready = sem("probs_ready")
        den_done = sem("den_done")
        ctx.callback(clear_semaphores, nc, sems)
        block = ctx.enter_context(nc.Block())
        OPS = 6

        def head(s):
            return s.i * 2 + s.k // G

        @block.sync
        def _(sync):
            for bk in [q_bank, k_bank, v_bank, s_bank, t_bank, o_bank] + pv_bank:
                sync.sem_inc(bk.free, 1)

            def load(h, p):
                sync.dma_start(weights[:, p, :, :], c.dram[f"l2_heads{a}"][h].rearrange("w p n -> p w n"))\
                    .then_inc(weights_loaded[p], 16)

            for p in range(2):
                load(p, p)
            with sync.Fori(1, H // 2) as i:
                for p in range(2):
                    sync.wait_ge(o_bank.full, ((i - 1) * 2 + p + 1) * G * 2)
                    load(i * 2 + p, p)

        @block.gpsimd
        def _(pool):
            pool.memset(shift[:, :], 0.0).then_inc(set_up, 1)
            pool.memset(V[:, :, :, P:P + 1], 1.0).then_inc(set_up, 1)

        @block.tensor
        def _(pe):
            pe.wait_ge(set_up, 2)

            def front_w(s, which):
                return weights[:, (s.k // G) % 2, which, :].rearrange("p (t n) -> p t n", t=2)

            def q_or_k(s, which):
                if which == 0 and s.k % G == 0:
                    pe.wait_ge(weights_loaded[(s.k // G) % 2], (s.i + s.k // 8) * 16 + 16)
                g = s.k % G
                bk = (q_bank, k_bank)[which]
                src = (c.nT, c.ctx_T)[which]
                pe.wait_ge(bk.free, s.n + 1)
                for t in range(2):
                    last = pe.matmul(bk.ap[:, :], front_w(s, which)[:, t, :], src[:, t, g * G:(g + 1) * G, :],
                                     start=(t == 0), stop=(t == 1))
                last.then_inc(bk.full, 1)

            def values(s):
                g = s.k % G
                pe.wait_ge(v_bank.free, s.n + 1)
                for i in range(G):
                    for t in range(2):
                        last = pe.matmul(v_bank.ap[:, i * P:(i + 1) * P], c.ctx_T[:, t, g * G + i, :],
                                         front_w(s, 2)[:, t, :], start=(t == 0), stop=(t == 1))
                last.then_inc(v_bank.full, 1)

            def scores(s):
                pe.wait_ge(copied, s.times(2, 2))
                pe.wait_ge(s_bank.free, s_bank.nth(s.n, 0))
                for i in range(G):
                    last = pe.matmul(s_bank.ap[:, i * S:(i + 1) * S], q_bf[:, i * S:(i + 1) * S],
                                     k_bf[:, i * S:(i + 1) * S], start=True, stop=True)
                last.then_inc(s_bank.full, 1)

            def turn_shift(s):
                pe.wait_ge(max_done, s.times(OPS, OPS - 2))
                pe.wait_ge(s_bank.free, s_bank.nth(s.n, 1))
                pe.transpose(s_bank.ap[:, :].bitcast(BF16)[:, 0:P], shift[:, :], c.ident_bf[:, :])\
                    .then_inc(s_bank.full, 1)

            def scores_T(s):
                p = s.k % 2
                pe.wait_ge(s_bank.free, s_bank.nth(s.n, 1) + 1)
                pe.wait_ge(t_bank.free, t_bank.nth(s.n, 0))
                for i in range(G):
                    cols = slice(i * S, (i + 1) * S)
                    pe.matmul(t_bank.ap[:, cols], KT[:, p, cols], QT[:, p, cols], start=True, stop=False)
                    last = pe.matmul(t_bank.ap[:, cols], c.select4[:, i:i + 1].to_broadcast([P, P]), shift_T[:, p, :],
                                     start=False, stop=True)
                last.then_inc(t_bank.full, 1)

            def context(s):
                p = s.k % 2
                pe.wait_ge(v_bank.free, s.n + 2)
                pe.wait_ge(t_bank.free, t_bank.nth(s.n, 0) + 1)
                for i in range(G):
                    bk = pv_bank[i // 2]
                    if i % 2 == 0:
                        pe.wait_ge(bk.free, s.n + 1)
                    last = pe.matmul(bk.ap[:, (i % 2) * (P + 1):(i % 2 + 1) * (P + 1)], PT[:, i * S:(i + 1) * S],
                                     V[:, p, i, :], start=True, stop=True)
                    if i % 2 == 1:
                        last.then_inc(bk.full, 1)

            def turn_context(s):
                for bk in pv_bank:
                    pe.wait_ge(bk.free, s.n + 2)
                for i in range(G):
                    last = pe.transpose(t_bank.ap[:, i * P:(i + 1) * P], ctx_q[:, i, :], c.ident[:, :])
                last.then_inc(t_bank.full, 1)

            def output(s, t):
                wo = weights[:, (s.k // G) % 2, 3, :]
                if t == 0:
                    pe.wait_ge(t_bank.free, t_bank.nth(s.n, 1) + 1)
                pe.wait_ge(o_bank.free, o_bank.nth(s.n, t))
                pe.matmul(o_bank.ap[:, :], wo[:, t * P:(t + 1) * P], ctx_T[:, :], start=True, stop=True)\
                    .then_inc(o_bank.full, 1)

            def both(fr, bk):
                if bk is not None:
                    scores_T(bk)
                if fr is not None:
                    q_or_k(fr, 0)
                    q_or_k(fr, 1)
                if bk is not None:
                    context(bk)
                if fr is not None:
                    values(fr)
                if bk is not None:
                    turn_context(bk)
                if fr is not None:
                    scores(fr)
                if bk is not None:
                    output(bk, 0)
                    output(bk, 1)
                if fr is not None:
                    turn_shift(fr)

            pipelined(pe, steps, 8, both)

        @block.scalar
        def _(act):
            def vectors(s):
                at = COL_AT[f"l2_bq{a}"][0]
                act.activation(head_vectors[:, (s.k // G) % 2, :, :],
                               c.cols[:, at:at + 4 * H].rearrange("p (v h) -> p v h", v=4)[:, :, bass.ds(head(s), 1)],
                               ACT.Copy).then_inc(vectors_ready, 1)
                act.wait_ge(vectors_ready, head(s) + 1)

            def vector(s, which):
                return head_vectors[:, (s.k // G) % 2, which, :]

            def q_or_k(s, which):
                bk = (q_bank, k_bank)[which]
                dst = (QT, KT)[which][:, s.k % 2, :]
                act.wait_ge(bk.full, s.n + 1)
                act.activation(dst, bk.ap[:, :], ACT.Identity, bias=vector(s, which),
                               scale=1.0).then_inc(bk.free, 1)

            def probs(s):
                act.wait_ge(t_bank.full, t_bank.nth(s.n, 0))
                act.activation(PT[:, :], t_bank.ap[:, :], ACT.Exp, scale=scale).then_inc(t_bank.free, 1)

            def extra(s):
                act.wait_ge(max_done, s.times(OPS, OPS))
                act.activation(extra_prob[:, s.k % 2, :], extra_arg[:, s.k % 2, :], ACT.Exp, scale=scale)\
                    .then_inc(extra_ready, 1)

            def context(s):
                act.wait_ge(t_bank.full, t_bank.nth(s.n, 1))
                act.activation(ctx_T[:, :], t_bank.ap[:, :], ACT.Identity, bias=vector(s, 3), scale=1.0)\
                    .then_inc(t_bank.free, 1)

            def both(fr, bk):
                if bk is not None:
                    probs(bk)
                if fr is not None:
                    if fr.k % G == 0:
                        vectors(fr)
                    q_or_k(fr, 0)
                    q_or_k(fr, 1)
                if bk is not None:
                    context(bk)
                if fr is not None:
                    extra(fr)

            pipelined(act, steps, 8, both)

        @block.vector
        def _(dve):
            dve.wait_ge(set_up, 2)

            def copies(s):
                for bk, dst, src in ((q_bank, q_bf, QT), (k_bank, k_bf, KT)):
                    dve.wait_ge(bk.free, s.n + 2)
                    dve.tensor_copy(dst[:, :], src[:, s.k % 2, :]).then_inc(copied, 1)

            def values(s):
                dve.wait_ge(v_bank.full, s.n + 1)
                bias = c.value_bias[:, bass.ds(head(s) * P, P)].unsqueeze(1).to_broadcast([P, G, P])
                dve.tensor_tensor(out=V[:, s.k % 2, :, 0:P], in0=v_bank.ap[:, :].rearrange("p (i d) -> p i d", i=G),
                                  in1=bias, op=ALU.add).then_inc(v_bank.free, 1)

            def maxima(s):
                g, p = s.k % G, s.k % 2
                extra = c.extra[:, head(s), g * G:(g + 1) * G]
                dve.wait_ge(s_bank.full, s_bank.nth(s.n, 0))
                dve.tensor_reduce(max_s[:, :], s_bank.ap[:, :].rearrange("p (i k) -> p i k", i=G), AX, ALU.max)\
                    .then_inc(s_bank.free, 1)
                dve.wait_ge(s_bank.free, s_bank.nth(s.n, 0) + 1)
                dve.tensor_tensor(out=max_all[:, :], in0=max_s[:, :], in1=extra, op=ALU.max).then_inc(max_done, 1)
                dve.wait_ge(max_done, s.times(OPS, 1))
                dve.tensor_scalar(out=shift[:, 0:G], in0=max_all[:, :], scalar1=-1.0, scalar2=None, op0=ALU.mult)\
                    .then_inc(max_done, 1)
                dve.wait_ge(max_done, s.times(OPS, 2))
                dve.scalar_tensor_tensor(out=shift[:, G:2 * G], in0=max_all[:, :], scalar=-1.0, in1=shift[:, 0:G],
                                         op0=ALU.mult, op1=ALU.subtract).then_inc(max_done, 1)
                dve.tensor_tensor(out=extra_arg[:, p, :], in0=extra, in1=shift[:, 0:G], op=ALU.add)\
                    .then_inc(max_done, 1)
                dve.wait_ge(max_done, s.times(OPS, 4))
                dve.tensor_tensor(out=extra_arg[:, p, :], in0=extra_arg[:, p, :], in1=shift[:, G:2 * G], op=ALU.add)\
                    .then_inc(max_done, 1)
                dve.wait_ge(max_done, s.times(OPS, 5))
                dve.sem_inc(max_done, 1)

            def turned_shift(s):
                dve.wait_ge(s_bank.full, s_bank.nth(s.n, 1))
                dve.tensor_copy(shift_T[:, s.k % 2, :], s_bank.ap[:, :].bitcast(BF16)[:, 0:P]).then_inc(s_bank.free, 1)

            def context(s):
                p = s.k % 2
                dve.wait_ge(extra_ready, s.n + 1)
                for j, bk in enumerate(pv_bank):
                    two = slice(2 * j, 2 * j + 2)
                    pv = bk.ap[:, 0:2 * (P + 1)].rearrange("p (i d) -> p i d", i=2)
                    dve.wait_ge(bk.full, s.n + 1)
                    dve.tensor_tensor(out=den[:, two].unsqueeze(2), in0=extra_prob[:, p, two].unsqueeze(2),
                                      in1=pv[:, :, P:P + 1], op=ALU.add).then_inc(den_done, 1)
                    dve.wait_ge(den_done, s.times(4, 2 * j + 1))
                    dve.reciprocal(rden[:, two], den[:, two]).then_inc(den_done, 1)
                    dve.wait_ge(den_done, s.times(4, 2 * j + 2))
                    dve.tensor_tensor(out=ctx_q[:, two, :], in0=pv[:, :, 0:P],
                                      in1=rden[:, two].unsqueeze(2).to_broadcast([P, 2, P]), op=ALU.mult)\
                        .then_inc(bk.free, 1)

            def output(s, t):
                g = s.k % G
                acc = c.acc[:, t, g * G:(g + 1) * G, :].rearrange("p b s -> p (b s)")
                dve.wait_ge(o_bank.full, o_bank.nth(s.n, t))
                dve.tensor_tensor(out=acc, in0=acc, in1=o_bank.ap[:, :], op=ALU.add).then_inc(o_bank.free, 1)

            def both(fr, bk):
                if fr is not None:
                    copies(fr)
                if bk is not None:
                    context(bk)
                if fr is not None:
                    values(fr)
                    maxima(fr)
                if bk is not None:
                    output(bk, 0)
                    output(bk, 1)
                if fr is not None:
                    turned_shift(fr)

            pipelined(dve, steps, 8, both)


def build(nc, dram, out):
    c = Chip()
    c.nc, c.dram, c.out = nc, dram, out
    with ExitStack() as ctx:
        def sb(n, shape, dt=F32):
            return ctx.enter_context(nc.sbuf_tensor(n, shape, dt))

        c.x_flat = sb("x", [P, B * D])
        c.x = c.x_flat[:, :].rearrange("p (b d) -> p b d", b=B)
        c.nT_flat = sb("nT", [P, 2 * B * S])
        c.nT = c.nT_flat[:, :].rearrange("p (t b s) -> p t b s", t=2, b=B)
        c.acc_flat = sb("acc", [P, 2 * B * S])
        c.acc = c.acc_flat[:, :].rearrange("p (t b s) -> p t b s", t=2, b=B)
        c.cols = sb("cols", [P, N_COLS])
        c.rows = sb("rows", [P, N_ROWS])
        c.ident = sb("ident", [P, P])
        c.ident_bf = sb("ident_bf", [P, P], BF16)
        c.ones_bf = sb("ones_bf", [P, P], BF16)
        c.minus_half = sb("minus_half", [P, 4])
        c.epsilons = sb("epsilons", [P, 2])
        c.quarter = sb("quarter", [P, 1])
        c.waiter = sb("waiter", [P, 1])
        c.waiter_act = sb("waiter_act", [P, 8])
        c.carried = 0
        c.shapes = sb("shapes", [P, 2 * H + H + 4])
        c.select = sb("select", [P, H + 4], BF16)
        c.select16 = c.select[:, 0:H]
        c.select4 = c.select[:, H:H + 4]

        def col(name, t):
            at, n = COL_AT[name]
            return c.cols[:, at + t:at + t + 1]

        def row(name):
            return c.rows[:, ROW_AT[name]:ROW_AT[name] + ROW_LEN[name]]

        def pair(name):
            return c.rows[:, ROW_AT[name]:ROW_AT[name] + 2 * S].rearrange("p (s c) -> p s c", s=2).unsqueeze(2)\
                .to_broadcast([P, 2, 2, S])

        def head_mask(dim):
            return c.shapes[:, 0:H] if dim == 8 else c.shapes[:, H:2 * H]

        c.col, c.row, c.pair, c.head_mask = col, row, pair, head_mask
        c.w = {}
        c.lasting = lambda n: ctx.enter_context(nc.semaphore(n))
        l1_loaded = c.lasting("l1_weights_loaded")
        l23_loaded = c.lasting("l23_weights_loaded")

        with ExitStack() as early:
            for name in WEIGHTS_01:
                shape = WEIGHTS_01[name]
                c.w[name] = early.enter_context(nc.sbuf_tensor(name, list(shape), F32))
            load_constants(c, l1_loaded)
            with nc.sbuf_tensor("pos", [P, 4, P], F32) as pos:
                c.pos = pos
                load_positions(c)
                narrow_attention(c, LAYER0)
            mlp(c, "l0_mlp", c.w["l0_w1"], "l0_b1", c.w["l0_w2"], ACT.Gelu, P, 2 * P, "channels")
            narrow_attention(c, LAYER1)
            mlp(c, "l1_mlp", c.w["l1_w1"], "l1_b1", c.w["l1_w2"], ACT.Gelu_apprx_tanh, D, FF, "l1_b2")
        with ExitStack() as late:
            for name in WEIGHTS_23:
                c.w[name] = late.enter_context(nc.sbuf_tensor(name, list(WEIGHTS_23[name]), F32))
            with ExitStack() as two:
                c.ctx_T_flat = two.enter_context(nc.sbuf_tensor("ctx_T_all", [P, 2 * B * S], F32))
                c.ctx_T = c.ctx_T_flat[:, :].rearrange("p (t b s) -> p t b s", t=2, b=B)
                c.value_bias = two.enter_context(nc.sbuf_tensor("value_bias", [P, H * P], F32))
                c.extra = two.enter_context(nc.sbuf_tensor("extra", [P, H, B], F32))
                load_late(c, l23_loaded)
                for a in (1, 2):
                    norm_transposed(c, f"l2_norm{a}", f"l2_ln{a}_g", f"l2_ln{a}_b", add=(a == 2))
                    extra_scores(c, a)
                    wide_heads(c, a)
                norm_transposed(c, "l2_norm3", "l2_lnm_g", "l2_lnm_b", add=True)
            mlp(c, "l2_mlp", c.w["l2_w1"], "l2_b1", c.w["l2_w2"], ACT.Gelu, D, FF, "l2_b2")
            narrow_attention(c, LAYER3_SELF)
            narrow_attention(c, LAYER3_CROSS)
            norm_transposed(c, "l3_norm3", "l3_ln3_g", "l3_ln3_b")
            mlp(c, "l3_mlp", c.w["l3_w1"], "l3_b1", c.w["l3_w2"], ACT.Gelu_apprx_tanh, D, FF, "l3_b2")


def load_positions(c):
    loaded = c.lasting("positions_loaded")
    with c.nc.Block() as block:
        @block.sync
        def _(sync):
            sync.dma_start(c.pos[:, :, :], c.dram["pos"]).then_inc(loaded, 16)
            sync.wait_ge(loaded, 16)


def load_late(c, loaded):
    with c.nc.Block() as block:
        @block.sync
        def _(sync):
            for t in range(2):
                sync.dma_start(c.ctx_T[:, t, :, :], c.dram["ctx_T"][:, t * P:(t + 1) * P, :].rearrange("b p s -> p b s"))\
                    .then_inc(loaded, 16)
            for name in WEIGHTS_23:
                sync.dma_start(c.w[name][:, :, :], c.dram[name]).then_inc(loaded, 16)
            sync.wait_ge(loaded, 16 * (2 + len(WEIGHTS_23)))


WEIGHTS_01 = {
    "l0_wq": (P, 1, P), "l0_wk": (P, 1, P), "l0_wv": (P, 1, P), "l0_wo": (P, 1, P),
    "l0_w1": (P, 1, 2 * P), "l0_w2": (P, 2, P),
    "l1_wq": (P, 2, D), "l1_wk": (P, 2, D), "l1_wv": (P, 2, D), "l1_wo": (P, 2, D),
    "l1_w1": (P, 2, FF), "l1_w2": (P, 8, D),
}
WEIGHTS_23 = {
    "l2_w1": (P, 2, FF), "l2_w2": (P, 8, D),
    "l3_wq": (P, 2, D), "l3_wk": (P, 2, D), "l3_wv": (P, 2, D), "l3_wao": (P, 2, D),
    "l3_wqc": (P, 2, D), "l3_wkc": (P, 2, D), "l3_wvc": (P, 2, D), "l3_wco": (P, 2, D),
    "l3_w1": (P, 2, FF), "l3_w2": (P, 8, D),
}


def positions():
    pos = np.arange(2 * P, dtype=np.float32)[:, None]
    div = np.exp(np.arange(0, P, 2, dtype=np.float32) * np.float32(-np.log(10000.0) / P)).astype(np.float32)
    ang = (pos * div).astype(np.float32)
    pe = np.zeros((2 * P, P), np.float32)
    pe[:, 0::2], pe[:, 1::2] = np.sin(ang), np.cos(ang)
    return pe


def laid_out(i):
    g = {k: np.asarray(v) for k, v in i.items()}
    a = {}
    a["x_T"] = g["x"].transpose(0, 2, 1)
    a["ctx_T"] = g["ctx_2048"].transpose(0, 2, 1)
    a["mask"] = g["mask_BxS2_ik0"]
    a["mask_T"] = g["mask_BxS2_ik0"].T
    m = g["mask_1x1xSxS2_fc1"][0, 0]
    a["self_mask"] = np.stack([m, m.T])
    m = g["mask_Bx1xSxS2_ff1"][:, 0]
    a["cross_mask"] = np.stack([m, m.transpose(0, 2, 1)], 1)

    def tiles(w):
        return w.reshape(-1, P, w.shape[1]).transpose(1, 0, 2)

    kv_w = g["L1_xattn_kv_w"].reshape(D, D, 2)
    kv_b = g["L1_xattn_kv_b"].reshape(D, 2)
    qkv, kvc = g["L3_xattn_w_qkv"], g["L3_xattn_w_kv"]
    b_qkv, b_kvc = g["L3_xattn_b_qkv"], g["L3_xattn_b_kv"]
    w = {
        "l0_wq": g["L0_xattn_Wq"], "l0_wk": g["L0_xattn_Wk"], "l0_wv": g["L0_xattn_Wv"], "l0_wo": g["L0_xattn_Wo"],
        "l0_w1": g["L0_xattn_W1"], "l0_w2": g["L0_xattn_W2"],
        "l1_wq": g["L1_xattn_q_w"], "l1_wk": kv_w[:, :, 0], "l1_wv": kv_w[:, :, 1], "l1_wo": g["L1_xattn_out_w"],
        "l1_w1": g["L1_xattn_mlp_w1"], "l1_w2": g["L1_xattn_mlp_w2"],
        "l2_w1": g["L2_xattn_w_fc1"], "l2_w2": g["L2_xattn_w_fc2"],
        "l3_wq": qkv[:, 0:D], "l3_wk": qkv[:, D:2 * D], "l3_wv": qkv[:, 2 * D:], "l3_wao": g["L3_xattn_w_ao"],
        "l3_wqc": g["L3_xattn_w_q"], "l3_wkc": kvc[:, 0:D], "l3_wvc": kvc[:, D:], "l3_wco": g["L3_xattn_w_co"],
        "l3_w1": g["L3_xattn_w1"], "l3_w2": g["L3_xattn_w2"],
    }
    for name, x in w.items():
        a[name] = tiles(x)
    vec = {
        "l0_ffn_g": g["L0_xattn_ffn_ln_g"], "l0_ffn_b": g["L0_xattn_ffn_ln_b"], "l0_b1": g["L0_xattn_b1"],
        "l0_b2": g["L0_xattn_b2"],
        "l1_q_b": g["L1_xattn_q_b"], "l1_k_b": kv_b[:, 0], "l1_v_b": kv_b[:, 1], "l1_post": g["L1_xattn_postnorm_w"],
        "l1_b1": g["L1_xattn_mlp_b1"],
        "l2_lnm_g": g["L2_xattn_ln_mlp_scale"], "l2_lnm_b": g["L2_xattn_ln_mlp_offset"], "l2_b1": g["L2_xattn_b_fc1"],
        "l3_ln1_g": g["L3_xattn_ln1_s"], "l3_ln1_b": g["L3_xattn_ln1_b"],
        "l3_q_b1": b_qkv[0:D], "l3_k_b1": b_qkv[D:2 * D], "l3_v_b1": b_qkv[2 * D:],
        "l3_ln2_g": g["L3_xattn_ln2_s"], "l3_ln2_b": g["L3_xattn_ln2_b"],
        "l3_q_b2": g["L3_xattn_b_q"], "l3_k_b2": b_kvc[0:D], "l3_v_b2": b_kvc[D:],
        "l3_ln3_g": g["L3_xattn_ln3_s"], "l3_ln3_b": g["L3_xattn_ln3_b"], "l3_b1": g["L3_xattn_b1"],
    }
    for n in (1, 2):
        vec[f"l2_ln{n}_g"] = g[f"L2_xattn_ln{n}_scale"]
        vec[f"l2_ln{n}_b"] = g[f"L2_xattn_ln{n}_offset"]
        for v in ("bq", "bk", "bias_k", "bias_v", "bo"):
            vec[f"l2_{v}{n}"] = g[f"L2_xattn_{v}{n}"].reshape(-1)
        a[f"l2_wq{n}"] = g[f"L2_xattn_wq{n}"]
        a[f"l2_rows{n}"] = np.stack([g[f"L2_xattn_{v}{n}"].reshape(-1) for v in ("bq", "bias_k", "bv", "bias_v")])
        by_head = [g[f"L2_xattn_w{v}{n}"].reshape(2, P, H, P).transpose(2, 1, 0, 3).reshape(H, P, D) for v in "qkv"]
        a[f"l2_heads{n}"] = np.stack(by_head + [g[f"L2_xattn_wo{n}"].reshape(H, P, D)], 1)
    a["cols"] = np.concatenate([vec[name].reshape(n, P) for name, n in COLUMNS]).T
    rows = {
        "l0_q_g": g["L0_xattn_ln_q_g"], "l0_kv_g": g["L0_xattn_ln_kv_g"],
        "l0_q_b": g["L0_xattn_ln_q_b"], "l0_kv_b": g["L0_xattn_ln_kv_b"],
        "l1_out_b": g["L1_xattn_out_b"], "l1_b2": g["L1_xattn_mlp_b2"], "l2_b2": g["L2_xattn_b_fc2"],
        "l3_ao_b": g["L3_xattn_b_ao"], "l3_co_b": g["L3_xattn_b_co"], "l3_b2": g["L3_xattn_b2"],
    }
    a["rows"] = np.concatenate([rows[name] for name in ROWS])
    pe = positions().reshape(2, P, P).transpose(1, 0, 2)
    a["pos"] = np.concatenate([pe, pe], 1)
    p, h = np.arange(P)[:, None], np.arange(H)[None, :]
    n4 = np.arange(4)[None, :]
    a["shapes"] = np.concatenate([p // 8 == h, p // 16 == h % 8, (p < 32) & (p % 16 == h), (p < 8) & (p % 4 == n4)],
                                 1).astype(np.float32)
    return {k: np.ascontiguousarray(v) for k, v in a.items()}


def kernel(**inputs):
    import concourse.bacc as bacc
    from concourse.bass_utils import run_bass_kernel_spmd

    nc = bacc.Bacc("TRN2", target_bir_lowering=False, num_devices=1)
    arrays = laid_out(inputs)
    dram = {k: nc.dram_tensor(f"in_{k}", v.shape, mybir.dt.from_np(v.dtype), kind="ExternalInput").ap()
            for k, v in arrays.items()}
    out = nc.dram_tensor("out", (B, S, D), F32, kind="ExternalOutput").ap()
    build(nc, dram, out)
    result = run_bass_kernel_spmd(nc, [{f"in_{k}": v for k, v in arrays.items()}], core_ids=[0])
    return result.results[0]["out"]
```

```python
from contextlib import ExitStack

import numpy as np

import concourse.bass as bass
from concourse import mybir

F32 = mybir.dt.float32
BF16 = mybir.dt.bfloat16
I32 = mybir.dt.int32
ALU = mybir.AluOpType
ACT = mybir.ActivationFunctionType
AX = mybir.AxisListType.X

P = 128
B = 16
D = 256
S = 128
H = 16
BANK = 512
SLOT = 32
FF = 1024
NEG = -1.0e30

COLUMNS = [
    ("l0_ffn_g", 1), ("l0_ffn_b", 1), ("l0_b1", 2), ("l0_b2", 1),
    ("l1_q_b", 2), ("l1_k_b", 2), ("l1_v_b", 2), ("l1_post", 2), ("l1_b1", 8),
    ("l2_ln1_g", 2), ("l2_ln1_b", 2), ("l2_bq1", 16), ("l2_bk1", 16), ("l2_bias_k1", 16), ("l2_bias_v1", 16),
    ("l2_bo1", 2),
    ("l2_ln2_g", 2), ("l2_ln2_b", 2), ("l2_bq2", 16), ("l2_bk2", 16), ("l2_bias_k2", 16), ("l2_bias_v2", 16),
    ("l2_bo2", 2),
    ("l2_lnm_g", 2), ("l2_lnm_b", 2), ("l2_b1", 8),
    ("l3_ln1_g", 2), ("l3_ln1_b", 2), ("l3_q_b1", 2), ("l3_k_b1", 2), ("l3_v_b1", 2),
    ("l3_ln2_g", 2), ("l3_ln2_b", 2), ("l3_q_b2", 2), ("l3_k_b2", 2), ("l3_v_b2", 2),
    ("l3_ln3_g", 2), ("l3_ln3_b", 2), ("l3_b1", 8),
]
COL_AT = {}
for _name, _n in COLUMNS:
    COL_AT[_name] = (sum(n for _, n in COLUMNS[:len(COL_AT)]), _n)
N_COLS = sum(n for _, n in COLUMNS)
ROWS = ["l0_q_g", "l0_kv_g", "l0_q_b", "l0_kv_b", "l1_out_b", "l1_b2", "l2_b2", "l3_ao_b", "l3_co_b", "l3_b2"]
ROW_LEN = {n: (S if n.startswith("l0") else D) for n in ROWS}
ROW_AT = {n: sum(ROW_LEN[m] for m in ROWS[:i]) for i, n in enumerate(ROWS)}
N_ROWS = sum(ROW_LEN.values())


class Bank:

    def __init__(self, ap, full, free, jobs):
        self.ap, self.full, self.free, self.jobs = ap, full, free, jobs

    def nth(self, step, job):
        return step * self.jobs + job + 1


class Step:

    def __init__(self, i, k, per):
        self.i, self.k, self.per = i, k, per
        self.n = i * per + k

    def times(self, count, more):
        return self.n * count + more


def pipelined(eng, steps, per, both):
    both(Step(0, 0, per), None)
    rounds = steps // per
    if rounds > 1:
        with eng.Fori(0, rounds - 1) as i:
            for k in range(per):
                both(Step(i, k + 1, per), Step(i, k, per))
    for k in range(per):
        both(Step(rounds - 1, k + 1, per) if k < per - 1 else None, Step(rounds - 1, k, per))


def pipelined3(eng, steps, per, period):
    period(Step(0, 0, per), None, None)
    period(Step(0, 1, per), Step(0, 0, per), None)
    rounds, left = (steps - 2) // per, (steps - 2) % per
    with eng.Fori(0, rounds) as i:
        for k in range(per):
            period(Step(i, k + 2, per), Step(i, k + 1, per), Step(i, k, per))
    for k in range(left):
        period(Step(rounds, k + 2, per), Step(rounds, k + 1, per), Step(rounds, k, per))
    period(None, Step(rounds, left + 1, per), Step(rounds, left, per))
    period(None, None, Step(rounds, left + 1, per))


class Chip:
    pass


def clear_semaphores(nc, sems):
    for s in sems:
        nc.gpsimd.sem_clear(s)
    nc.all_engine_barrier()


def load_constants(c, l1_loaded, l2_loaded):
    nc = c.nc
    loaded, made, shapes_loaded = (c.lasting(n) for n in ("constants_loaded", "constants_made", "shapes_loaded"))
    with nc.Block() as block:

        @block.sync
        def _(sync):
            sync.dma_start(c.shapes[:, :], c.dram["shapes"]).then_inc(shapes_loaded, 16)
            sync.dma_start(c.cols[:, :], c.dram["cols"]).then_inc(loaded, 16)
            sync.dma_start(c.rows[:, :], c.dram["rows"].rearrange("(a n) -> a n", a=1).to_broadcast([P, N_ROWS]))\
                .then_inc(loaded, 16)
            mine = [n for n in WEIGHTS_01 if n.startswith("l0")]
            for name in mine:
                sync.dma_start(c.w[name][:, :, :], c.dram[name]).then_inc(loaded, 16)
            sync.dma_start(c.pos[:, :, :], c.dram["pos"]).then_inc(loaded, 16)
            for name in WEIGHTS_01:
                if name not in mine:
                    sync.dma_start(c.w[name][:, :, :], c.dram[name]).then_inc(l1_loaded, 16)
            for name in WEIGHTS_2:
                sync.dma_start(c.w[name][:, :, :], c.dram[name]).then_inc(l2_loaded, 16)
            for t in range(2):
                sync.dma_start(c.ctx_T[:, t, :, :], c.dram["ctx_T"][:, t * P:(t + 1) * P, :].rearrange("b p s -> p b s"))\
                    .then_inc(l2_loaded, 16)
            sync.wait_ge(loaded, 16 * (3 + len(mine)))

        @block.gpsimd
        def _(pool):
            pool.memset(c.ident[:, :], 0.0).then_inc(made, 1)
            pool.memset(c.ident_bf[:, :], 0.0).then_inc(made, 1)
            pool.memset(c.ones_bf[:, :], 1.0).then_inc(made, 1)
            pool.memset(c.minus_half[:, :], -0.5).then_inc(made, 1)
            pool.memset(c.epsilons[:, 0:1], 1e-5).then_inc(made, 1)
            pool.memset(c.epsilons[:, 1:2], 1e-6).then_inc(made, 1)
            pool.memset(c.quarter[:, :], 0.25).then_inc(made, 1)
            pool.memset(c.one[:, :], 1.0).then_inc(made, 1)
            pool.wait_ge(made, 8)
            for m in (c.ident, c.ident_bf):
                pool.affine_select(out=m[:, :], in_=m[:, :], compare_op=ALU.not_equal, fill=1.0, base=0,
                                   pattern=[[-1, P]], channel_multiplier=1).then_inc(made, 1)
            pool.wait_ge(shapes_loaded, 16)
            pool.tensor_copy(c.select[:, :], c.shapes[:, 2 * H:]).then_inc(made, 1)
            pool.wait_ge(made, 11)


def inverse_root(pool, c, chain, at, value, out, eps, n):
    small = c.epsilons[:, 0 if eps == 1e-5 else 1:1 if eps == 1e-5 else 2].unsqueeze(1).to_broadcast([P, n, 1])
    pool.tensor_tensor(out=out, in0=value, in1=small, op=ALU.add).then_inc(chain, 1)
    pool.wait_ge(chain, at + 1)
    return pool.tensor_tensor(out=out, in0=out, in1=c.minus_half[:, 0:n].unsqueeze(2), op=ALU.pow)


def upper_half(ap):
    return ap.bitcast(BF16)[:, 1::2]


def carry_wait(act, c):
    c.carried = (c.carried + 1) % 8
    act.activation(c.waiter_act[:, c.carried:c.carried + 1], c.minus_half[:, 0:1], ACT.Copy)


def norm_transposed(c, name, gamma, beta, add=None, ahead_of=None):
    nc = c.nc
    with ExitStack() as ctx:
        def sb(n, shape, dt=F32):
            return ctx.enter_context(nc.sbuf_tensor(f"{name}_{n}", shape, dt))

        sems = []

        def sem(n):
            sems.append(ctx.enter_context(nc.semaphore(f"{name}_{n}")))
            return sems[-1]

        staged = sb("staged", [P, 2, 2, S])
        stats = sb("stats", [P, 2, 6])
        mean_var = sb("mean_var", [P, 2, 2])
        rstd = sb("rstd", [P, 2, 1])
        xn = sb("xn", [P, 2, D])
        psum = [ctx.enter_context(nc.psum_tensor(f"{name}_psum{i}", [P, BANK], F32)) for i in range(4)]
        added = [Bank(psum[i], sem(f"added_full{i}"), sem(f"added_free{i}"), 1) for i in range(2)]
        turned = [Bank(psum[2 + i], sem(f"turned_full{i}"), sem(f"turned_free{i}"), 1) for i in range(2)]
        acc_staged = sem("acc_staged")
        stats_done = sem("stats_done")
        var_done = sem("var_done")
        rstd_done = sem("rstd_done")
        pool_chain = sem("pool_chain")
        xn_done = sem("xn_done")
        rows_loaded = sem("rows_loaded")
        if ahead_of:
            wq_T = sb("wq_T", [P, H, D])
            U = sb("U", [P, 2, H])
            products = sb("products", [P, H])
            offset = sb("offset", [P, H])
            ones = sb("ones", [P, P])
            u_psum = ctx.enter_context(nc.psum_tensor(f"{name}_u_psum", [P, BANK], F32))
            extra_psum = ctx.enter_context(nc.psum_tensor(f"{name}_extra_psum", [P, BANK], F32))
            wq_loaded, u_full, u_ready, extra_full, extra_done = (
                sem(n) for n in ("wq_loaded", "u_full", "u_ready", "extra_full", "extra_done"))
        cleared = sem("cleared")
        ctx.callback(clear_semaphores, nc, sems)
        block = ctx.enter_context(nc.Block())

        def turn(s):
            return s.i + s.k // 2 + 1

        @block.sync
        def _(sync):
            for bank in added + turned:
                sync.sem_inc(bank.free, 1)
            if ahead_of:
                sync.dma_start(c.value_rows[:, :, :], c.dram[f"l2_rows{ahead_of}"].rearrange("(a v) n -> a v n", a=1)
                               .to_broadcast([P, 2, H * P])).then_inc(rows_loaded, 16)
                sync.dma_start(wq_T[:, :, :], c.dram[f"l2_wq_T{ahead_of}"]).then_inc(wq_loaded, 16)

        @block.gpsimd
        def _(pool):
            def period(_, mid, __):
                if mid is None:
                    return
                p = mid.k % 2
                pool.wait_ge(var_done, mid.n + 1)
                inverse_root(pool, c, pool_chain, mid.n, mean_var[:, p:p + 1, 1:2], rstd[:, p:p + 1, :], 1e-5, 1)\
                    .then_inc(rstd_done, 1)

            pipelined3(pool, B, 2, period)
            if ahead_of:
                pool.memset(ones[:, :], 1.0).then_inc(cleared, 1)
                at = {v: COL_AT[f"l2_{v}{ahead_of}"][0] for v in ("bq", "bias_k")}
                pool.tensor_tensor(out=products[:, :], in0=c.cols[:, at["bq"]:at["bq"] + H],
                                   in1=c.cols[:, at["bias_k"]:at["bias_k"] + H], op=ALU.mult).then_inc(cleared, 1)
                if add:
                    pool.wait_ge(acc_staged, B)
                pool.memset(c.acc_flat[:, :], 0.0).then_inc(cleared, 1)
                pool.wait_ge(rows_loaded, 16)
                pool.tensor_tensor(out=c.value_bias[:, :], in0=c.value_rows[:, 0, :], in1=c.value_rows[:, 1, :],
                                   op=ALU.subtract).then_inc(cleared, 1)

        @block.tensor
        def _(pe):
            def turn_normed(bk):
                p = bk.k % 2
                pe.wait_ge(xn_done, bk.n + 1)
                pe.wait_ge(turned[p].free, turn(bk))
                for t in range(2):
                    last = pe.transpose(turned[p].ap[:, t * S:(t + 1) * S], xn[:, p, t * P:(t + 1) * P],
                                        c.ident[:, :])
                last.then_inc(turned[p].full, 1)

            def period(fr, _, bk):
                if add and fr is not None:
                    p = fr.k % 2
                    pe.wait_ge(acc_staged, fr.n + 1)
                    pe.wait_ge(added[p].free, turn(fr))
                    for t in range(2):
                        last = pe.transpose(added[p].ap[:, t * S:(t + 1) * S], staged[:, p, t, :], c.ident[:, :])
                    last.then_inc(added[p].full, 1)
                if bk is not None:
                    turn_normed(bk)
            pipelined3(pe, B, 2, period)
            if ahead_of:
                pe.wait_ge(wq_loaded, 16)
                bias_k = c.cols[:, COL_AT[f"l2_bias_k{ahead_of}"][0]:][:, 0:H]
                for h in range(H):
                    for t in range(2):
                        last = pe.matmul(u_psum[:, t * H + h:t * H + h + 1], wq_T[:, h, t * P:(t + 1) * P],
                                         bias_k[:, h:h + 1], start=True, stop=True)
                last.then_inc(u_full, 1)
                pe.wait_ge(u_ready, 1)
                pe.wait_ge(cleared, 2)
                for bank in turned:
                    pe.wait_ge(bank.free, B // 2 + 1)
                pe.matmul(u_psum[:, 2 * H:3 * H], ones[:, :], products[:, :], start=True, stop=True)
                for b in range(B):
                    for t in range(2):
                        last = pe.matmul(extra_psum[:, b * H:(b + 1) * H], c.nT[:, t, b, :], U[:, t, :],
                                         start=(t == 0), stop=(t == 1))
                last.then_inc(extra_full, 1)

        @block.vector
        def _(dve):
            def period(_, fr, bk):
                if fr is not None:
                    p = fr.k % 2
                    x = c.x[:, fr.n, :]
                    if add:
                        dve.wait_ge(added[p].full, turn(fr))
                        dve.tensor_tensor(out=x, in0=x, in1=added[p].ap[:, 0:D], op=ALU.add).then_inc(added[p].free, 1)
                        dve.wait_ge(added[p].free, turn(fr) + 1)
                        dve.memset(c.waiter[:, :], 0.0)
                    dve.bn_stats(stats[:, p, :], x).then_inc(stats_done, 1)
                    dve.wait_ge(stats_done, fr.n + 1)
                    dve.memset(c.waiter[:, :], 0.0)
                    dve.bn_aggr(mean_var[:, p, :], stats[:, p, :]).then_inc(var_done, 1)
                if bk is not None:
                    p = bk.k % 2
                    dve.wait_ge(rstd_done, bk.n + 1)
                    dve.wait_ge(turned[p].free, turn(bk))
                    dve.tensor_scalar(out=xn[:, p, :], in0=c.x[:, bk.n, :], scalar1=mean_var[:, p, 0:1],
                                      scalar2=rstd[:, p, :], op0=ALU.subtract, op1=ALU.mult).then_inc(xn_done, 1)

            pipelined3(dve, B, 2, period)
            if ahead_of:
                dve.wait_ge(u_full, 1)
                dve.tensor_copy(U[:, :, :], u_psum[:, 0:2 * H].rearrange("p (t h) -> p t h", t=2)).then_inc(u_ready, 1)
                dve.wait_ge(extra_full, 1)
                dve.tensor_copy(offset[:, :], u_psum[:, 2 * H:3 * H]).then_inc(extra_done, 1)
                dve.wait_ge(extra_done, 1)
                dve.tensor_tensor(out=c.extra[:, :, :], in0=extra_psum[:, 0:B * H].rearrange("p (b h) -> p h b", h=H),
                                  in1=offset[:, :].unsqueeze(2).to_broadcast([P, H, B]), op=ALU.add)\
                    .then_inc(extra_done, 1)

        @block.scalar
        def _(act):
            def period(fr, _, bk):
                if add and fr is not None:
                    p = fr.k % 2
                    act.wait_ge(added[p].free, turn(fr))
                    carry_wait(act, c)
                    for t in range(2):
                        last = act.activation(staged[:, p, t, :], c.acc[:, t, fr.n, :], ACT.Identity,
                                              bias=c.col(add, t), scale=1.0)
                    last.then_inc(acc_staged, 1)
                if bk is not None:
                    p = bk.k % 2
                    act.wait_ge(turned[p].full, turn(bk))
                    carry_wait(act, c)
                    for t in range(2):
                        last = act.activation(c.nT[:, t, bk.n, :], turned[p].ap[:, t * S:(t + 1) * S], ACT.Identity,
                                              bias=c.col(beta, t), scale=c.col(gamma, t))
                    last.then_inc(turned[p].free, 1)

            pipelined3(act, B, 2, period)


def mlp(c, name, w1, b1, w2, func, width, hidden, finish):
    nc = c.nc
    kt, ft = width // P, hidden // P
    channels = finish == "channels"
    groups = 8 if channels else 4
    store = name == "l3_mlp"
    with ExitStack() as ctx:
        def sb(n, shape, dt=F32):
            return ctx.enter_context(nc.sbuf_tensor(f"{name}_{n}", shape, dt))

        sems = []

        def sem(n):
            sems.append(ctx.enter_context(nc.semaphore(f"{name}_{n}")))
            return sems[-1]

        hT = sb("hT", [P, 2, ft, BANK])
        psum = [ctx.enter_context(nc.psum_tensor(f"{name}_psum{i}", [P, BANK], F32)) for i in range(8)]
        ups = min(ft, 4)
        up = [Bank(psum[i], sem(f"up_full{i}"), sem(f"up_free{i}"), ft // ups) for i in range(ups)]
        down = [Bank(psum[4 + i], sem(f"down_full{i}"), sem(f"down_free{i}"), 1) for i in range(4)]
        bias_added = sem("bias_added")
        stored = sem("stored")
        ctx.callback(clear_semaphores, nc, sems)
        block = ctx.enter_context(nc.Block())

        def source(t, g):
            if width == P:
                return c.nT_flat[:, bass.ds(g * BANK, BANK)]
            return c.nT[:, t, bass.ds(g * 4, 4), :]

        @block.sync
        def _(sync):
            for bank in up + down:
                sync.sem_inc(bank.free, 1)
            if store:
                with sync.Fori(0, groups) as g:
                    for bank in down:
                        sync.wait_ge(bank.free, g + 2)
                    sync.dma_start(c.out[bass.ds(g * 4, 4), :, :].rearrange("b p d -> p b d"),
                                   c.x[:, bass.ds(g * 4, 4), :]).then_inc(stored, 16)
                sync.wait_ge(stored, 16 * groups)

        @block.gpsimd
        def _(pool):
            if not channels:
                with pool.Fori(0, B) as b:
                    pool.tensor_tensor(out=c.x[:, b, :], in0=c.x[:, b, :], in1=c.row(finish), op=ALU.add)\
                        .then_inc(bias_added, 1)

        @block.tensor
        def _(pe):
            with pe.Fori(0, groups // 2) as i:
                for p in range(2):
                    g = i * 2 + p
                    for f in range(ft):
                        bank = up[f % ups]
                        pe.wait_ge(bank.free, bank.nth(g, f // ups))
                        for t in range(kt):
                            last = pe.matmul(bank.ap[:, :], w1[:, t, f * P:(f + 1) * P], source(t, g),
                                             start=(t == 0), stop=(t == kt - 1))
                        last.then_inc(bank.full, 1)
                    for bank in up:
                        pe.wait_ge(bank.free, bank.nth(g, bank.jobs - 1) + 1)
                    if channels:
                        bank = down[p]
                        pe.wait_ge(bank.free, i + 1)
                        for f in range(ft):
                            last = pe.matmul(bank.ap[:, :], w2[:, f, :], hT[:, p, f, :],
                                             start=(f == 0), stop=(f == ft - 1))
                        last.then_inc(bank.full, 1)
                    else:
                        for n in range(4):
                            bank = down[n]
                            pe.wait_ge(bank.free, g + 1)
                            for f in range(ft):
                                last = pe.matmul(bank.ap[:, 0:D], hT[:, p, f, n * P:(n + 1) * P], w2[:, f, :],
                                                 start=(f == 0), stop=(f == ft - 1))
                            last.then_inc(bank.full, 1)

        @block.scalar
        def _(act):
            with act.Fori(0, groups // 2) as i:
                for p in range(2):
                    g = i * 2 + p
                    for f in range(ft):
                        bank = up[f % ups]
                        act.wait_ge(bank.full, bank.nth(g, f // ups))
                        act.activation(hT[:, p, f, :], bank.ap[:, :], func, bias=c.col(b1, f), scale=1.0)\
                            .then_inc(bank.free, 1)

        @block.vector
        def _(dve):
            with dve.Fori(0, groups // 2) as i:
                for p in range(2):
                    g = i * 2 + p
                    if channels:
                        bank = down[p]
                        dve.wait_ge(bank.full, i + 1)
                        dve.scalar_tensor_tensor(out=c.x_flat[:, bass.ds(g * BANK, BANK)], in0=bank.ap[:, :],
                                                 scalar=c.col("l0_b2", 0), in1=c.acc_flat[:, bass.ds(g * BANK, BANK)],
                                                 op0=ALU.add, op1=ALU.add).then_inc(bank.free, 1)
                    else:
                        for n in range(4):
                            bank = down[n]
                            b = g * 4 + n
                            dve.wait_ge(bias_added, b + 1)
                            dve.wait_ge(bank.full, g + 1)
                            dve.tensor_tensor(out=c.x[:, b, :], in0=c.x[:, b, :], in1=bank.ap[:, 0:D], op=ALU.add)\
                                .then_inc(bank.free, 1)


class Narrow:

    def __init__(self, name, channel_tiles, queries, keys, head_dim, scale, lag, early_jobs, back_jobs, schedule):
        self.name = name
        self.ct = channel_tiles
        self.nq, self.nk, self.dh = queries, keys, head_dim
        self.scale = scale
        self.qt, self.kt = queries // P, keys // P
        self.heads_a_tile = H // channel_tiles
        self.hq, self.hk = BANK // queries, BANK // keys
        self.score_jobs = self.qt * H // self.hk
        self.turned_jobs = self.kt * H // self.hq
        self.lag = lag
        self.early_jobs = early_jobs
        self.back_jobs = back_jobs
        self.schedule = schedule.split()


LAYER0 = Narrow("l0", 1, 256, 256, 8, 8.0 ** -0.5, 1, 3, 6, """
    tail1 begin0 tail2 begin1 stream0 stream1 tail3 stream2 begin2 stream3 tail4 stream4 early0 stream5
    early1 early2 blocks tail5 stream6 tail6 stream7 score0 score1 stream8 stream9 score2 score3 stream10
    score4 score5 stream11 score6 score7 stream12 score8 score9 stream13 score10 score11 stream14 score12
    score13 stream15 score14 score15 parts stream16 turn end""")
LAYER1 = Narrow("l1", 2, 128, 256, 16, 1.0 / 16, 1, 5, 4, """
    early0 tail1 begin0 stream0 tail2 early1 stream1 tail3 early2 stream2 early3 blocks stream3 tail4 early4
    stream4 score0 stream5 score1 score2 stream6 score3 score4 score5 stream7 score6 score7 parts stream8
    turn end""")
SCHEDULE3 = """
    tail1 begin0 begin1 stream0 begin2 early0 tail2 stream1 early1 early2 blocks end tail3 stream2 score0
    stream3 score1 stream4 score2 score3 stream5 parts turn"""
LAYER3_SELF = Narrow("l3s", 2, 128, 128, 16, 1.0, 2, 3, 3, SCHEDULE3)
LAYER3_CROSS = Narrow("l3c", 2, 128, 128, 16, 1.0, 2, 3, 3, """
    tail1 begin0 begin1 stream0 begin2 tail2 early0 stream1 tail3 end early1 blocks early2 stream2 score0
    stream3 score1 stream4 score2 stream5 score3 parts turn""")


def narrow_attention(c, z):
    nc = c.nc
    l0, l1 = z is LAYER0, z is LAYER1
    masked = z.name.startswith("l3")
    cross = z is LAYER3_CROSS
    with ExitStack() as ctx:
        def sb(n, shape, dt=F32):
            return ctx.enter_context(nc.sbuf_tensor(f"{z.name}_{n}", shape, dt))

        sems = []

        def sem(n):
            sems.append(ctx.enter_context(nc.semaphore(f"{z.name}_{n}")))
            return sems[-1]

        QK = sb("QK", [P, 2, z.ct * (z.nq + z.nk)])
        QT = [QK[:, p, 0:z.ct * z.nq].rearrange("p (t q) -> p t q", t=z.ct) for p in range(2)]
        KT = [QK[:, p, z.ct * z.nq:].rearrange("p (t k) -> p t k", t=z.ct) for p in range(2)]
        q_blocks = sb("q_blocks", [P, 2, H, z.nq])
        V = sb("V", [P, 2, z.kt, H, SLOT])
        neg_max_T = sb("neg_max_T", [P, 2, z.nq], BF16)
        width = z.ct * P
        neg_max = sb("neg_max", [P, z.qt, H])
        neg_max_bf = sb("neg_max_bf", [P, z.qt, P], BF16)
        PT = sb("PT", [P, 3, BANK])
        ctx_den = sb("ctx_den", [P, 4, z.nq])
        rden = sb("rden", [P, z.qt, H, 1])
        ctx_q = sb("ctx_q", [P, z.qt, H, z.dh])
        ctx_T = sb("ctx_T", [P, z.ct, z.nq])
        x_T = sb("x_T", [P, 2, 4 * P])
        if l0:
            x_in = sb("x_in", [P, 2, 4, P])
        else:
            res = sb("res", [P, 2, D])
        if l1:
            x_in = sb("x_in", [P, 2, D])
            mask_col = sb("mask_col", [P, B])
            mask_step = sb("mask_step", [P, 1])
            mask_row = sb("mask_row", [P, B, z.nk], BF16)
            mask_int = sb("mask_int", [P, B], I32)
            mask_row_int = sb("mask_row_int", [1, B, S], I32)
        else:
            stats = sb("stats", [P, 4, 6])
            mean_var = sb("mean_var", [P, 4, 2])
            rstd = sb("rstd", [P, 4, 1])
            xn = sb("xn", [P, 4, P])
        if l0 or l1:
            r = sb("r", [P, z.qt, width])
            rn = sb("rn", [P, z.qt, width])
            stats_b = sb("stats_b", [P, 2, 6])
            mean_var_b = sb("mean_var_b", [P, 2, 2])
            rstd_b = sb("rstd_b", [P, 2, 1])
        if l1 or cross:
            ctx_in = sb("ctx_in", [P, 2, 2, S])
        if masked:
            mask_in = sb("mask_in", [P, 2, 2, S])
            mask_mul = sb("mask_mul", [P, 2, 2, S])
            mask_add = sb("mask_add", [P, 2, 2, S])
            mask_left = sb("mask_left", [P, S])
            mask_parts = sb("mask_parts", [P, 2, 3, S], BF16)
            s_masked = sb("s_masked", [P, 2, BANK])
            s_biased = sb("s_biased", [P, 2, BANK])
            t_masked = sb("t_masked", [P, 3, BANK])
            t_shifted = sb("t_shifted", [P, 2, BANK])

        banks = [ctx.enter_context(nc.psum_tensor(f"{z.name}_psum{i}", [P, BANK], F32)) for i in range(8)]

        def group(at, what, n, jobs):
            return [Bank(banks[at + i], sem(f"{what}{i}_full"), sem(f"{what}{i}_free"), -(-(jobs - i) // n))
                    for i in range(n)]

        front = group(0, "front", 2, z.early_jobs + z.score_jobs + 1)
        turned = group(2, "turned", 2, z.turned_jobs)
        if masked:
            shifts = group(4, "shifts", 2, z.turned_jobs)
            context = group(6, "context", 1, 1)
            back = group(7, "back", 1, z.back_jobs)
        else:
            shifts = []
            context = [Bank(banks[4 + i], sem(f"context{i}_full"), sem(f"context{i}_free"), 1)
                       for i in range(2 if l0 else 1)]
            back = group(6, "back", 2, z.back_jobs)

        loaded = sem("loaded")
        set_up = sem("set_up")
        x_loaded = [sem(f"x_loaded{p}") for p in range(2)]
        mask_loaded = [sem(f"mask_loaded{p}") for p in range(2)]
        mask_made = sem("mask_made")
        mask_copied = sem("mask_copied")
        x_ready = sem("x_ready")
        stats_done = sem("stats_done")
        var_done = sem("var_done")
        rstd_done = sem("rstd_done")
        rstd_part = sem("rstd_part")
        xn_done = sem("xn_done")
        scaled = sem("scaled")
        ln_done = sem("ln_done")
        res_ready = sem("res_ready")
        q_blocks_ready = [sem("q_blocks_ready"), sem("q_blocks_ready_pool")] if masked else [sem("q_blocks_ready")]
        s_ready = sem("s_ready")
        max_done = sem("max_done")
        probs_ready = sem("probs_ready")
        rden_done = sem("rden_done")
        stats_b_done = sem("stats_b_done")
        var_b_done = sem("var_b_done")
        rstd_b_part = sem("rstd_b_part")
        rstd_b_done = sem("rstd_b_done")
        rn_done = sem("rn_done")
        ctx.callback(clear_semaphores, nc, sems)
        block = ctx.enter_context(nc.Block())

        lag = z.lag

        def F(f):
            return front[f % 2], f // 2

        def K(m):
            return back[(m - 1) % len(back)], (m - 1) // len(back)

        def period(stages):
            def run(front_step, middle_step, back_step):
                for entry in z.schedule:
                    stage = entry.rstrip("0123456789")
                    step = {"stream": middle_step, "tail": back_step}.get(stage, front_step)
                    if stage in stages and step is not None:
                        stages[stage](step, int(entry[len(stage):] or 0))
            return run

        N_JOB = z.early_jobs + z.score_jobs
        T, Q_JOB, K_JOB, V_JOBS = 0, (2 if l1 else 1), (1 if l1 else 1), ([3, 4] if l1 else [2])
        TURN = list(range(1, 1 + z.qt))
        CTX_T = z.qt + 1
        OUT = CTX_T + 1
        TAIL = list(range(OUT + 1, z.back_jobs + 1))

        MASK_OPS = 6

        def by_head(ap):
            return ap.rearrange("p (h s) -> p h s", h=4)

        def all_heads(ap):
            return ap.unsqueeze(1).to_broadcast([P, 4, S])

        def out_evacuated(b):
            bk, k = K(OUT)
            return bk.free, bk.nth(b, k) + 1

        def q_to_blocks(eng, b, t, done):
            bk, k = F(Q_JOB)
            eng.wait_ge(bk.free, bk.nth(b.n, k) + 1)
            for half in range(2):
                n = z.heads_a_tile // 2
                heads = slice(t * z.heads_a_tile + half * n, t * z.heads_a_tile + (half + 1) * n)
                shape = [P, n, z.nq]
                eng.tensor_tensor(out=q_blocks[:, b.k % 2, heads, :],
                                  in0=QT[b.k % 2][:, t, :].unsqueeze(1).to_broadcast(shape),
                                  in1=c.head_mask(z.dh)[:, heads].unsqueeze(2).to_broadcast(shape),
                                  op=ALU.mult).then_inc(done, 1)

        @block.sync
        def _(sync):
            for bk in front + turned + shifts + context + back:
                sync.sem_inc(bk.free, 1)
            if l1:
                sync.dma_start(mask_int[:, :], c.dram["mask_T"]).then_inc(loaded, 16)
                sync.dma_start(mask_row_int[:, :, :], c.dram["mask"].rearrange("(a b) s -> a b s", a=1))\
                    .then_inc(loaded, 16)
            if masked and not cross:
                sync.dma_start(mask_in[:, 0, :, :], c.dram["self_mask"].rearrange("w p s -> p w s"))\
                    .then_inc(loaded, 16)

            def load(b, p):
                if l0:
                    sync.dma_start(x_in[:, p, 0:2, :], c.dram["x_T"][b].rearrange("(t p) s -> p t s", p=P))\
                        .then_inc(x_loaded[p], 16)
                    sync.dma_start(x_in[:, p, 2:4, :], c.dram["ctx_T"][b].rearrange("(t p) s -> p t s", p=P))\
                        .then_inc(x_loaded[p], 16)
                if l1 or cross:
                    sync.dma_start(ctx_in[:, p, :, :], c.dram["ctx_T"][b].rearrange("(t p) s -> p t s", p=P))\
                        .then_inc(x_loaded[p], 16)
                if cross:
                    sync.dma_start(mask_in[:, p, :, :], c.dram["cross_mask"][b].rearrange("w p s -> p w s"))\
                        .then_inc(mask_loaded[p], 16)

            if l0 or l1 or cross:
                for p in range(2):
                    load(p, p)
                with sync.Fori(1, B // 2) as i:
                    for p in range(2):
                        before = (i - 1) * 2 + p
                        if l0:
                            bk, k = F(T)
                            sync.wait_ge(bk.full, bk.nth(before, k))
                        else:
                            bk, k = F(V_JOBS[-1])
                            sync.wait_ge(bk.full, bk.nth(before, k))
                        if cross:
                            sync.wait_ge(mask_made, (before + 1) * MASK_OPS)
                        load(i * 2 + p, p)

        @block.gpsimd
        def _(pool):
            pool.memset(neg_max_bf[:, :, :], 0.0).then_inc(set_up, 1)
            pool.memset(V[:, :, :, :, :], 0.0).then_inc(set_up, 1)
            pool.wait_ge(set_up, 2)
            pool.memset(V[:, :, :, :, z.dh:z.dh + 1], 1.0).then_inc(set_up, 1)
            if l1:
                pool.memset(mask_row[:, :, :], 0.0).then_inc(set_up, 1)
                pool.wait_ge(set_up, 4)
                pool.wait_ge(loaded, 32)
                pool.tensor_scalar(out=mask_col[:, :], in0=mask_int[:, :], scalar1=0.0, scalar2=NEG,
                                   op0=ALU.is_equal, op1=ALU.mult).then_inc(set_up, 1)
                pool.tensor_scalar(out=mask_row[0:1, :, 0:S], in0=mask_row_int[:, :, :], scalar1=0.0, scalar2=NEG,
                                   op0=ALU.is_equal, op1=ALU.mult).then_inc(set_up, 1)
                pool.wait_ge(set_up, 6)

            def make_masks(p, before):
                pool.tensor_tensor(out=mask_mul[:, p, :, :], in0=mask_in[:, p, :, :],
                                   in1=c.quarter[:, :].unsqueeze(2).to_broadcast([P, 2, S]), op=ALU.mult)\
                    .then_inc(mask_made, 1)
                pool.tensor_scalar(out=mask_add[:, p, :, :], in0=mask_in[:, p, :, :], scalar1=10000.0,
                                   scalar2=-10000.0, op0=ALU.mult, op1=ALU.add).then_inc(mask_made, 1)
                left, one = mask_left[:, :], c.one[:, :].to_broadcast([P, S])
                pool.wait_ge(mask_made, before + 2)
                pool.tensor_tensor(out=mask_parts[:, p, 0, :], in0=mask_add[:, p, 1, :], in1=one, op=ALU.mult)\
                    .then_inc(mask_made, 1)
                pool.wait_ge(mask_made, before + 3)
                pool.tensor_tensor(out=left, in0=mask_add[:, p, 1, :], in1=mask_parts[:, p, 0, :], op=ALU.subtract)\
                    .then_inc(mask_made, 1)
                pool.wait_ge(mask_made, before + 4)
                pool.tensor_tensor(out=mask_parts[:, p, 1, :], in0=left, in1=one, op=ALU.mult).then_inc(mask_made, 1)
                pool.wait_ge(mask_made, before + 5)
                pool.tensor_tensor(out=mask_parts[:, p, 2, :], in0=left, in1=mask_parts[:, p, 1, :],
                                   op=ALU.subtract).then_inc(mask_made, 1)

            if masked and not cross:
                pool.wait_ge(loaded, 16)
                make_masks(0, 0)

            def wait_first(sem, value):
                pool.wait_ge(sem, value)
                c.carried = (c.carried + 1) % 8
                pool.tensor_tensor(out=c.waiter_pool[:, c.carried:c.carried + 1], in0=c.one[:, :], in1=c.one[:, :], op=ALU.mult)

            def begin(b, part, first):
                p = b.k % 2
                if part == 0 and l0:
                    pool.wait_ge(x_loaded[p], (b.n - p) * 16 + 32)
                    x = x_in[:, p, :, :]
                    pool.tensor_tensor(out=x, in0=x, in1=c.pos[:, :, :], op=ALU.add).then_inc(x_ready, 1)
                if part == 0 and l1:
                    if not first:
                        bk, k = F(T)
                        wait_first(bk.full, b.times(bk.jobs, k + 1 - 2 * bk.jobs))
                    pool.tensor_copy(x_in[:, p, :], c.x[:, b.n, :]).then_inc(x_ready, 1)
                if part == 1 and not l1:
                    pool.wait_ge(var_done, b.n + 1)
                    n = 4 if l0 else 1
                    inverse_root(pool, c, rstd_part, b.n, mean_var[:, 0:n, 1:2], rstd[:, 0:n, :], 1e-5, n)\
                        .then_inc(rstd_done, 1)
                if part == 2 and l0:
                    x = x_in[:, p, :, :].rearrange("p (s t) c -> p s t c", s=2)
                    n = xn[:, :, :].rearrange("p (s t) c -> p s t c", s=2)
                    pool.wait_ge(xn_done, b.n + 1)
                    pool.tensor_tensor(out=x, in0=n, in1=c.pair("l0_q_g"), op=ALU.mult).then_inc(scaled, 1)
                    pool.wait_ge(scaled, b.n + 1)
                    pool.tensor_tensor(out=x, in0=x, in1=c.pair("l0_q_b"), op=ALU.add).then_inc(ln_done, 1)

            def end(b, _, first):
                p = b.k % 2
                if l0:
                    return
                if not first:
                    bk, k = K(OUT)
                    wait_first(bk.free, b.times(bk.jobs, k + 2 - 2 * bk.jobs))
                pool.tensor_tensor(out=res[:, p, :], in0=c.x[:, b.n, :], in1=c.row(
                    "l1_out_b" if l1 else "l3_co_b" if cross else "l3_ao_b"), op=ALU.add).then_inc(res_ready, 1)
                if cross:
                    pool.wait_ge(mask_loaded[p], (b.n - p) * 8 + 16)
                    if not first:
                        bk = shifts[-1]
                        pool.wait_ge(bk.free, b.times(bk.jobs, 1 - bk.jobs))
                    make_masks(p, b.times(MASK_OPS, 0))

            def blocks(b, _):
                if masked:
                    q_to_blocks(pool, b, 1, q_blocks_ready[1])

            def score(b, j):
                if masked:
                    bk, k = F(z.early_jobs + j)
                    pool.wait_ge(bk.free, bk.nth(b.n, k) + 1)
                    p = b.k % 2 if cross else 0
                    pool.tensor_tensor(out=by_head(s_biased[:, j % 2, :]), in0=by_head(s_masked[:, j % 2, :]),
                                       in1=all_heads(mask_add[:, p, 0, :]), op=ALU.add).then_inc(s_ready, 1)

            def tail(b, m):
                if TAIL and m == OUT:
                    pool.wait_ge(var_b_done, b.n + 1)
                    n = z.qt
                    inverse_root(pool, c, rstd_b_part, b.n, mean_var_b[:, 0:n, 1:2], rstd_b[:, 0:n, :],
                                 1e-5 if l0 else 1e-6, n).then_inc(rstd_b_done, 1)

            stages = {"blocks": blocks, "score": score, "tail": tail}

            def one_period(early_step, front_step, back_step):
                stages["begin"] = lambda b, n: begin(b, n, back_step is None)
                stages["end"] = lambda b, n: end(b, n, back_step is None)
                period(stages)(early_step, front_step, back_step)

            pipelined3(pool, B, 2, one_period)

        @block.tensor
        def _(pe):
            pe.wait_ge(set_up, 6 if l1 else 3)

            def early(b, f):
                p = b.k % 2
                bk, k = F(f)
                out = bk.ap
                if f == T:
                    if l1:
                        pe.wait_ge(x_ready, b.n + 1)
                    elif l0:
                        pe.wait_ge(ln_done, b.n + 1)
                    else:
                        pe.wait_ge(xn_done, b.n + 1)
                    pe.wait_ge(bk.free, bk.nth(b.n, k))
                    for t in range(4 if l0 else 2):
                        src = x_in[:, p, t, :] if l0 else x_in[:, p, t * P:(t + 1) * P] if l1 else xn[:, t, :]
                        last = pe.transpose(out[:, t * P:(t + 1) * P], src, c.ident[:, :])
                    last.then_inc(bk.full, 1)
                    return
                tk, t0 = F(T)
                pe.wait_ge(tk.free, tk.nth(b.n, t0) + 1)
                if l1 or cross:
                    pe.wait_ge(x_loaded[p], (b.n - p) * 8 + 16)
                pe.wait_ge(bk.free, bk.nth(b.n, k))
                tokens = x_T[:, p, :]
                own = tokens[:, 0:2 * P].rearrange("p (t s) -> p t s", t=2)
                w = c.w
                if l0:
                    if f == K_JOB:
                        pe.matmul(out[:, 0:256], w["l0_wq"][:, 0, :], tokens[:, 0:256], start=True, stop=True)
                        last = pe.matmul(out[:, 256:512], w["l0_wk"][:, 0, :], tokens[:, 256:512], start=True, stop=True)
                    else:
                        for t in range(2):
                            last = pe.matmul(out[:, t * P:(t + 1) * P], tokens[:, (2 + t) * P:(3 + t) * P],
                                             w["l0_wv"][:, 0, :], start=True, stop=True)
                elif l1:
                    other = ctx_in[:, p, :, :]
                    if f == K_JOB:
                        for m in range(2):
                            for half, src in enumerate((other, own)):
                                for t in range(2):
                                    last = pe.matmul(out[:, m * 256 + half * P:m * 256 + (half + 1) * P],
                                                     w["l1_wk"][:, t, m * P:(m + 1) * P], src[:, t, :],
                                                     start=(t == 0), stop=(t == 1))
                    elif f == Q_JOB:
                        for m in range(2):
                            for t in range(2):
                                last = pe.matmul(out[:, m * P:(m + 1) * P], w["l1_wq"][:, t, m * P:(m + 1) * P],
                                                 own[:, t, :], start=(t == 0), stop=(t == 1))
                    else:
                        src = (other, own)[f - V_JOBS[0]]
                        for t in range(2):
                            last = pe.matmul(out[:, 0:D], src[:, t, :], w["l1_wv"][:, t, :],
                                             start=(t == 0), stop=(t == 1))
                else:
                    other = ctx_in[:, p, :, :] if cross else own
                    wq, wk, wv = (w["l3_wqc"], w["l3_wkc"], w["l3_wvc"]) if cross else (w["l3_wq"], w["l3_wk"], w["l3_wv"])
                    if f == K_JOB:
                        for j, (wt, src) in enumerate(((wq, own), (wk, other))):
                            for m in range(2):
                                for t in range(2):
                                    last = pe.matmul(out[:, (2 * j + m) * P:(2 * j + m + 1) * P],
                                                     wt[:, t, m * P:(m + 1) * P], src[:, t, :],
                                                     start=(t == 0), stop=(t == 1))
                    else:
                        for t in range(2):
                            last = pe.matmul(out[:, 0:D], other[:, t, :], wv[:, t, :], start=(t == 0), stop=(t == 1))
                last.then_inc(bk.full, 1)

            def score(b, j):
                per_tile = H // z.hk
                q, h = j // per_tile, j % per_tile * z.hk
                p = b.k % 2
                if j == 0:
                    kb, kk = F(K_JOB)
                    pe.wait_ge(kb.free, kb.nth(b.n, kk) + 1)
                part = H // (2 * z.ct)
                if q == 0 and h % part == 0:
                    t, half = h // z.heads_a_tile, h % z.heads_a_tile // part
                    if masked:
                        pe.wait_ge(q_blocks_ready[t], b.times(2, 1 + half))
                    else:
                        pe.wait_ge(q_blocks_ready[0], b.times(2 * z.ct, 1 + 2 * t + half))
                bk, k = F(z.early_jobs + j)
                pe.wait_ge(bk.free, bk.nth(b.n, k))
                t = h // z.heads_a_tile
                for i in range(z.hk):
                    last = pe.matmul(bk.ap[:, i * z.nk:(i + 1) * z.nk],
                                     upper_half(q_blocks[:, p, h + i, q * P:(q + 1) * P]), upper_half(KT[p][:, t, :]),
                                     start=True, stop=True)
                if l1:
                    last = pe.matmul(bk.ap[:, :], c.ones_bf[:, :],
                                     mask_row[:, b.n, :].unsqueeze(1).to_broadcast([P, z.hk, z.nk]),
                                     start=False, stop=True, skip_group_check=True)
                last.then_inc(bk.full, 1)

            def turn(b, _):
                bk, k = F(N_JOB)
                pe.wait_ge(max_done, b.times(3, 3))
                pe.wait_ge(bk.free, bk.nth(b.n, k))
                for q in range(z.qt):
                    last = pe.transpose(bk.ap[:, :].bitcast(BF16)[:, q * P:(q + 1) * P], neg_max_bf[:, q, :],
                                        c.ident_bf[:, :])
                last.then_inc(bk.full, 1)

            def stream(b, n):
                p = b.k % 2
                if n == 0:
                    bk, k = F(N_JOB)
                    pe.wait_ge(bk.free, bk.nth(b.n, k) + 1)
                    for job in V_JOBS:
                        bk, k = F(job)
                        pe.wait_ge(bk.free, bk.nth(b.n, k) + 1)
                    if masked:
                        pe.wait_ge(mask_made, b.times(MASK_OPS, MASK_OPS) if cross else MASK_OPS)
                if n < z.turned_jobs:
                    chunk, kt = n // z.kt, n % z.kt
                    h = chunk * z.hq
                    t = h // z.heads_a_tile
                    bk, k = turned[n % 2], n // 2
                    pe.wait_ge(bk.free, bk.nth(b.n, k))
                    last = pe.matmul(bk.ap[:, :], KT[p][:, t, kt * P:(kt + 1) * P], q_blocks[:, p, h:h + z.hq, :],
                                     start=True, stop=True)
                    if masked:
                        last.then_inc(bk.full, 1)
                        bk = shifts[n % 2]
                        pe.wait_ge(bk.free, bk.nth(b.n, k))
                        for part in range(3):
                            pe.matmul(bk.ap[:, :], c.ident_bf[:, :],
                                      all_heads(mask_parts[:, p if cross else 0, part, :]),
                                      start=(part == 0), stop=True, skip_group_check=(part > 0))
                    for i in range(z.hq):
                        last = pe.matmul(bk.ap[:, i * z.nq:(i + 1) * z.nq],
                                         c.select16[:, h + i:h + i + 1].to_broadcast([P, P]), neg_max_T[:, p, :],
                                         start=False, stop=True, skip_group_check=True)
                    last.then_inc(bk.full, 1)
                if n >= lag:
                    m = n - lag
                    chunk, kt = m // z.kt, m % z.kt
                    pe.wait_ge(probs_ready, b.times(z.turned_jobs, m + 1))
                    for i in range(z.hq):
                        h = chunk * z.hq + i
                        g, j = h // 4, h % 4
                        cb, at = g * z.nq // BANK, g * z.nq % BANK
                        if kt == 0 and j == 0 and at == 0:
                            pe.wait_ge(context[cb].free, b.n + 1)
                        last = pe.matmul(context[cb].ap[j * SLOT:(j + 1) * SLOT, at:at + z.nq], V[:, p, kt, h, :],
                                         PT[:, m % 3, i * z.nq:(i + 1) * z.nq],
                                         start=(kt == 0), stop=(kt == z.kt - 1))
                    if kt == z.kt - 1 and (h + 1) * z.nq % (4 * BANK) == 0:
                        last.then_inc(context[cb].full, 1)

            def tail(b, m):
                bk, k = K(m)
                out = bk.ap
                if m in TURN:
                    if m == TURN[0]:
                        for cb in context:
                            pe.wait_ge(cb.free, b.n + 2)
                    pe.wait_ge(bk.free, bk.nth(b.n, k))
                    q = m - TURN[0]
                    for g in range(4):
                        last = pe.transpose(out[:, g * P:(g + 1) * P], ctx_den[:, g, q * P:(q + 1) * P], c.ident[:, :])
                elif m == CTX_T:
                    for j in TURN:
                        tb, tk = K(j)
                        pe.wait_ge(tb.free, tb.nth(b.n, tk) + 1)
                    pe.wait_ge(bk.free, bk.nth(b.n, k))
                    flat = ctx_q[:, :, :, :].rearrange("p q h d -> p q (h d)")
                    for i in range(2):
                        src = flat[:, i, :] if l0 else flat[:, 0, i * P:(i + 1) * P]
                        last = pe.transpose(out[:, i * P:(i + 1) * P], src, c.ident[:, :])
                elif m == OUT:
                    tb, tk = K(CTX_T)
                    pe.wait_ge(tb.free, tb.nth(b.n, tk) + 1)
                    pe.wait_ge(bk.free, bk.nth(b.n, k))
                    wo = c.w["l0_wo" if l0 else "l1_wo" if l1 else "l3_wco" if cross else "l3_wao"]
                    for q in range(z.qt):
                        for t in range(z.ct):
                            last = pe.matmul(out[:, q * width:(q + 1) * width], ctx_T[:, t, q * P:(q + 1) * P],
                                             wo[:, t, :], start=(t == 0), stop=(t == z.ct - 1 and not l0))
                        if l0:
                            last = pe.matmul(out[:, q * P:(q + 1) * P], x_T[:, b.k % 2, q * P:(q + 1) * P],
                                             c.ident[:, :], start=False, stop=True)
                else:
                    src = r
                    if m == TAIL[-1]:
                        pe.wait_ge(rn_done, b.n + 1)
                        src = rn
                    else:
                        ob, ok = K(OUT)
                        pe.wait_ge(ob.free, ob.nth(b.n, ok) + 1)
                    pe.wait_ge(bk.free, bk.nth(b.n, k))
                    flat = src[:, :, :].rearrange("p q c -> p (q c)")
                    for i in range(2):
                        last = pe.transpose(out[:, i * P:(i + 1) * P], flat[:, i * P:(i + 1) * P], c.ident[:, :])
                last.then_inc(bk.full, 1)

            pipelined3(pe, B, 2, period({"early": early, "score": score, "turn": turn, "stream": stream, "tail": tail}))

        @block.scalar
        def _(act):
            act.wait_ge(set_up, 6 if l1 else 3)

            def early(b, f):
                p = b.k % 2
                bk, k = F(f)
                if f in V_JOBS:
                    return
                act.wait_ge(bk.full, bk.nth(b.n, k))
                if f == T:
                    if masked:
                        g, be = ("l3_ln2_g", "l3_ln2_b") if cross else ("l3_ln1_g", "l3_ln1_b")
                        for t in range(2):
                            last = act.activation(x_T[:, p, t * P:(t + 1) * P], bk.ap[:, t * P:(t + 1) * P], ACT.Identity,
                                                  bias=c.col(be, t), scale=c.col(g, t))
                    else:
                        n = 4 if l0 else 2
                        last = act.activation(x_T[:, p, 0:n * P], bk.ap[:, 0:n * P], ACT.Copy)
                elif l0:
                    last = act.activation(QK[:, p, :], bk.ap[:, :], ACT.Copy)
                elif l1:
                    dst, name = (QT[p], "l1_q_b") if f == Q_JOB else (KT[p], "l1_k_b")
                    n = z.nq if f == Q_JOB else z.nk
                    for t in range(2):
                        last = act.activation(dst[:, t, :], bk.ap[:, t * n:(t + 1) * n], ACT.Identity,
                                              bias=c.col(name, t), scale=1.0)
                else:
                    for j, (dst, name) in enumerate(((QT[p], "l3_q_b"), (KT[p], "l3_k_b"))):
                        at = 2 * P * j
                        for t in range(2):
                            last = act.activation(dst[:, t, :], bk.ap[:, at + t * P:at + (t + 1) * P],
                                                  ACT.Identity, bias=c.col(name + ("2" if cross else "1"), t), scale=1.0)
                last.then_inc(bk.free, 1)

            def stream(b, n):
                if masked:
                    n -= 1
                if n not in range(z.turned_jobs):
                    return
                if l1 and n == 0:
                    act.activation(mask_step[:, :], mask_col[:, bass.ds(b.n, 1)], ACT.Copy).then_inc(mask_copied, 1)
                    act.wait_ge(mask_copied, b.n + 1)
                if masked:
                    act.wait_ge(shifts[n % 2].free, shifts[n % 2].nth(b.n, n // 2) + 1)
                    act.activation(PT[:, n % 3, :], t_shifted[:, n % 2, :], ACT.Exp).then_inc(probs_ready, 1)
                    return
                bk, k = turned[n % 2], n // 2
                act.wait_ge(bk.full, bk.nth(b.n, k))
                bias = mask_step[:, :] if l1 and n % z.kt == 0 else 0.0
                act.activation(PT[:, n % 3, :], bk.ap[:, :], ACT.Exp, bias=bias, scale=z.scale).then_inc(probs_ready, 1)
                act.wait_ge(probs_ready, b.times(z.turned_jobs, n + 1))
                act.sem_inc(bk.free, 1)

            def tail(b, m):
                bk, k = K(m)
                if m in TURN or m == OUT:
                    return
                act.wait_ge(bk.full, bk.nth(b.n, k))
                if m == CTX_T:
                    if l0:
                        last = act.activation(ctx_T[:, 0, :], bk.ap[:, 0:z.nq], ACT.Copy)
                    else:
                        name = "l1_v_b" if l1 else "l3_v_b2" if cross else "l3_v_b1"
                        for t in range(2):
                            last = act.activation(ctx_T[:, t, :], bk.ap[:, t * P:(t + 1) * P], ACT.Identity,
                                                  bias=c.col(name, t), scale=1.0)
                elif l0:
                    carry_wait(act, c)
                    if m == TAIL[-1]:
                        last = act.activation(c.nT_flat[:, bass.ds(b.n * 256, 256)], bk.ap[:, 0:256], ACT.Identity,
                                              bias=c.col("l0_ffn_b", 0), scale=c.col("l0_ffn_g", 0))
                    else:
                        last = act.activation(c.acc_flat[:, bass.ds(b.n * 256, 256)], bk.ap[:, 0:256], ACT.Copy)
                else:
                    carry_wait(act, c)
                    for t in range(2):
                        last = act.activation(c.nT[:, t, b.n, :], bk.ap[:, t * P:(t + 1) * P], ACT.Copy,
                                              scale=c.col("l1_post", t))
                last.then_inc(bk.free, 1)

            pipelined3(act, B, 2, period({"early": early, "stream": stream, "tail": tail}))

        @block.vector
        def _(dve):
            dve.wait_ge(set_up, 6 if l1 else 3)

            def begin(b, part):
                if l1:
                    return
                p = b.k % 2
                tiles = [x_in[:, p, t, :] for t in range(4)] if l0 else [c.x[:, b.n, :]]
                if part == 1:
                    if l0:
                        dve.wait_ge(x_ready, b.n + 1)
                    for t, x in enumerate(tiles):
                        last = dve.bn_stats(stats[:, t, :], x)
                    last.then_inc(stats_done, 1)
                    dve.wait_ge(stats_done, b.n + 1)
                    dve.memset(c.waiter[:, :], 0.0)
                    for t in range(len(tiles)):
                        last = dve.bn_aggr(mean_var[:, t, :], stats[:, t, :])
                    last.then_inc(var_done, 1)
                if part == 2:
                    dve.wait_ge(rstd_done, b.n + 1)
                    for t, x in enumerate(tiles):
                        out = xn[:, t, :] if l0 else xn[:, 0:2, :].rearrange("p t c -> p (t c)")
                        last = dve.tensor_scalar(out=out, in0=x, scalar1=mean_var[:, t, 0:1], scalar2=rstd[:, t, :],
                                                 op0=ALU.subtract, op1=ALU.mult)
                    last.then_inc(xn_done, 1)

            def early(b, f):
                p = b.k % 2
                if f not in V_JOBS:
                    return
                bk, k = F(f)
                dve.wait_ge(bk.full, bk.nth(b.n, k))
                for t in range(2 if l0 else 1):
                    kt = t if l0 else f - V_JOBS[0]
                    src = bk.ap[:, t * width:(t + 1) * width].rearrange("p (h d) -> p h d", h=H)
                    last = dve.tensor_copy(V[:, p, kt, :, 0:z.dh], src)
                last.then_inc(bk.free, 1)

            def blocks(b, _):
                for t in range(1 if masked else z.ct):
                    q_to_blocks(dve, b, t, q_blocks_ready[0])

            def maximum(b, j, src):
                per_tile = H // z.hk
                q, h = j // per_tile, j % per_tile * z.hk
                return dve.tensor_reduce(neg_max[:, q, h:h + z.hk], src.rearrange("p (h k) -> p h k", h=z.hk), AX,
                                         ALU.max, negate=True)

            def score(b, j):
                bk, k = F(z.early_jobs + j)
                dve.wait_ge(bk.full, bk.nth(b.n, k))
                if not masked:
                    maximum(b, j, bk.ap[:, :]).then_inc(bk.free, 1)
                    return
                p = b.k % 2 if cross else 0
                if cross:
                    dve.wait_ge(mask_made, b.times(MASK_OPS, MASK_OPS))
                dve.tensor_tensor(out=by_head(s_masked[:, j % 2, :]), in0=by_head(bk.ap[:, :]),
                                  in1=all_heads(mask_mul[:, p, 0, :]), op=ALU.mult).then_inc(bk.free, 1)
                if j > 0:
                    dve.wait_ge(s_ready, b.times(4, j))
                    maximum(b, j - 1, s_biased[:, (j - 1) % 2, :])

            def parts(b, _):
                if masked:
                    dve.wait_ge(s_ready, b.times(4, 4))
                    maximum(b, 3, s_biased[:, 1, :]).then_inc(max_done, 1)
                    dve.wait_ge(max_done, b.times(3, 1))
                else:
                    for j in (z.score_jobs - 2, z.score_jobs - 1):
                        bk, k = F(z.early_jobs + j)
                        dve.wait_ge(bk.free, bk.nth(b.n, k) + 1)
                    dve.sem_inc(max_done, 1)
                dve.tensor_copy(neg_max_bf[:, :, 0:H], neg_max[:, :, :]).then_inc(max_done, 1)
                dve.wait_ge(max_done, b.times(3, 2))
                dve.tensor_tensor(out=neg_max_bf[:, :, H:2 * H], in0=neg_max[:, :, :], in1=neg_max_bf[:, :, 0:H],
                                  op=ALU.subtract).then_inc(max_done, 1)

            def turn(b, _):
                bk, k = F(N_JOB)
                dve.wait_ge(bk.full, bk.nth(b.n, k))
                dve.tensor_copy(neg_max_T[:, b.k % 2, :], bk.ap[:, :].bitcast(BF16)[:, 0:z.nq]).then_inc(bk.free, 1)

            def shift(b, n):
                bk, k = shifts[n % 2], n // 2
                dve.wait_ge(bk.full, bk.nth(b.n, k))
                tb = turned[n % 2]
                dve.wait_ge(tb.free, tb.nth(b.n, k) + 1)
                if n >= 2:
                    dve.wait_ge(probs_ready, b.times(4, n - 1))
                dve.tensor_tensor(out=t_shifted[:, n % 2, :], in0=t_masked[:, n % 3, :], in1=bk.ap[:, :],
                                  op=ALU.add).then_inc(bk.free, 1)

            def stream(b, n):
                if masked:
                    if n < z.turned_jobs:
                        p = b.k % 2 if cross else 0
                        bk, k = turned[n % 2], n // 2
                        dve.wait_ge(bk.full, bk.nth(b.n, k))
                        dve.tensor_tensor(out=by_head(t_masked[:, n % 3, :]), in0=by_head(bk.ap[:, :]),
                                          in1=all_heads(mask_mul[:, p, 1, :]), op=ALU.mult).then_inc(bk.free, 1)
                    if 1 <= n <= z.turned_jobs:
                        shift(b, n - 1)
                for i, cb in enumerate(context):
                    if n == (z.turned_jobs * (i + 1)) // len(context) + lag - 1:
                        dve.wait_ge(cb.full, b.n + 1)
                        per = 4 // len(context)
                        dve.tensor_copy(ctx_den[:, i * per:(i + 1) * per, :].rearrange("p g q -> p (g q)"),
                                        cb.ap[:, 0:per * z.nq]).then_inc(cb.free, 1)

            def tail(b, m):
                p = b.k % 2
                bk, k = K(m)
                if m in TURN:
                    q = m - TURN[0]
                    dve.wait_ge(bk.full, bk.nth(b.n, k))
                    slots = bk.ap[:, :].rearrange("p (h s) -> p h s", h=H)
                    dve.reciprocal(rden[:, q, :, :], slots[:, :, z.dh:z.dh + 1]).then_inc(rden_done, 1)
                    dve.wait_ge(rden_done, b.times(z.qt, q + 1))
                    dve.tensor_tensor(out=ctx_q[:, q, :, :], in0=slots[:, :, 0:z.dh],
                                      in1=rden[:, q, :, :].to_broadcast([P, H, z.dh]), op=ALU.mult).then_inc(bk.free, 1)
                elif m == OUT:
                    dve.wait_ge(bk.full, bk.nth(b.n, k))
                    if masked:
                        dve.tensor_tensor(out=c.x[:, b.n, :], in0=res[:, p, :], in1=bk.ap[:, 0:D], op=ALU.add)\
                            .then_inc(bk.free, 1)
                        return
                    flat = r[:, :, :].rearrange("p q c -> p (q c)")
                    if l0:
                        dve.tensor_copy(flat, bk.ap[:, 0:256]).then_inc(bk.free, 1)
                    else:
                        dve.tensor_tensor(out=flat, in0=res[:, p, :], in1=bk.ap[:, 0:256], op=ALU.add)\
                            .then_inc(bk.free, 1)
                    dve.wait_ge(bk.free, bk.nth(b.n, k) + 1)
                    if l0:
                        for q in range(z.qt):
                            last = dve.bn_stats(stats_b[:, q, :], r[:, q, :])
                        last.then_inc(stats_b_done, 1)
                        dve.wait_ge(stats_b_done, b.n + 1)
                        dve.memset(c.waiter[:, :], 0.0)
                        for q in range(z.qt):
                            last = dve.bn_aggr(mean_var_b[:, q, :], stats_b[:, q, :])
                        last.then_inc(var_b_done, 1)
                        dve.wait_ge(rstd_b_done, b.n + 1)
                        for q in range(z.qt):
                            last = dve.tensor_scalar(out=rn[:, q, :], in0=r[:, q, :], scalar1=mean_var_b[:, q, 0:1],
                                                     scalar2=rstd_b[:, q, :], op0=ALU.subtract, op1=ALU.mult)
                        last.then_inc(rn_done, 1)
                    else:
                        dve.tensor_tensor_reduce(out=rn[:, 0, :], in0=r[:, 0, :], in1=r[:, 0, :], scale=1.0 / D,
                                                 scalar=0.0, op0=ALU.mult, op1=ALU.add,
                                                 accum_out=mean_var_b[:, 0, 1:2]).then_inc(var_b_done, 1)
                        dve.wait_ge(rstd_b_done, b.n + 1)
                        dve.tensor_scalar(out=rn[:, 0, :], in0=r[:, 0, :], scalar1=rstd_b[:, 0, :], scalar2=None,
                                          op0=ALU.mult).then_inc(rn_done, 1)

            pipelined3(dve, B, 2, period({"begin": begin, "early": early, "blocks": blocks, "score": score, "parts": parts,
                                          "turn": turn, "stream": stream, "tail": tail}))


def wide_heads(c, a):
    nc = c.nc
    G = 4
    T = G * S
    scale = float(P) ** -0.5
    steps = H * G
    with ExitStack() as ctx:
        def sb(n, shape, dt=F32):
            return ctx.enter_context(nc.sbuf_tensor(f"l2h{a}_{n}", shape, dt))

        sems = []

        def sem(n):
            sems.append(ctx.enter_context(nc.semaphore(f"l2h{a}_{n}")))
            return sems[-1]

        weights = sb("weights", [P, 2, 4, D])
        QT = sb("QT", [P, 2, T])
        KT = sb("KT", [P, 2, T])
        V = sb("V", [P, 2, G, P + 1])
        max_s = sb("max_s", [P, G])
        max_all = sb("max_all", [P, G])
        shift = sb("shift", [P, P], BF16)
        extra_arg = sb("extra_arg", [P, 2, G])
        extra_prob = sb("extra_prob", [P, 2, G])
        shift_T = sb("shift_T", [P, 2, P], BF16)
        PT = sb("PT", [P, T])
        den = sb("den", [P, G])
        rden = sb("rden", [P, G])
        ctx_q = sb("ctx_q", [P, G, P])
        ctx_T = sb("ctx_T", [P, T])
        head_vectors = sb("head_vectors", [P, 2, 4, 1])
        banks = [ctx.enter_context(nc.psum_tensor(f"l2h{a}_psum{i}", [P, BANK], F32)) for i in range(8)]

        def bank(n, what, jobs):
            return Bank(banks[n], sem(f"{what}_full"), sem(f"{what}_free"), jobs)

        q_bank = bank(0, "q", 1)
        k_bank = bank(1, "k", 1)
        v_bank = bank(2, "v", 1)
        s_bank = bank(3, "s", 2)
        t_bank = bank(4, "t", 1)
        pv_bank = [bank(5, "pv0", 2), bank(6, "pv1", 1)]
        o_bank = [bank(7, "o0", 1), bank(0, "o1", 1)]

        weights_loaded = [sem(f"weights_loaded{p}") for p in range(2)]
        set_up = sem("set_up")
        max_done = sem("max_done")
        extra_ready = sem("extra_ready")
        vectors_ready = sem("vectors_ready")
        probs_ready = sem("probs_ready")
        den_done = sem("den_done")
        ctx.callback(clear_semaphores, nc, sems)
        block = ctx.enter_context(nc.Block())
        OPS = 6

        def head(s):
            return s.i * 2 + s.k // G

        @block.sync
        def _(sync):
            for bk in [q_bank, k_bank, v_bank, s_bank, t_bank, o_bank[0]] + pv_bank:
                sync.sem_inc(bk.free, 1)
            sync.sem_inc(o_bank[1].free, 3)

            def load(h, p):
                sync.dma_start(weights[:, p, :, :], c.dram[f"l2_heads{a}"][h].rearrange("w p n -> p w n"))\
                    .then_inc(weights_loaded[p], 16)

            for p in range(2):
                load(p, p)
            with sync.Fori(1, H // 2) as i:
                for p in range(2):
                    sync.wait_ge(o_bank[1].full, ((i - 1) * 2 + p + 1) * G)
                    load(i * 2 + p, p)

        @block.gpsimd
        def _(pool):
            pool.memset(shift[:, :], 0.0).then_inc(set_up, 1)
            pool.memset(V[:, :, :, P:P + 1], 1.0).then_inc(set_up, 1)

        @block.tensor
        def _(pe):
            pe.wait_ge(set_up, 2)

            def front_w(s, which):
                return weights[:, (s.k // G) % 2, which, :].rearrange("p (t n) -> p t n", t=2)

            def q_or_k(s, which):
                if which == 0 and s.k % G == 0:
                    pe.wait_ge(weights_loaded[(s.k // G) % 2], (s.i + s.k // 8) * 16 + 16)
                g = s.k % G
                bk = (q_bank, k_bank)[which]
                src = (c.nT, c.ctx_T)[which]
                pe.wait_ge(bk.free, bk.nth(s.n, 0))
                if which == 0:
                    pe.wait_ge(o_bank[1].free, s.n + 1)
                for t in range(2):
                    last = pe.matmul(bk.ap[:, :], front_w(s, which)[:, t, :], src[:, t, g * G:(g + 1) * G, :],
                                     start=(t == 0), stop=(t == 1))
                last.then_inc(bk.full, 1)

            def values(s):
                g = s.k % G
                pe.wait_ge(v_bank.free, s.n + 1)
                for i in range(G):
                    for t in range(2):
                        last = pe.matmul(v_bank.ap[:, i * P:(i + 1) * P], c.ctx_T[:, t, g * G + i, :],
                                         front_w(s, 2)[:, t, :], start=(t == 0), stop=(t == 1))
                last.then_inc(v_bank.full, 1)

            def scores(s):
                p = s.k % 2
                pe.wait_ge(q_bank.free, s.n + 2)
                pe.wait_ge(k_bank.free, k_bank.nth(s.n, 0) + 1)
                pe.wait_ge(s_bank.free, s_bank.nth(s.n, 0))
                for i in range(G):
                    cols = slice(i * S, (i + 1) * S)
                    last = pe.matmul(s_bank.ap[:, cols], upper_half(QT[:, p, cols]), upper_half(KT[:, p, cols]),
                                     start=True, stop=True)
                last.then_inc(s_bank.full, 1)

            def turn_shift(s):
                pe.wait_ge(max_done, s.times(OPS, OPS - 2))
                pe.wait_ge(s_bank.free, s_bank.nth(s.n, 1))
                pe.transpose(s_bank.ap[:, :].bitcast(BF16)[:, 0:P], shift[:, :], c.ident_bf[:, :])\
                    .then_inc(s_bank.full, 1)

            def scores_T(s):
                p = s.k % 2
                pe.wait_ge(s_bank.free, s_bank.nth(s.n, 1) + 1)
                pe.wait_ge(t_bank.free, t_bank.nth(s.n, 0))
                for i in range(G):
                    cols = slice(i * S, (i + 1) * S)
                    pe.matmul(t_bank.ap[:, cols], KT[:, p, cols], QT[:, p, cols], start=True, stop=False)
                    last = pe.matmul(t_bank.ap[:, cols], c.select4[:, i:i + 1].to_broadcast([P, P]), shift_T[:, p, :],
                                     start=False, stop=True)
                last.then_inc(t_bank.full, 1)

            def context(s):
                p = s.k % 2
                pe.wait_ge(v_bank.free, s.n + 2)
                pe.wait_ge(t_bank.free, t_bank.nth(s.n, 0) + 1)
                for i in range(G):
                    bk = pv_bank[i // 2]
                    if i % 2 == 0:
                        pe.wait_ge(bk.free, bk.nth(s.n, 0))
                    last = pe.matmul(bk.ap[:, (i % 2) * (P + 1):(i % 2 + 1) * (P + 1)], PT[:, i * S:(i + 1) * S],
                                     V[:, p, i, :], start=True, stop=True)
                    if i % 2 == 1:
                        last.then_inc(bk.full, 1)

            def turn_context(s):
                for bk in pv_bank:
                    pe.wait_ge(bk.free, bk.nth(s.n, 0) + 1)
                for i in range(G):
                    last = pe.transpose(pv_bank[0].ap[:, i * P:(i + 1) * P], ctx_q[:, i, :], c.ident[:, :])
                last.then_inc(pv_bank[0].full, 1)

            def output(s, t):
                wo = weights[:, (s.k // G) % 2, 3, :]
                bk = o_bank[t]
                if t == 0:
                    pe.wait_ge(pv_bank[0].free, pv_bank[0].nth(s.n, 1) + 1)
                    pe.wait_ge(bk.free, s.n + 1)
                pe.matmul(bk.ap[:, :], wo[:, t * P:(t + 1) * P], ctx_T[:, :], start=True, stop=True)\
                    .then_inc(bk.full, 1)

            def period(fr, mid, bk):
                if bk is not None:
                    turn_context(bk)
                if mid is not None:
                    scores_T(mid)
                if fr is not None:
                    q_or_k(fr, 0)
                    q_or_k(fr, 1)
                if mid is not None:
                    context(mid)
                if bk is not None:
                    output(bk, 0)
                    if fr is not None:
                        pe.wait_ge(q_bank.free, fr.n + 2)
                    pe.wait_ge(o_bank[1].free, bk.n + 3)
                    output(bk, 1)
                if fr is not None:
                    scores(fr)
                    values(fr)
                    turn_shift(fr)

            pipelined3(pe, steps, 8, period)

        @block.scalar
        def _(act):
            def vectors(s):
                at = COL_AT[f"l2_bq{a}"][0]
                act.activation(head_vectors[:, (s.k // G) % 2, :, :],
                               c.cols[:, at:at + 4 * H].rearrange("p (v h) -> p v h", v=4)[:, :, bass.ds(head(s), 1)],
                               ACT.Copy).then_inc(vectors_ready, 1)
                act.wait_ge(vectors_ready, head(s) + 1)

            def vector(s, which):
                return head_vectors[:, (s.k // G) % 2, which, :]

            def q_or_k(s, which):
                bk = (q_bank, k_bank)[which]
                dst = (QT, KT)[which][:, s.k % 2, :]
                act.wait_ge(bk.full, bk.nth(s.n, 0))
                act.activation(dst, bk.ap[:, :], ACT.Identity, bias=vector(s, which),
                               scale=1.0).then_inc(bk.free, 1)

            def probs(s):
                act.wait_ge(t_bank.full, t_bank.nth(s.n, 0))
                act.activation(PT[:, :], t_bank.ap[:, :], ACT.Exp, scale=scale).then_inc(t_bank.free, 1)

            def extra(s):
                act.wait_ge(max_done, s.times(OPS, OPS))
                act.activation(extra_prob[:, s.k % 2, :], extra_arg[:, s.k % 2, :], ACT.Exp, scale=scale)\
                    .then_inc(extra_ready, 1)

            def context(s):
                act.wait_ge(pv_bank[0].full, pv_bank[0].nth(s.n, 1))
                act.activation(ctx_T[:, :], pv_bank[0].ap[:, :], ACT.Identity, bias=vector(s, 3), scale=1.0)\
                    .then_inc(pv_bank[0].free, 1)

            def period(fr, mid, bk):
                if bk is not None:
                    context(bk)
                if mid is not None:
                    probs(mid)
                if fr is not None:
                    if fr.k % G == 0:
                        vectors(fr)
                    q_or_k(fr, 0)
                    q_or_k(fr, 1)
                    extra(fr)

            pipelined3(act, steps, 8, period)

        @block.vector
        def _(dve):
            dve.wait_ge(set_up, 2)

            def values(s):
                dve.wait_ge(v_bank.full, s.n + 1)
                bias = c.value_bias[:, bass.ds(head(s) * P, P)].unsqueeze(1).to_broadcast([P, G, P])
                dve.tensor_tensor(out=V[:, s.k % 2, :, 0:P], in0=v_bank.ap[:, :].rearrange("p (i d) -> p i d", i=G),
                                  in1=bias, op=ALU.add).then_inc(v_bank.free, 1)

            def maxima(s):
                g, p = s.k % G, s.k % 2
                extra = c.extra[:, head(s), g * G:(g + 1) * G]
                dve.wait_ge(s_bank.full, s_bank.nth(s.n, 0))
                dve.tensor_reduce(max_s[:, :], s_bank.ap[:, :].rearrange("p (i k) -> p i k", i=G), AX, ALU.max)\
                    .then_inc(s_bank.free, 1)
                dve.wait_ge(s_bank.free, s_bank.nth(s.n, 0) + 1)
                dve.tensor_tensor(out=max_all[:, :], in0=max_s[:, :], in1=extra, op=ALU.max).then_inc(max_done, 1)
                dve.wait_ge(max_done, s.times(OPS, 1))
                dve.tensor_scalar(out=shift[:, 0:G], in0=max_all[:, :], scalar1=-1.0, scalar2=None, op0=ALU.mult)\
                    .then_inc(max_done, 1)
                dve.wait_ge(max_done, s.times(OPS, 2))
                dve.scalar_tensor_tensor(out=shift[:, G:2 * G], in0=max_all[:, :], scalar=-1.0, in1=shift[:, 0:G],
                                         op0=ALU.mult, op1=ALU.subtract).then_inc(max_done, 1)
                dve.tensor_tensor(out=extra_arg[:, p, :], in0=extra, in1=shift[:, 0:G], op=ALU.add)\
                    .then_inc(max_done, 1)
                dve.wait_ge(max_done, s.times(OPS, 4))
                dve.tensor_tensor(out=extra_arg[:, p, :], in0=extra_arg[:, p, :], in1=shift[:, G:2 * G], op=ALU.add)\
                    .then_inc(max_done, 1)
                dve.wait_ge(max_done, s.times(OPS, 5))
                dve.sem_inc(max_done, 1)

            def turned_shift(s):
                dve.wait_ge(s_bank.full, s_bank.nth(s.n, 1))
                dve.tensor_copy(shift_T[:, s.k % 2, :], s_bank.ap[:, :].bitcast(BF16)[:, 0:P]).then_inc(s_bank.free, 1)

            def context(s):
                p = s.k % 2
                dve.wait_ge(extra_ready, s.n + 1)
                for j, bk in enumerate(pv_bank):
                    two = slice(2 * j, 2 * j + 2)
                    pv = bk.ap[:, 0:2 * (P + 1)].rearrange("p (i d) -> p i d", i=2)
                    dve.wait_ge(bk.full, bk.nth(s.n, 0))
                    dve.tensor_tensor(out=den[:, two].unsqueeze(2), in0=extra_prob[:, p, two].unsqueeze(2),
                                      in1=pv[:, :, P:P + 1], op=ALU.add).then_inc(den_done, 1)
                    dve.wait_ge(den_done, s.times(4, 2 * j + 1))
                    dve.reciprocal(rden[:, two], den[:, two]).then_inc(den_done, 1)
                    dve.wait_ge(den_done, s.times(4, 2 * j + 2))
                    dve.tensor_tensor(out=ctx_q[:, two, :], in0=pv[:, :, 0:P],
                                      in1=rden[:, two].unsqueeze(2).to_broadcast([P, 2, P]), op=ALU.mult)\
                        .then_inc(bk.free, 1)

            def output(s, t):
                g = s.k % G
                acc = c.acc[:, t, g * G:(g + 1) * G, :].rearrange("p b s -> p (b s)")
                dve.wait_ge(o_bank[t].full, s.n + 1)
                dve.tensor_tensor(out=acc, in0=acc, in1=o_bank[t].ap[:, :], op=ALU.add).then_inc(o_bank[t].free, 1)

            def period(fr, mid, bk):
                if mid is not None:
                    context(mid)
                if bk is not None:
                    output(bk, 0)
                    output(bk, 1)
                if fr is not None:
                    maxima(fr)
                    turned_shift(fr)
                    values(fr)

            pipelined3(dve, steps, 8, period)


def build(nc, dram, out):
    c = Chip()
    c.nc, c.dram, c.out = nc, dram, out
    with ExitStack() as ctx:
        def sb(n, shape, dt=F32):
            return ctx.enter_context(nc.sbuf_tensor(n, shape, dt))

        c.x_flat = sb("x", [P, B * D])
        c.x = c.x_flat[:, :].rearrange("p (b d) -> p b d", b=B)
        c.nT_flat = sb("nT", [P, 2 * B * S])
        c.nT = c.nT_flat[:, :].rearrange("p (t b s) -> p t b s", t=2, b=B)
        c.acc_flat = sb("acc", [P, 2 * B * S])
        c.acc = c.acc_flat[:, :].rearrange("p (t b s) -> p t b s", t=2, b=B)
        c.cols = sb("cols", [P, N_COLS])
        c.rows = sb("rows", [P, N_ROWS])
        c.ident = sb("ident", [P, P])
        c.ident_bf = sb("ident_bf", [P, P], BF16)
        c.ones_bf = sb("ones_bf", [P, P], BF16)
        c.minus_half = sb("minus_half", [P, 4])
        c.epsilons = sb("epsilons", [P, 2])
        c.quarter = sb("quarter", [P, 1])
        c.one = sb("one", [P, 1])
        c.waiter = sb("waiter", [P, 1])
        c.waiter_pool = sb("waiter_pool", [P, 8])
        c.waiter_act = sb("waiter_act", [P, 8])
        c.carried = 0
        c.shapes = sb("shapes", [P, 2 * H + H + 4])
        c.select = sb("select", [P, H + 4], BF16)
        c.select16 = c.select[:, 0:H]
        c.select4 = c.select[:, H:H + 4]

        def col(name, t):
            at, n = COL_AT[name]
            return c.cols[:, at + t:at + t + 1]

        def row(name):
            return c.rows[:, ROW_AT[name]:ROW_AT[name] + ROW_LEN[name]]

        def pair(name):
            return c.rows[:, ROW_AT[name]:ROW_AT[name] + 2 * S].rearrange("p (s c) -> p s c", s=2).unsqueeze(2)\
                .to_broadcast([P, 2, 2, S])

        def head_mask(dim):
            return c.shapes[:, 0:H] if dim == 8 else c.shapes[:, H:2 * H]

        c.col, c.row, c.pair, c.head_mask = col, row, pair, head_mask
        c.w = {}
        c.lasting = lambda n: ctx.enter_context(nc.semaphore(n))
        l1_loaded = c.lasting("l1_weights_loaded")
        l2_loaded = c.lasting("l2_loaded")
        l3_loaded = c.lasting("l3_weights_loaded")
        l1_dmas = sum(name.startswith("l1") for name in WEIGHTS_01)

        for name in WEIGHTS_2:
            c.w[name] = ctx.enter_context(nc.sbuf_tensor(name, list(WEIGHTS_2[name]), F32))
        c.ctx_T_flat = ctx.enter_context(nc.sbuf_tensor("ctx_T_all", [P, 2 * B * S], F32))
        c.ctx_T = c.ctx_T_flat[:, :].rearrange("p (t b s) -> p t b s", t=2, b=B)
        with ExitStack() as early:
            for name in WEIGHTS_01:
                c.w[name] = early.enter_context(nc.sbuf_tensor(name, list(WEIGHTS_01[name]), F32))
            with nc.sbuf_tensor("pos", [P, 4, P], F32) as pos:
                c.pos = pos
                load_constants(c, l1_loaded, l2_loaded)
                narrow_attention(c, LAYER0)
            mlp(c, "l0_mlp", c.w["l0_w1"], "l0_b1", c.w["l0_w2"], ACT.Gelu, P, 2 * P, "channels")
            wait_for(c, l1_loaded, l1_dmas)
            narrow_attention(c, LAYER1)
            mlp(c, "l1_mlp", c.w["l1_w1"], "l1_b1", c.w["l1_w2"], ACT.Gelu_apprx_tanh, D, FF, "l1_b2")
        wait_for(c, l2_loaded, len(WEIGHTS_2) + 2)
        with ExitStack() as late:
            for name in WEIGHTS_3:
                c.w[name] = late.enter_context(nc.sbuf_tensor(name, list(WEIGHTS_3[name]), F32))
            start_loads(c, WEIGHTS_3, l3_loaded)
            with ExitStack() as two:
                c.value_rows = two.enter_context(nc.sbuf_tensor("value_rows", [P, 2, H * P], F32))
                c.extra = two.enter_context(nc.sbuf_tensor("extra", [P, H, B], F32))
                c.value_bias = two.enter_context(nc.sbuf_tensor("value_bias", [P, H * P], F32))
                for a in (1, 2):
                    norm_transposed(c, f"l2_norm{a}", f"l2_ln{a}_g", f"l2_ln{a}_b",
                                    add="l2_bo1" if a == 2 else None, ahead_of=a)
                    wide_heads(c, a)
                norm_transposed(c, "l2_norm3", "l2_lnm_g", "l2_lnm_b", add="l2_bo2")
            mlp(c, "l2_mlp", c.w["l2_w1"], "l2_b1", c.w["l2_w2"], ACT.Gelu, D, FF, "l2_b2")
            wait_for(c, l3_loaded, len(WEIGHTS_3))
            narrow_attention(c, LAYER3_SELF)
            narrow_attention(c, LAYER3_CROSS)
            norm_transposed(c, "l3_norm3", "l3_ln3_g", "l3_ln3_b")
            mlp(c, "l3_mlp", c.w["l3_w1"], "l3_b1", c.w["l3_w2"], ACT.Gelu_apprx_tanh, D, FF, "l3_b2")


def start_loads(c, names, loaded):
    with c.nc.Block() as block:
        @block.sync
        def _(sync):
            for name in names:
                sync.dma_start(c.w[name][:, :, :], c.dram[name]).then_inc(loaded, 16)


def wait_for(c, loaded, dmas):
    with c.nc.Block() as block:
        @block.sync
        def _(sync):
            sync.wait_ge(loaded, 16 * dmas)


WEIGHTS_01 = {
    "l0_wq": (P, 1, P), "l0_wk": (P, 1, P), "l0_wv": (P, 1, P), "l0_wo": (P, 1, P),
    "l0_w1": (P, 1, 2 * P), "l0_w2": (P, 2, P),
    "l1_wq": (P, 2, D), "l1_wk": (P, 2, D), "l1_wv": (P, 2, D), "l1_wo": (P, 2, D),
    "l1_w1": (P, 2, FF), "l1_w2": (P, 8, D),
}
WEIGHTS_2 = {"l2_w1": (P, 2, FF), "l2_w2": (P, 8, D)}
WEIGHTS_3 = {
    "l3_wq": (P, 2, D), "l3_wk": (P, 2, D), "l3_wv": (P, 2, D), "l3_wao": (P, 2, D),
    "l3_wqc": (P, 2, D), "l3_wkc": (P, 2, D), "l3_wvc": (P, 2, D), "l3_wco": (P, 2, D),
    "l3_w1": (P, 2, FF), "l3_w2": (P, 8, D),
}


def positions():
    pos = np.arange(2 * P, dtype=np.float32)[:, None]
    div = np.exp(np.arange(0, P, 2, dtype=np.float32) * np.float32(-np.log(10000.0) / P)).astype(np.float32)
    ang = (pos * div).astype(np.float32)
    pe = np.zeros((2 * P, P), np.float32)
    pe[:, 0::2], pe[:, 1::2] = np.sin(ang), np.cos(ang)
    return pe


def laid_out(i):
    g = {k: np.asarray(v) for k, v in i.items()}
    a = {}
    a["x_T"] = g["x"].transpose(0, 2, 1)
    a["ctx_T"] = g["ctx_2048"].transpose(0, 2, 1)
    a["mask"] = g["mask_BxS2_ik0"]
    a["mask_T"] = g["mask_BxS2_ik0"].T
    m = g["mask_1x1xSxS2_fc1"][0, 0]
    a["self_mask"] = np.stack([m, m.T])
    m = g["mask_Bx1xSxS2_ff1"][:, 0]
    a["cross_mask"] = np.stack([m, m.transpose(0, 2, 1)], 1)

    def tiles(w):
        return w.reshape(-1, P, w.shape[1]).transpose(1, 0, 2)

    kv_w = g["L1_xattn_kv_w"].reshape(D, D, 2)
    kv_b = g["L1_xattn_kv_b"].reshape(D, 2)
    qkv, kvc = g["L3_xattn_w_qkv"], g["L3_xattn_w_kv"]
    b_qkv, b_kvc = g["L3_xattn_b_qkv"], g["L3_xattn_b_kv"]
    w = {
        "l0_wq": g["L0_xattn_Wq"], "l0_wk": g["L0_xattn_Wk"], "l0_wv": g["L0_xattn_Wv"], "l0_wo": g["L0_xattn_Wo"],
        "l0_w1": g["L0_xattn_W1"], "l0_w2": g["L0_xattn_W2"],
        "l1_wq": g["L1_xattn_q_w"], "l1_wk": kv_w[:, :, 0], "l1_wv": kv_w[:, :, 1], "l1_wo": g["L1_xattn_out_w"],
        "l1_w1": g["L1_xattn_mlp_w1"], "l1_w2": g["L1_xattn_mlp_w2"],
        "l2_w1": g["L2_xattn_w_fc1"], "l2_w2": g["L2_xattn_w_fc2"],
        "l3_wq": qkv[:, 0:D], "l3_wk": qkv[:, D:2 * D], "l3_wv": qkv[:, 2 * D:], "l3_wao": g["L3_xattn_w_ao"],
        "l3_wqc": g["L3_xattn_w_q"], "l3_wkc": kvc[:, 0:D], "l3_wvc": kvc[:, D:], "l3_wco": g["L3_xattn_w_co"],
        "l3_w1": g["L3_xattn_w1"], "l3_w2": g["L3_xattn_w2"],
    }
    for name, x in w.items():
        a[name] = tiles(x)
    vec = {
        "l0_ffn_g": g["L0_xattn_ffn_ln_g"], "l0_ffn_b": g["L0_xattn_ffn_ln_b"], "l0_b1": g["L0_xattn_b1"],
        "l0_b2": g["L0_xattn_b2"],
        "l1_q_b": g["L1_xattn_q_b"], "l1_k_b": kv_b[:, 0], "l1_v_b": kv_b[:, 1], "l1_post": g["L1_xattn_postnorm_w"],
        "l1_b1": g["L1_xattn_mlp_b1"],
        "l2_lnm_g": g["L2_xattn_ln_mlp_scale"], "l2_lnm_b": g["L2_xattn_ln_mlp_offset"], "l2_b1": g["L2_xattn_b_fc1"],
        "l3_ln1_g": g["L3_xattn_ln1_s"], "l3_ln1_b": g["L3_xattn_ln1_b"],
        "l3_q_b1": b_qkv[0:D], "l3_k_b1": b_qkv[D:2 * D], "l3_v_b1": b_qkv[2 * D:],
        "l3_ln2_g": g["L3_xattn_ln2_s"], "l3_ln2_b": g["L3_xattn_ln2_b"],
        "l3_q_b2": g["L3_xattn_b_q"], "l3_k_b2": b_kvc[0:D], "l3_v_b2": b_kvc[D:],
        "l3_ln3_g": g["L3_xattn_ln3_s"], "l3_ln3_b": g["L3_xattn_ln3_b"], "l3_b1": g["L3_xattn_b1"],
    }
    for n in (1, 2):
        vec[f"l2_ln{n}_g"] = g[f"L2_xattn_ln{n}_scale"]
        vec[f"l2_ln{n}_b"] = g[f"L2_xattn_ln{n}_offset"]
        for v in ("bq", "bk", "bias_k", "bias_v", "bo"):
            vec[f"l2_{v}{n}"] = g[f"L2_xattn_{v}{n}"].reshape(-1)
        a[f"l2_wq_T{n}"] = g[f"L2_xattn_wq{n}"].reshape(D, H, P).transpose(2, 1, 0)
        a[f"l2_rows{n}"] = np.stack([g[f"L2_xattn_{v}{n}"].reshape(-1) for v in ("bv", "bias_v")])
        by_head = [g[f"L2_xattn_w{v}{n}"].reshape(2, P, H, P).transpose(2, 1, 0, 3).reshape(H, P, D) for v in "qkv"]
        a[f"l2_heads{n}"] = np.stack(by_head + [g[f"L2_xattn_wo{n}"].reshape(H, P, D)], 1)
    a["cols"] = np.concatenate([vec[name].reshape(n, P) for name, n in COLUMNS]).T
    rows = {
        "l0_q_g": g["L0_xattn_ln_q_g"], "l0_kv_g": g["L0_xattn_ln_kv_g"],
        "l0_q_b": g["L0_xattn_ln_q_b"], "l0_kv_b": g["L0_xattn_ln_kv_b"],
        "l1_out_b": g["L1_xattn_out_b"], "l1_b2": g["L1_xattn_mlp_b2"], "l2_b2": g["L2_xattn_b_fc2"],
        "l3_ao_b": g["L3_xattn_b_ao"], "l3_co_b": g["L3_xattn_b_co"], "l3_b2": g["L3_xattn_b2"],
    }
    a["rows"] = np.concatenate([rows[name] for name in ROWS])
    pe = positions().reshape(2, P, P).transpose(1, 0, 2)
    a["pos"] = np.concatenate([pe, pe], 1)
    p, h = np.arange(P)[:, None], np.arange(H)[None, :]
    n4 = np.arange(4)[None, :]
    a["shapes"] = np.concatenate([p // 8 == h, p // 16 == h % 8, (p < 32) & (p % 16 == h), (p < 8) & (p % 4 == n4)],
                                 1).astype(np.float32)
    return {k: np.ascontiguousarray(v) for k, v in a.items()}


def kernel(**inputs):
    import concourse.bacc as bacc
    from concourse.bass_utils import run_bass_kernel_spmd

    nc = bacc.Bacc("TRN2", target_bir_lowering=False, num_devices=1)
    arrays = laid_out(inputs)
    dram = {k: nc.dram_tensor(f"in_{k}", v.shape, mybir.dt.from_np(v.dtype), kind="ExternalInput").ap()
            for k, v in arrays.items()}
    out = nc.dram_tensor("out", (B, S, D), F32, kind="ExternalOutput").ap()
    build(nc, dram, out)
    result = run_bass_kernel_spmd(nc, [{f"in_{k}": v for k, v in arrays.items()}], core_ids=[0])
    return result.results[0]["out"]
```

```python
from contextlib import ExitStack

import numpy as np

import concourse.bass as bass
from concourse import mybir

F32 = mybir.dt.float32
F32R = mybir.dt.float32r
BF16 = mybir.dt.bfloat16
I32 = mybir.dt.int32
ALU = mybir.AluOpType
ACT = mybir.ActivationFunctionType
AX = mybir.AxisListType.X

P = 128
B = 16
D = 256
S = 128
H = 16
BANK = 512
SLOT = 32
FF = 1024
NEG = -1.0e30

COLUMNS = [
    ("l0_ffn_g", 1), ("l0_ffn_b", 1), ("l0_b1", 2), ("l0_b2", 1),
    ("l1_q_b", 2), ("l1_k_b", 2), ("l1_v_b", 2), ("l1_post", 2), ("l1_b1", 8),
    ("l2_ln1_g", 2), ("l2_ln1_b", 2), ("l2_bq1", 16), ("l2_bk1", 16), ("l2_bias_k1", 16), ("l2_bias_v1", 16),
    ("l2_bo1", 2),
    ("l2_ln2_g", 2), ("l2_ln2_b", 2), ("l2_bq2", 16), ("l2_bk2", 16), ("l2_bias_k2", 16), ("l2_bias_v2", 16),
    ("l2_bo2", 2),
    ("l2_lnm_g", 2), ("l2_lnm_b", 2), ("l2_b1", 8),
    ("l3_ln1_g", 2), ("l3_ln1_b", 2), ("l3_q_b1", 2), ("l3_k_b1", 2), ("l3_v_b1", 2),
    ("l3_ln2_g", 2), ("l3_ln2_b", 2), ("l3_q_b2", 2), ("l3_k_b2", 2), ("l3_v_b2", 2),
    ("l3_ln3_g", 2), ("l3_ln3_b", 2), ("l3_b1", 8),
]
COL_AT = {}
for _name, _n in COLUMNS:
    COL_AT[_name] = (sum(n for _, n in COLUMNS[:len(COL_AT)]), _n)
N_COLS = sum(n for _, n in COLUMNS)
ROWS = ["l0_q_g", "l0_kv_g", "l0_q_b", "l0_kv_b", "l1_out_b", "l1_b2", "l2_b2", "l3_ao_b", "l3_co_b", "l3_b2"]
ROW_LEN = {n: (S if n.startswith("l0") else D) for n in ROWS}
ROW_AT = {n: sum(ROW_LEN[m] for m in ROWS[:i]) for i, n in enumerate(ROWS)}
N_ROWS = sum(ROW_LEN.values())


class Bank:

    def __init__(self, ap, full, free, jobs):
        self.ap, self.full, self.free, self.jobs = ap, full, free, jobs

    def nth(self, step, job):
        return step * self.jobs + job + 1


class Step:

    def __init__(self, i, k, per):
        self.i, self.k, self.per = i, k, per
        self.n = i * per + k

    def times(self, count, more):
        return self.n * count + more


def pipelined3(eng, steps, per, period):
    period(Step(0, 0, per), None, None)
    period(Step(0, 1, per), Step(0, 0, per), None)
    rounds, left = (steps - 2) // per, (steps - 2) % per
    with eng.Fori(0, rounds) as i:
        for k in range(per):
            period(Step(i, k + 2, per), Step(i, k + 1, per), Step(i, k, per))
    for k in range(left):
        period(Step(rounds, k + 2, per), Step(rounds, k + 1, per), Step(rounds, k, per))
    period(None, Step(rounds, left + 1, per), Step(rounds, left, per))
    period(None, None, Step(rounds, left + 1, per))


def pipelined4(eng, steps, per, period):
    def full(i, k):
        period(*(Step(i, k + d, per) for d in (3, 2, 1, 0)))

    period(Step(0, 0, per), None, None, None)
    period(Step(0, 1, per), Step(0, 0, per), None, None)
    period(Step(0, 2, per), Step(0, 1, per), Step(0, 0, per), None)
    rounds, left = (steps - 3) // per, (steps - 3) % per
    with eng.Fori(0, rounds) as i:
        for k in range(per):
            full(i, k)
    for k in range(left):
        full(rounds, k)
    period(None, *(Step(rounds, left + d, per) for d in (2, 1, 0)))
    period(None, None, *(Step(rounds, left + d, per) for d in (2, 1)))
    period(None, None, None, Step(rounds, left + 2, per))


class Chip:
    pass


def clear_semaphores(nc, sems):
    for s in sems:
        nc.gpsimd.sem_clear(s)
    nc.all_engine_barrier()


def load_constants(c):
    nc = c.nc
    loaded, made, shapes_loaded = (c.lasting(n) for n in ("constants_loaded", "constants_made", "shapes_loaded"))
    with nc.Block() as block:

        @block.sync
        def _(sync):
            sync.dma_start(c.shapes[:, :], c.dram["shapes"]).then_inc(shapes_loaded, 16)
            sync.dma_start(c.cols[:, :], c.dram["cols"]).then_inc(loaded, 16)
            sync.dma_start(c.rows[:, :], c.dram["rows"].rearrange("(a n) -> a n", a=1).to_broadcast([P, N_ROWS]))\
                .then_inc(loaded, 16)
            mine = [n for n in WEIGHTS_01 if n.startswith("l0")]
            for name in mine:
                sync.dma_start(c.w[name][:, :, :], c.dram[name]).then_inc(loaded, 16)
            sync.dma_start(c.pos[:, :, :], c.dram["pos"]).then_inc(loaded, 16)
            sync.wait_ge(loaded, 16 * (3 + len(mine)))

        @block.gpsimd
        def _(pool):
            pool.memset(c.ident[:, :], 0.0).then_inc(made, 1)
            pool.memset(c.ident_bf[:, :], 0.0).then_inc(made, 1)
            pool.memset(c.ones_bf[:, :], 1.0).then_inc(made, 1)
            pool.memset(c.minus_half[:, :], -0.5).then_inc(made, 1)
            pool.memset(c.epsilons[:, 0:1], 1e-5).then_inc(made, 1)
            pool.memset(c.epsilons[:, 1:2], 1e-6).then_inc(made, 1)
            pool.memset(c.quarter[:, :], 0.25).then_inc(made, 1)
            pool.memset(c.one[:, :], 1.0).then_inc(made, 1)
            pool.wait_ge(made, 8)
            for m in (c.ident, c.ident_bf):
                pool.affine_select(out=m[:, :], in_=m[:, :], compare_op=ALU.not_equal, fill=1.0, base=0,
                                   pattern=[[-1, P]], channel_multiplier=1).then_inc(made, 1)
            pool.wait_ge(shapes_loaded, 16)
            pool.tensor_copy(c.select[:, :], c.shapes[:, 2 * H:]).then_inc(made, 1)
            pool.wait_ge(made, 11)


def load_weights(sync, c, names, loaded):
    for name in names:
        sync.dma_start(c.w[name][:, :, :], c.dram[name]).then_inc(loaded, 16)


def inverse_root(pool, c, chain, at, value, out, eps, n):
    small = c.epsilons[:, 0 if eps == 1e-5 else 1:1 if eps == 1e-5 else 2].unsqueeze(1).to_broadcast([P, n, 1])
    pool.tensor_tensor(out=out, in0=value, in1=small, op=ALU.add).then_inc(chain, 1)
    pool.wait_ge(chain, at + 1)
    return pool.tensor_tensor(out=out, in0=out, in1=c.minus_half[:, 0:n].unsqueeze(2), op=ALU.pow)


def product(pe, out, left, right, start, stop):
    for n, (a, b) in enumerate(((0, 0), (1, 0), (0, 1))):
        last = pe.matmul(out, left[a], right[b], start=(start and n == 0), stop=(stop and n == 2))
    return last


def upper_half(ap):
    return ap.bitcast(BF16)[:, 1::2]


def carry_wait(act, c):
    c.carried = (c.carried + 1) % 8
    act.activation(c.waiter_act[:, c.carried:c.carried + 1], c.minus_half[:, 0:1], ACT.Copy)


def carry_wait_pool(pool, c):
    c.carried = (c.carried + 1) % 8
    pool.tensor_tensor(out=c.waiter_pool[:, c.carried:c.carried + 1], in0=c.one[:, :], in1=c.one[:, :], op=ALU.mult)


def norm_transposed(c, name, gamma, beta, add=None, ahead_of=None):
    nc = c.nc
    with ExitStack() as ctx:
        def sb(n, shape, dt=F32):
            return ctx.enter_context(nc.sbuf_tensor(f"{name}_{n}", shape, dt))

        sems = []

        def sem(n):
            sems.append(ctx.enter_context(nc.semaphore(f"{name}_{n}")))
            return sems[-1]

        staged = sb("staged", [P, 2, 2, S])
        stats = sb("stats", [P, 2, 6])
        mean_var = sb("mean_var", [P, 2, 2])
        rstd = sb("rstd", [P, 2, 1])
        xn = sb("xn", [P, 2, D])
        psum = [ctx.enter_context(nc.psum_tensor(f"{name}_psum{i}", [P, BANK], F32)) for i in range(4)]
        added = [Bank(psum[i], sem(f"added_full{i}"), sem(f"added_free{i}"), 1) for i in range(2)]
        turned = [Bank(psum[2 + i], sem(f"turned_full{i}"), sem(f"turned_free{i}"), 1) for i in range(2)]
        acc_staged = sem("acc_staged")
        stats_done = sem("stats_done")
        var_done = sem("var_done")
        rstd_done = sem("rstd_done")
        pool_chain = sem("pool_chain")
        xn_done = sem("xn_done")
        rows_loaded = sem("rows_loaded")
        if ahead_of:
            wq_T = sb("wq_T", [P, H, D])
            value_rows = sb("value_rows", [P, 2, H * P])
            ctx_split, n_split = sem("ctx_split"), sem("n_split")
            U = sb("U", [P, 2, H])
            products = sb("products", [P, H])
            offset = sb("offset", [P, H])
            ones = sb("ones", [P, P])
            u_psum = ctx.enter_context(nc.psum_tensor(f"{name}_u_psum", [P, BANK], F32))
            extra_psum = ctx.enter_context(nc.psum_tensor(f"{name}_extra_psum", [P, BANK], F32))
            wq_loaded, u_full, u_ready, extra_full, extra_done = (
                sem(n) for n in ("wq_loaded", "u_full", "u_ready", "extra_full", "extra_done"))
        cleared = sem("cleared")
        ctx.callback(clear_semaphores, nc, sems)
        block = ctx.enter_context(nc.Block())

        def turn(s):
            return s.i + s.k // 2 + 1

        @block.sync
        def _(sync):
            for bank in added + turned:
                sync.sem_inc(bank.free, 1)
            if ahead_of:
                sync.dma_start(value_rows[:, :, :], c.dram[f"l2_rows{ahead_of}"].rearrange("(a v) n -> a v n", a=1)
                               .to_broadcast([P, 2, H * P])).then_inc(rows_loaded, 16)
                sync.dma_start(wq_T[:, :, :], c.dram[f"l2_wq_T{ahead_of}"]).then_inc(wq_loaded, 16)

        @block.gpsimd
        def _(pool):
            def period(fr, mid, _):
                if add and fr is not None:
                    p = fr.k % 2
                    pool.wait_ge(added[p].free, turn(fr))
                    carry_wait_pool(pool, c)
                    at = COL_AT[add][0]
                    pool.tensor_tensor(out=staged[:, p, :, :], in0=c.acc[:, :, fr.n, :],
                                       in1=c.cols[:, at:at + 2].unsqueeze(2).to_broadcast([P, 2, S]), op=ALU.add)\
                        .then_inc(acc_staged, 1)
                if mid is not None:
                    p = mid.k % 2
                    pool.wait_ge(var_done, mid.n + 1)
                    inverse_root(pool, c, pool_chain, mid.n, mean_var[:, p:p + 1, 1:2], rstd[:, p:p + 1, :], 1e-5, 1)\
                        .then_inc(rstd_done, 1)

            pipelined3(pool, B, 2, period)
            if ahead_of:
                pool.memset(ones[:, :], 1.0).then_inc(cleared, 1)
                at = {v: COL_AT[f"l2_{v}{ahead_of}"][0] for v in ("bq", "bias_k")}
                pool.tensor_tensor(out=products[:, :], in0=c.cols[:, at["bq"]:at["bq"] + H],
                                   in1=c.cols[:, at["bias_k"]:at["bias_k"] + H], op=ALU.mult).then_inc(cleared, 1)
                if add:
                    pool.wait_ge(acc_staged, B)
                pool.memset(c.acc_flat[:, :], 0.0).then_inc(cleared, 1)
                pool.wait_ge(rows_loaded, 16)
                pool.tensor_tensor(out=c.value_bias[:, :], in0=value_rows[:, 0, :], in1=value_rows[:, 1, :],
                                   op=ALU.subtract).then_inc(cleared, 1)

        @block.tensor
        def _(pe):
            def turn_normed(bk):
                p = bk.k % 2
                pe.wait_ge(xn_done, bk.n + 1)
                pe.wait_ge(turned[p].free, turn(bk))
                for t in range(2):
                    last = pe.transpose(turned[p].ap[:, t * S:(t + 1) * S], xn[:, p, t * P:(t + 1) * P],
                                        c.ident[:, :])
                last.then_inc(turned[p].full, 1)

            def period(fr, _, bk):
                if add and fr is not None:
                    p = fr.k % 2
                    pe.wait_ge(acc_staged, fr.n + 1)
                    pe.wait_ge(added[p].free, turn(fr))
                    for t in range(2):
                        last = pe.transpose(added[p].ap[:, t * S:(t + 1) * S], staged[:, p, t, :], c.ident[:, :])
                    last.then_inc(added[p].full, 1)
                if bk is not None:
                    turn_normed(bk)
            pipelined3(pe, B, 2, period)
            if ahead_of:
                pe.wait_ge(wq_loaded, 16)
                bias_k = c.cols[:, COL_AT[f"l2_bias_k{ahead_of}"][0]:][:, 0:H]
                for h in range(H):
                    for t in range(2):
                        last = pe.matmul(u_psum[:, t * H + h:t * H + h + 1], wq_T[:, h, t * P:(t + 1) * P],
                                         bias_k[:, h:h + 1], start=True, stop=True)
                last.then_inc(u_full, 1)
                pe.wait_ge(u_ready, 1)
                pe.wait_ge(cleared, 2)
                for bank in turned:
                    pe.wait_ge(bank.free, B // 2 + 1)
                pe.matmul(u_psum[:, 2 * H:3 * H], ones[:, :], products[:, :], start=True, stop=True)
                for b in range(B):
                    for t in range(2):
                        last = pe.matmul(extra_psum[:, b * H:(b + 1) * H], c.nT[:, t, b, :], U[:, t, :],
                                         start=(t == 0), stop=(t == 1))
                last.then_inc(extra_full, 1)

        @block.vector
        def _(dve):
            def period(_, fr, bk):
                if fr is not None:
                    p = fr.k % 2
                    x = c.x[:, fr.n, :]
                    if add:
                        dve.wait_ge(added[p].full, turn(fr))
                        dve.tensor_tensor(out=x, in0=x, in1=added[p].ap[:, 0:D], op=ALU.add).then_inc(added[p].free, 1)
                        dve.wait_ge(added[p].free, turn(fr) + 1)
                        dve.memset(c.waiter[:, :], 0.0)
                    dve.bn_stats(stats[:, p, :], x).then_inc(stats_done, 1)
                    dve.wait_ge(stats_done, fr.n + 1)
                    dve.memset(c.waiter[:, :], 0.0)
                    dve.bn_aggr(mean_var[:, p, :], stats[:, p, :]).then_inc(var_done, 1)
                if bk is not None:
                    p = bk.k % 2
                    dve.wait_ge(rstd_done, bk.n + 1)
                    dve.wait_ge(turned[p].free, turn(bk))
                    dve.tensor_scalar(out=xn[:, p, :], in0=c.x[:, bk.n, :], scalar1=mean_var[:, p, 0:1],
                                      scalar2=rstd[:, p, :], op0=ALU.subtract, op1=ALU.mult).then_inc(xn_done, 1)

            pipelined3(dve, B, 2, period)

            def split(parts, full, done):
                high, low = (part[:, :, :, :].rearrange("p t b s -> p (t b s)") for part in parts)
                dve.tensor_copy(high, full).then_inc(done, 1)
                dve.wait_ge(done, 1)
                dve.tensor_tensor(out=low, in0=full, in1=high.bitcast(F32), op=ALU.subtract).then_inc(done, 1)

            if ahead_of == 1:
                dve.wait_ge(c.l2_loaded, 16 * (len(WEIGHTS_2) + 2))
                split(c.ctx_parts, c.ctx_T_flat[:, :], ctx_split)
            if ahead_of:
                dve.wait_ge(u_full, 1)
                dve.tensor_copy(U[:, :, :], u_psum[:, 0:2 * H].rearrange("p (t h) -> p t h", t=2)).then_inc(u_ready, 1)
                for bank in turned:
                    dve.wait_ge(bank.free, B // 2 + 1)
                split(c.n_parts, c.nT_flat[:, :], n_split)
                dve.wait_ge(extra_full, 1)
                dve.tensor_copy(offset[:, :], u_psum[:, 2 * H:3 * H]).then_inc(extra_done, 1)
                dve.wait_ge(extra_done, 1)
                dve.tensor_tensor(out=c.extra[:, :, :], in0=extra_psum[:, 0:B * H].rearrange("p (b h) -> p h b", h=H),
                                  in1=offset[:, :].unsqueeze(2).to_broadcast([P, H, B]), op=ALU.add)\
                    .then_inc(extra_done, 1)

        @block.scalar
        def _(act):
            def period(_, __, bk):
                if bk is not None:
                    p = bk.k % 2
                    act.wait_ge(turned[p].full, turn(bk))
                    carry_wait(act, c)
                    for t in range(2):
                        last = act.activation(c.nT[:, t, bk.n, :], turned[p].ap[:, t * S:(t + 1) * S], ACT.Identity,
                                              bias=c.col(beta, t), scale=c.col(gamma, t))
                    last.then_inc(turned[p].free, 1)

            pipelined3(act, B, 2, period)


def mlp(c, name, w1, b1, w2, func, width, hidden, finish, load_ahead=None):
    nc = c.nc
    kt, ft = width // P, hidden // P
    channels = finish == "channels"
    groups = 8 if channels else 4
    store = name == "l3_mlp"
    with ExitStack() as ctx:
        def sb(n, shape, dt=F32):
            return ctx.enter_context(nc.sbuf_tensor(f"{name}_{n}", shape, dt))

        sems = []

        def sem(n):
            sems.append(ctx.enter_context(nc.semaphore(f"{name}_{n}")))
            return sems[-1]

        hT = sb("hT", [P, 2, ft, BANK])
        w1_parts = [sb(f"w1_{n}", [P, kt, hidden], F32R) for n in ("high", "low")]
        n_parts = [sb(f"n_{n}", [P, 2, kt, BANK], F32R) for n in ("high", "low")]
        psum = [ctx.enter_context(nc.psum_tensor(f"{name}_psum{i}", [P, BANK], F32)) for i in range(8)]
        ups = min(ft, 4)
        up = [Bank(psum[i], sem(f"up_full{i}"), sem(f"up_free{i}"), ft // ups) for i in range(ups)]
        down = [Bank(psum[4 + i], sem(f"down_full{i}"), sem(f"down_free{i}"), 1) for i in range(4)]
        bias_added = sem("bias_added")
        w1_high, w1_low, n_high, n_low = (sem(n) for n in ("w1_high_ready", "w1_low_ready", "n_high", "n_low"))
        stored = sem("stored")
        ctx.callback(clear_semaphores, nc, sems)
        block = ctx.enter_context(nc.Block())

        def tokens(g):
            return c.nT_flat[:, :].rearrange("p (t n) -> p t n", t=kt)[:, :, bass.ds(g * BANK, BANK)]

        @block.sync
        def _(sync):
            for bank in up + down:
                sync.sem_inc(bank.free, 1)
            if load_ahead:
                load_ahead(sync)
            if store:
                with sync.Fori(0, groups) as g:
                    for bank in down:
                        sync.wait_ge(bank.free, g + 2)
                    sync.dma_start(c.out[bass.ds(g * 4, 4), :, :].rearrange("b p d -> p b d"),
                                   c.x[:, bass.ds(g * 4, 4), :]).then_inc(stored, 16)
                sync.wait_ge(stored, 16 * groups)

        @block.gpsimd
        def _(pool):
            if not channels:
                with pool.Fori(0, B) as b:
                    pool.tensor_tensor(out=c.x[:, b, :], in0=c.x[:, b, :], in1=c.row(finish), op=ALU.add)\
                        .then_inc(bias_added, 1)

        @block.tensor
        def _(pe):
            pe.wait_ge(w1_low, 1)
            with pe.Fori(0, groups // 2) as i:
                for p in range(2):
                    g = i * 2 + p
                    pe.wait_ge(n_low, g + 1)
                    for f in range(ft):
                        bank = up[f % ups]
                        pe.wait_ge(bank.free, bank.nth(g, f // ups))
                        for t in range(kt):
                            last = product(pe, bank.ap[:, :], [part[:, t, f * P:(f + 1) * P] for part in w1_parts],
                                           [part[:, p, t, :] for part in n_parts], start=(t == 0), stop=(t == kt - 1))
                        last.then_inc(bank.full, 1)
                    for bank in up:
                        pe.wait_ge(bank.free, bank.nth(g, bank.jobs - 1) + 1)
                    if channels:
                        bank = down[p]
                        pe.wait_ge(bank.free, i + 1)
                        for f in range(ft):
                            last = pe.matmul(bank.ap[:, :], w2[:, f, :], hT[:, p, f, :],
                                             start=(f == 0), stop=(f == ft - 1))
                        last.then_inc(bank.full, 1)
                    else:
                        for n in range(4):
                            bank = down[n]
                            pe.wait_ge(bank.free, g + 1)
                            for f in range(ft):
                                last = pe.matmul(bank.ap[:, 0:D], hT[:, p, f, n * P:(n + 1) * P], w2[:, f, :],
                                                 start=(f == 0), stop=(f == ft - 1))
                            last.then_inc(bank.full, 1)

        @block.scalar
        def _(act):
            act.activation(w1_parts[0][:, :, :], w1[:, :, :], ACT.Copy).then_inc(w1_high, 1)
            with act.Fori(0, groups // 2) as i:
                for p in range(2):
                    g = i * 2 + p
                    for f in range(ft):
                        bank = up[f % ups]
                        act.wait_ge(bank.full, bank.nth(g, f // ups))
                        act.activation(hT[:, p, f, :], bank.ap[:, :], func, bias=c.col(b1, f), scale=1.0)\
                            .then_inc(bank.free, 1)

        @block.vector
        def _(dve):
            def split_tokens(g, p):
                dve.tensor_copy(n_parts[0][:, p, :, :], tokens(g)).then_inc(n_high, 1)
                dve.wait_ge(n_high, g + 1)
                dve.memset(c.waiter[:, :], 0.0)
                dve.tensor_tensor(out=n_parts[1][:, p, :, :], in0=tokens(g), in1=n_parts[0][:, p, :, :].bitcast(F32),
                                  op=ALU.subtract).then_inc(n_low, 1)

            def add(g, i, p):
                if channels:
                    bank = down[p]
                    dve.wait_ge(bank.full, i + 1)
                    dve.scalar_tensor_tensor(out=c.x_flat[:, bass.ds(g * BANK, BANK)], in0=bank.ap[:, :],
                                             scalar=c.col("l0_b2", 0), in1=c.acc_flat[:, bass.ds(g * BANK, BANK)],
                                             op0=ALU.add, op1=ALU.add).then_inc(bank.free, 1)
                    return
                for n in range(4):
                    bank = down[n]
                    b = g * 4 + n
                    dve.wait_ge(bias_added, b + 1)
                    dve.wait_ge(bank.full, g + 1)
                    dve.tensor_tensor(out=c.x[:, b, :], in0=c.x[:, b, :], in1=bank.ap[:, 0:D], op=ALU.add)\
                        .then_inc(bank.free, 1)

            split_tokens(0, 0)
            dve.wait_ge(w1_high, 1)
            dve.tensor_tensor(out=w1_parts[1][:, :, :], in0=w1[:, :, :], in1=w1_parts[0][:, :, :].bitcast(F32),
                              op=ALU.subtract).then_inc(w1_low, 1)
            split_tokens(1, 1)
            with dve.Fori(0, groups // 2 - 1) as i:
                for p in range(2):
                    add(i * 2 + p, i, p)
                    split_tokens(i * 2 + p + 2, p)
            for p in range(2):
                add(groups - 2 + p, groups // 2 - 1, p)


class Narrow:

    def __init__(self, name, channel_tiles, queries, keys, head_dim, scale, lag, early_jobs, back_jobs, schedule):
        self.name = name
        self.ct = channel_tiles
        self.nq, self.nk, self.dh = queries, keys, head_dim
        self.scale = scale
        self.qt, self.kt = queries // P, keys // P
        self.heads_a_tile = H // channel_tiles
        self.hq, self.hk = BANK // queries, BANK // keys
        self.score_jobs = self.qt * H // self.hk
        self.turned_jobs = self.kt * H // self.hq
        self.lag = lag
        self.early_jobs = early_jobs
        self.back_jobs = back_jobs
        self.schedule = schedule.split()


LAYER0 = Narrow("l0", 1, 256, 256, 8, 8.0 ** -0.5, 1, 3, 6, """
    stream0 tail1 stream1 tail2 stream2 score0 stream3 begin0 score1 stream4 score2 score3 tail3 score4
    score5 tail4 begin1 stream5 score6 stream6 score7 begin2 stream7 tail5 stream8 score8 tail6 stream9
    score9 stream10 score10 stream11 score11 score12 stream12 score13 stream13 score14 score15 parts end
    stream14 stream15 turn early0 stream16 early1 early2 blocks""")
LAYER1 = Narrow("l1", 2, 128, 256, 16, 1.0 / 16, 1, 5, 4, """
    begin0 stream0 tail1 stream1 stream2 score0 tail2 stream3 score1 tail3 score2 stream4 score3 stream5
    score4 score5 stream6 score6 score7 end stream7 parts turn early0 stream8 tail4 early1 early2 early3
    early4 blocks""")
SCHEDULE3 = """
    masks stream0 begin0 score0 begin1 stream1 score1 begin2 score2 tail1 score3 stream2 tail2 stream3 parts
    end stream4 turn early0 tail3 stream5 early1 early2 blocks"""
LAYER3_SELF = Narrow("l3s", 2, 128, 128, 16, 1.0, 2, 3, 3, SCHEDULE3)
LAYER3_CROSS = Narrow("l3c", 2, 128, 128, 16, 1.0, 2, 3, 3, """
    tail1 begin0 masks stream0 begin1 stream1 score0 begin2 score1 score2 score3 stream2 tail2 parts stream3
    end turn tail3 early0 stream4 early1 stream5 blocks early2""")


def narrow_attention(c, z):
    nc = c.nc
    l0, l1 = z is LAYER0, z is LAYER1
    masked = z.name.startswith("l3")
    cross = z is LAYER3_CROSS
    with ExitStack() as ctx:
        def sb(n, shape, dt=F32):
            return ctx.enter_context(nc.sbuf_tensor(f"{z.name}_{n}", shape, dt))

        sems = []

        def sem(n):
            sems.append(ctx.enter_context(nc.semaphore(f"{z.name}_{n}")))
            return sems[-1]

        QK = sb("QK", [P, 2, z.ct * (z.nq + z.nk)])
        QT = [QK[:, p, 0:z.ct * z.nq].rearrange("p (t q) -> p t q", t=z.ct) for p in range(2)]
        KT = [QK[:, p, z.ct * z.nq:].rearrange("p (t k) -> p t k", t=z.ct) for p in range(2)]
        split = l0 or l1
        if split:
            QK_parts = [sb(f"QK_{n}", [P, 2, z.ct * (z.nq + z.nk)], F32R) for n in ("high", "low")]
            KT_parts = [[part[:, p, z.ct * z.nq:].rearrange("p (t k) -> p t k", t=z.ct) for part in QK_parts]
                        for p in range(2)]
            QT_parts = [[part[:, p, 0:z.ct * z.nq].rearrange("p (t q) -> p t q", t=z.ct) for part in QK_parts]
                        for p in range(2)]
            q_blocks_low = sb("q_blocks_low", [P, 2, H, z.nq], F32R)
        q_blocks = sb("q_blocks", [P, 2, H, z.nq], F32R if split else F32)
        V = sb("V", [P, 2, z.kt, H, SLOT])
        neg_max_T = sb("neg_max_T", [P, 2, z.nq], BF16)
        width = z.ct * P
        neg_max = sb("neg_max", [P, z.qt, H])
        neg_max_bf = sb("neg_max_bf", [P, z.qt, P], BF16)
        PT = sb("PT", [P, 3, BANK])
        ctx_den = sb("ctx_den", [P, 4, z.nq])
        rden = sb("rden", [P, z.qt, H, 1])
        ctx_q = sb("ctx_q", [P, z.qt, H, z.dh])
        ctx_T = sb("ctx_T", [P, z.ct, z.nq])
        per = 4 if l0 else 2
        x_T = sb("x_T", [P, per, 4 * P])
        if l0:
            x_in = sb("x_in", [P, 2, 4, P])
        else:
            res = sb("res", [P, 2, D])
        if l1:
            x_in = sb("x_in", [P, 2, D])
            mask_col = sb("mask_col", [P, B])
            mask_step = sb("mask_step", [P, 1])
            mask_row = sb("mask_row", [P, B, z.nk], BF16)
            mask_int = sb("mask_int", [P, B], I32)
            mask_row_int = sb("mask_row_int", [1, B, S], I32)
        else:
            stats = sb("stats", [P, 4, 6])
            mean_var = sb("mean_var", [P, 4, 2])
            rstd = sb("rstd", [P, 4, 1])
            xn = sb("xn", [P, 4, P])
        if l0 or l1:
            r = sb("r", [P, z.qt, width])
            rn = sb("rn", [P, z.qt, width])
            stats_b = sb("stats_b", [P, 2, 6])
            mean_var_b = sb("mean_var_b", [P, 2, 2])
            rstd_b = sb("rstd_b", [P, 2, 1])
        if l1 or cross:
            ctx_in = sb("ctx_in", [P, 2, 2, S])
        if masked:
            mask_in = sb("mask_in", [P, 2, 2, S])
            mask_mul = sb("mask_mul", [P, 2, 2, S])
            mask_add = sb("mask_add", [P, 2, 2, S])
            mask_left = sb("mask_left", [P, S])
            mask_parts = sb("mask_parts", [P, 2, 3, S], BF16)
            s_masked = sb("s_masked", [P, 2, BANK])
            s_biased = sb("s_biased", [P, 2, BANK])
            t_masked = sb("t_masked", [P, 3, BANK])
            t_shifted = sb("t_shifted", [P, 2, BANK])

        banks = [ctx.enter_context(nc.psum_tensor(f"{z.name}_psum{i}", [P, BANK], F32)) for i in range(8)]

        def group(at, what, n, jobs):
            return [Bank(banks[at + i], sem(f"{what}{i}_full"), sem(f"{what}{i}_free"), -(-(jobs - i) // n))
                    for i in range(n)]

        front = group(0, "front", 2, z.early_jobs + z.score_jobs + 1)
        turned = group(2, "turned", 2, z.turned_jobs)
        if masked:
            shifts = group(4, "shifts", 2, z.turned_jobs)
            context = group(6, "context", 1, 1)
            back = group(7, "back", 1, z.back_jobs)
        else:
            shifts = []
            context = [Bank(banks[4 + i], sem(f"context{i}_full"), sem(f"context{i}_free"), 1)
                       for i in range(2 if l0 else 1)]
            back = group(6, "back", 2, z.back_jobs)

        loaded = sem("loaded")
        set_up = sem("set_up")
        x_loaded = [sem(f"x_loaded{p}") for p in range(2)]
        mask_loaded = [sem(f"mask_loaded{p}") for p in range(2)]
        mask_made = sem("mask_made")
        mask_copied = sem("mask_copied")
        mask_row_ready = sem("mask_row_ready")
        x_ready = sem("x_ready")
        stats_done = sem("stats_done")
        var_done = sem("var_done")
        rstd_done = sem("rstd_done")
        rstd_part = sem("rstd_part")
        xn_done = sem("xn_done")
        scaled = sem("scaled")
        ln_done = sem("ln_done")
        res_ready = sem("res_ready")
        q_blocks_ready = [sem("q_blocks_ready"), sem("q_blocks_ready_pool")] if masked else [sem("q_blocks_ready")]
        low_ready = sem("low_ready")
        q_blocks_low_ready = sem("q_blocks_low_ready")
        s_ready = sem("s_ready")
        max_done = sem("max_done")
        probs_ready = sem("probs_ready")
        rden_done = sem("rden_done")
        stats_b_done = sem("stats_b_done")
        var_b_done = sem("var_b_done")
        rstd_b_part = sem("rstd_b_part")
        rstd_b_done = sem("rstd_b_done")
        rn_done = sem("rn_done")
        ctx.callback(clear_semaphores, nc, sems)
        block = ctx.enter_context(nc.Block())

        lag = z.lag

        def F(f):
            return front[f % 2], f // 2

        def K(m):
            return back[(m - 1) % len(back)], (m - 1) // len(back)

        def run(eng, stages):
            def period(early_step, score_step, stream_step, tail_step):
                for entry in z.schedule:
                    stage = entry.rstrip("0123456789")
                    step = {"begin": early_step, "early": early_step, "blocks": early_step,
                            "stream": stream_step, "tail": tail_step}.get(stage, score_step)
                    if stage in stages and step is not None:
                        stages[stage](step, int(entry[len(stage):] or 0))

            pipelined4(eng, B, per, period)

        N_JOB = z.early_jobs + z.score_jobs
        T, Q_JOB, K_JOB, V_JOBS = 0, (2 if l1 else 1), 1, ([3, 4] if l1 else [2])
        TURN = list(range(1, 1 + z.qt))
        CTX_T = z.qt + 1
        OUT = CTX_T + 1
        TAIL = list(range(OUT + 1, z.back_jobs + 1))

        MASK_OPS = 6

        def by_head(ap):
            return ap.rearrange("p (h s) -> p h s", h=4)

        def all_heads(ap):
            return ap.unsqueeze(1).to_broadcast([P, 4, S])

        def q_to_blocks(eng, b, t, done, blocks, q, before):
            eng.wait_ge(*before)
            for half in range(2):
                n = z.heads_a_tile // 2
                heads = slice(t * z.heads_a_tile + half * n, t * z.heads_a_tile + (half + 1) * n)
                shape = [P, n, z.nq]
                eng.tensor_tensor(out=blocks[:, b.k % 2, heads, :],
                                  in0=q[:, t, :].unsqueeze(1).to_broadcast(shape),
                                  in1=c.head_mask(z.dh)[:, heads].unsqueeze(2).to_broadcast(shape),
                                  op=ALU.mult).then_inc(done, 1)

        def q_evacuated(b):
            bk, k = F(Q_JOB)
            return bk.free, bk.nth(b.n, k) + 1

        @block.sync
        def _(sync):
            for bk in front + turned + shifts + context + back:
                sync.sem_inc(bk.free, 1)
            if l1:
                sync.dma_start(mask_int[:, :], c.dram["mask_T"]).then_inc(loaded, 16)
                sync.dma_start(mask_row_int[:, :, :], c.dram["mask"].rearrange("(a b) s -> a b s", a=1))\
                    .then_inc(loaded, 16)
            if masked and not cross:
                sync.dma_start(mask_in[:, 0, :, :], c.dram["self_mask"].rearrange("w p s -> p w s"))\
                    .then_inc(loaded, 16)

            def load(b, p):
                if l0:
                    sync.dma_start(x_in[:, p, 0:2, :], c.dram["x_T"][b].rearrange("(t p) s -> p t s", p=P))\
                        .then_inc(x_loaded[p], 16)
                    sync.dma_start(x_in[:, p, 2:4, :], c.dram["ctx_T"][b].rearrange("(t p) s -> p t s", p=P))\
                        .then_inc(x_loaded[p], 16)
                if l1 or cross:
                    sync.dma_start(ctx_in[:, p, :, :], c.dram["ctx_T"][b].rearrange("(t p) s -> p t s", p=P))\
                        .then_inc(x_loaded[p], 16)
                if cross:
                    sync.dma_start(mask_in[:, p, :, :], c.dram["cross_mask"][b].rearrange("w p s -> p w s"))\
                        .then_inc(mask_loaded[p], 16)

            if l0 or l1 or cross:
                for p in range(2):
                    load(p, p)
                if l0:
                    load_weights(sync, c, LAYER1_WEIGHTS, c.l1_loaded)
                with sync.Fori(1, B // 2) as i:
                    for p in range(2):
                        before = (i - 1) * 2 + p
                        if l0:
                            bk, k = F(T)
                            sync.wait_ge(bk.full, bk.nth(before, k))
                        else:
                            bk, k = F(V_JOBS[-1])
                            sync.wait_ge(bk.full, bk.nth(before, k))
                        if cross:
                            sync.wait_ge(mask_made, (before + 1) * MASK_OPS)
                        load(i * 2 + p, p)

        @block.gpsimd
        def _(pool):
            pool.memset(neg_max_bf[:, :, :], 0.0).then_inc(set_up, 1)
            pool.memset(V[:, :, :, :, :], 0.0).then_inc(set_up, 1)
            pool.wait_ge(set_up, 2)
            pool.memset(V[:, :, :, :, z.dh:z.dh + 1], 1.0).then_inc(set_up, 1)
            if l1:
                pool.wait_ge(set_up, 3)
                pool.wait_ge(loaded, 32)
                pool.tensor_scalar(out=mask_col[:, :], in0=mask_int[:, :], scalar1=0.0, scalar2=NEG,
                                   op0=ALU.is_equal, op1=ALU.mult).then_inc(set_up, 1)
                pool.wait_ge(set_up, 4)

            def make_masks(p, before):
                pool.tensor_tensor(out=mask_mul[:, p, :, :], in0=mask_in[:, p, :, :],
                                   in1=c.quarter[:, :].unsqueeze(2).to_broadcast([P, 2, S]), op=ALU.mult)\
                    .then_inc(mask_made, 1)
                pool.tensor_scalar(out=mask_add[:, p, :, :], in0=mask_in[:, p, :, :], scalar1=10000.0,
                                   scalar2=-10000.0, op0=ALU.mult, op1=ALU.add).then_inc(mask_made, 1)
                left, one = mask_left[:, :], c.one[:, :].to_broadcast([P, S])
                pool.wait_ge(mask_made, before + 2)
                pool.tensor_tensor(out=mask_parts[:, p, 0, :], in0=mask_add[:, p, 1, :], in1=one, op=ALU.mult)\
                    .then_inc(mask_made, 1)
                pool.wait_ge(mask_made, before + 3)
                pool.tensor_tensor(out=left, in0=mask_add[:, p, 1, :], in1=mask_parts[:, p, 0, :], op=ALU.subtract)\
                    .then_inc(mask_made, 1)
                pool.wait_ge(mask_made, before + 4)
                pool.tensor_tensor(out=mask_parts[:, p, 1, :], in0=left, in1=one, op=ALU.mult).then_inc(mask_made, 1)
                pool.wait_ge(mask_made, before + 5)
                pool.tensor_tensor(out=mask_parts[:, p, 2, :], in0=left, in1=mask_parts[:, p, 1, :],
                                   op=ALU.subtract).then_inc(mask_made, 1)

            if masked and not cross:
                pool.wait_ge(loaded, 16)
                make_masks(0, 0)

            def is_first(b):
                return isinstance(b.n, int) and b.n < 2

            def begin(b, part):
                p = b.k % 2
                first = is_first(b)
                if part == 0 and l0:
                    pool.wait_ge(x_loaded[p], (b.n - p) * 16 + 32)
                    x = x_in[:, p, :, :]
                    pool.tensor_tensor(out=x, in0=x, in1=c.pos[:, :, :], op=ALU.add).then_inc(x_ready, 1)
                if part == 0 and l1:
                    if not first:
                        bk, k = F(T)
                        pool.wait_ge(bk.full, b.times(bk.jobs, k + 1 - 2 * bk.jobs))
                        carry_wait_pool(pool, c)
                    pool.tensor_copy(x_in[:, p, :], c.x[:, b.n, :]).then_inc(x_ready, 1)
                if part == 1 and not l1:
                    pool.wait_ge(var_done, b.n + 1)
                    n = 4 if l0 else 1
                    inverse_root(pool, c, rstd_part, b.n, mean_var[:, 0:n, 1:2], rstd[:, 0:n, :], 1e-5, n)\
                        .then_inc(rstd_done, 1)
                if part == 2 and l0:
                    x = x_in[:, p, :, :].rearrange("p (s t) c -> p s t c", s=2)
                    n = xn[:, :, :].rearrange("p (s t) c -> p s t c", s=2)
                    pool.wait_ge(xn_done, b.n + 1)
                    pool.tensor_tensor(out=x, in0=n, in1=c.pair("l0_q_g"), op=ALU.mult).then_inc(scaled, 1)
                    pool.wait_ge(scaled, b.n + 1)
                    pool.tensor_tensor(out=x, in0=x, in1=c.pair("l0_q_b"), op=ALU.add).then_inc(ln_done, 1)

            def end(b, _):
                p = b.k % 2
                first = is_first(b)
                if l0:
                    return
                if not first:
                    bk, k = K(OUT)
                    pool.wait_ge(bk.free, b.times(bk.jobs, k + 2 - 2 * bk.jobs))
                    carry_wait_pool(pool, c)
                pool.tensor_tensor(out=res[:, p, :], in0=c.x[:, b.n, :], in1=c.row(
                    "l1_out_b" if l1 else "l3_co_b" if cross else "l3_ao_b"), op=ALU.add).then_inc(res_ready, 1)

            def masks(b, _):
                p = b.k % 2
                if cross:
                    pool.wait_ge(mask_loaded[p], (b.n - p) * 8 + 16)
                    if not is_first(b):
                        bk = shifts[-1]
                        pool.wait_ge(bk.free, b.times(bk.jobs, 1 - bk.jobs))
                    make_masks(p, b.times(MASK_OPS, 0))

            def blocks(b, _):
                p = b.k % 2
                if masked:
                    q_to_blocks(pool, b, 1, q_blocks_ready[1], q_blocks, QT[p], q_evacuated(b))
                    return
                pool.wait_ge(*q_evacuated(b))
                pool.tensor_tensor(out=QK_parts[1][:, p, :], in0=QK[:, p, :], in1=QK_parts[0][:, p, :].bitcast(F32),
                                   op=ALU.subtract).then_inc(low_ready, 1)
                for t in range(z.ct):
                    q_to_blocks(pool, b, t, q_blocks_low_ready, q_blocks_low, QT_parts[p][1].bitcast(F32),
                                (low_ready, b.n + 1))

            def score(b, j):
                if masked:
                    bk, k = F(z.early_jobs + j)
                    pool.wait_ge(bk.free, bk.nth(b.n, k) + 1)
                    p = b.k % 2 if cross else 0
                    pool.tensor_tensor(out=by_head(s_biased[:, j % 2, :]), in0=by_head(s_masked[:, j % 2, :]),
                                       in1=all_heads(mask_add[:, p, 0, :]), op=ALU.add).then_inc(s_ready, 1)

            def tail(b, m):
                if TAIL and m == OUT:
                    pool.wait_ge(var_b_done, b.n + 1)
                    n = z.qt
                    inverse_root(pool, c, rstd_b_part, b.n, mean_var_b[:, 0:n, 1:2], rstd_b[:, 0:n, :],
                                 1e-5 if l0 else 1e-6, n).then_inc(rstd_b_done, 1)

            run(pool, {"begin": begin, "blocks": blocks, "masks": masks, "score": score, "end": end, "tail": tail})

        @block.tensor
        def _(pe):
            pe.wait_ge(set_up, 4 if l1 else 3)
            if l1:
                pe.wait_ge(c.l1_loaded, 16 * len(LAYER1_WEIGHTS))
            if masked and not cross:
                pe.wait_ge(c.l3_loaded, 16 * len(WEIGHTS_3))

            def early(b, f):
                p = b.k % 2
                bk, k = F(f)
                out = bk.ap
                if f == T:
                    if l1:
                        pe.wait_ge(x_ready, b.n + 1)
                    elif l0:
                        pe.wait_ge(ln_done, b.n + 1)
                    else:
                        pe.wait_ge(xn_done, b.n + 1)
                    pe.wait_ge(bk.free, bk.nth(b.n, k))
                    for t in range(4 if l0 else 2):
                        src = x_in[:, p, t, :] if l0 else x_in[:, p, t * P:(t + 1) * P] if l1 else xn[:, t, :]
                        last = pe.transpose(out[:, t * P:(t + 1) * P], src, c.ident[:, :])
                    last.then_inc(bk.full, 1)
                    return
                tk, t0 = F(T)
                pe.wait_ge(tk.free, tk.nth(b.n, t0) + 1)
                if l1 or cross:
                    pe.wait_ge(x_loaded[p], (b.n - p) * 8 + 16)
                pe.wait_ge(bk.free, bk.nth(b.n, k))
                tokens = x_T[:, b.k % per, :]
                own = tokens[:, 0:2 * P].rearrange("p (t s) -> p t s", t=2)
                w = c.w
                if l0:
                    if f == K_JOB:
                        pe.matmul(out[:, 0:256], w["l0_wq"][:, 0, :], tokens[:, 0:256], start=True, stop=True)
                        last = pe.matmul(out[:, 256:512], w["l0_wk"][:, 0, :], tokens[:, 256:512], start=True, stop=True)
                    else:
                        for t in range(2):
                            last = pe.matmul(out[:, t * P:(t + 1) * P], tokens[:, (2 + t) * P:(3 + t) * P],
                                             w["l0_wv"][:, 0, :], start=True, stop=True)
                elif l1:
                    other = ctx_in[:, p, :, :]
                    if f == K_JOB:
                        for m in range(2):
                            for half, src in enumerate((other, own)):
                                for t in range(2):
                                    last = pe.matmul(out[:, m * 256 + half * P:m * 256 + (half + 1) * P],
                                                     w["l1_wk"][:, t, m * P:(m + 1) * P], src[:, t, :],
                                                     start=(t == 0), stop=(t == 1))
                    elif f == Q_JOB:
                        for m in range(2):
                            for t in range(2):
                                last = pe.matmul(out[:, m * P:(m + 1) * P], w["l1_wq"][:, t, m * P:(m + 1) * P],
                                                 own[:, t, :], start=(t == 0), stop=(t == 1))
                    else:
                        src = (other, own)[f - V_JOBS[0]]
                        for t in range(2):
                            last = pe.matmul(out[:, 0:D], src[:, t, :], w["l1_wv"][:, t, :],
                                             start=(t == 0), stop=(t == 1))
                else:
                    other = ctx_in[:, p, :, :] if cross else own
                    wq, wk, wv = (w["l3_wqc"], w["l3_wkc"], w["l3_wvc"]) if cross else (w["l3_wq"], w["l3_wk"], w["l3_wv"])
                    if f == K_JOB:
                        for j, (wt, src) in enumerate(((wq, own), (wk, other))):
                            for m in range(2):
                                for t in range(2):
                                    last = pe.matmul(out[:, (2 * j + m) * P:(2 * j + m + 1) * P],
                                                     wt[:, t, m * P:(m + 1) * P], src[:, t, :],
                                                     start=(t == 0), stop=(t == 1))
                    else:
                        for t in range(2):
                            last = pe.matmul(out[:, 0:D], other[:, t, :], wv[:, t, :], start=(t == 0), stop=(t == 1))
                last.then_inc(bk.full, 1)

            def score(b, j):
                per_tile = H // z.hk
                q, h = j // per_tile, j % per_tile * z.hk
                p = b.k % 2
                if j == 0:
                    kb, kk = F(K_JOB)
                    pe.wait_ge(kb.free, kb.nth(b.n, kk) + 1)
                part = H // (2 * z.ct)
                if q == 0 and h % part == 0:
                    t, half = h // z.heads_a_tile, h % z.heads_a_tile // part
                    if masked:
                        pe.wait_ge(q_blocks_ready[t], b.times(2, 1 + half))
                    else:
                        pe.wait_ge(q_blocks_ready[0], b.times(2 * z.ct, 1 + 2 * t + half))
                bk, k = F(z.early_jobs + j)
                pe.wait_ge(bk.free, bk.nth(b.n, k))
                t = h // z.heads_a_tile
                for i in range(z.hk):
                    last = pe.matmul(bk.ap[:, i * z.nk:(i + 1) * z.nk],
                                     upper_half(q_blocks[:, p, h + i, q * P:(q + 1) * P]), upper_half(KT[p][:, t, :]),
                                     start=True, stop=True)
                if l1:
                    pe.wait_ge(mask_row_ready, 2)
                    last = pe.matmul(bk.ap[:, :], c.ones_bf[:, :],
                                     mask_row[:, b.n, :].unsqueeze(1).to_broadcast([P, z.hk, z.nk]),
                                     start=False, stop=True, skip_group_check=True)
                last.then_inc(bk.full, 1)

            def turn(b, _):
                bk, k = F(N_JOB)
                pe.wait_ge(max_done, b.times(3, 3))
                pe.wait_ge(bk.free, bk.nth(b.n, k))
                for q in range(z.qt):
                    last = pe.transpose(bk.ap[:, :].bitcast(BF16)[:, q * P:(q + 1) * P], neg_max_bf[:, q, :],
                                        c.ident_bf[:, :])
                last.then_inc(bk.full, 1)

            def stream(b, n):
                p = b.k % 2
                if n == 0:
                    bk, k = F(N_JOB)
                    pe.wait_ge(bk.free, bk.nth(b.n, k) + 1)
                    for job in V_JOBS:
                        bk, k = F(job)
                        pe.wait_ge(bk.free, bk.nth(b.n, k) + 1)
                    if split:
                        pe.wait_ge(q_blocks_low_ready, b.times(2 * z.ct, 2 * z.ct))
                    if masked:
                        pe.wait_ge(mask_made, b.times(MASK_OPS, MASK_OPS) if cross else MASK_OPS)
                if n < z.turned_jobs:
                    chunk, kt = n // z.kt, n % z.kt
                    h = chunk * z.hq
                    t = h // z.heads_a_tile
                    bk, k = turned[n % 2], n // 2
                    pe.wait_ge(bk.free, bk.nth(b.n, k))
                    keys = slice(kt * P, (kt + 1) * P)
                    if split:
                        last = product(pe, bk.ap[:, :], [part[:, t, keys] for part in KT_parts[p]],
                                       [part[:, p, h:h + z.hq, :] for part in (q_blocks, q_blocks_low)],
                                       start=True, stop=True)
                    else:
                        last = pe.matmul(bk.ap[:, :], KT[p][:, t, keys], q_blocks[:, p, h:h + z.hq, :],
                                         start=True, stop=True)
                    if masked:
                        last.then_inc(bk.full, 1)
                        bk = shifts[n % 2]
                        pe.wait_ge(bk.free, bk.nth(b.n, k))
                        for part in range(3):
                            pe.matmul(bk.ap[:, :], c.ident_bf[:, :],
                                      all_heads(mask_parts[:, p if cross else 0, part, :]),
                                      start=(part == 0), stop=True, skip_group_check=(part > 0))
                    for i in range(z.hq):
                        last = pe.matmul(bk.ap[:, i * z.nq:(i + 1) * z.nq],
                                         c.select16[:, h + i:h + i + 1].to_broadcast([P, P]), neg_max_T[:, p, :],
                                         start=False, stop=True, skip_group_check=True)
                    last.then_inc(bk.full, 1)
                if n >= lag:
                    m = n - lag
                    chunk, kt = m // z.kt, m % z.kt
                    pe.wait_ge(probs_ready, b.times(z.turned_jobs, m + 1))
                    for i in range(z.hq):
                        h = chunk * z.hq + i
                        g, j = h // 4, h % 4
                        cb, at = g * z.nq // BANK, g * z.nq % BANK
                        if kt == 0 and j == 0 and at == 0:
                            pe.wait_ge(context[cb].free, b.n + 1)
                        last = pe.matmul(context[cb].ap[j * SLOT:(j + 1) * SLOT, at:at + z.nq], V[:, p, kt, h, :],
                                         PT[:, m % 3, i * z.nq:(i + 1) * z.nq],
                                         start=(kt == 0), stop=(kt == z.kt - 1))
                    if kt == z.kt - 1 and (h + 1) * z.nq % (4 * BANK) == 0:
                        last.then_inc(context[cb].full, 1)

            def tail(b, m):
                bk, k = K(m)
                out = bk.ap
                if m in TURN:
                    if m == TURN[0]:
                        for cb in context:
                            pe.wait_ge(cb.free, b.n + 2)
                    pe.wait_ge(bk.free, bk.nth(b.n, k))
                    q = m - TURN[0]
                    for g in range(4):
                        last = pe.transpose(out[:, g * P:(g + 1) * P], ctx_den[:, g, q * P:(q + 1) * P], c.ident[:, :])
                elif m == CTX_T:
                    for j in TURN:
                        tb, tk = K(j)
                        pe.wait_ge(tb.free, tb.nth(b.n, tk) + 1)
                    pe.wait_ge(bk.free, bk.nth(b.n, k))
                    flat = ctx_q[:, :, :, :].rearrange("p q h d -> p q (h d)")
                    for i in range(2):
                        src = flat[:, i, :] if l0 else flat[:, 0, i * P:(i + 1) * P]
                        last = pe.transpose(out[:, i * P:(i + 1) * P], src, c.ident[:, :])
                elif m == OUT:
                    tb, tk = K(CTX_T)
                    pe.wait_ge(tb.free, tb.nth(b.n, tk) + 1)
                    pe.wait_ge(bk.free, bk.nth(b.n, k))
                    wo = c.w["l0_wo" if l0 else "l1_wo" if l1 else "l3_wco" if cross else "l3_wao"]
                    for q in range(z.qt):
                        for t in range(z.ct):
                            last = pe.matmul(out[:, q * width:(q + 1) * width], ctx_T[:, t, q * P:(q + 1) * P],
                                             wo[:, t, :], start=(t == 0), stop=(t == z.ct - 1 and not l0))
                        if l0:
                            last = pe.matmul(out[:, q * P:(q + 1) * P], x_T[:, b.k % per, q * P:(q + 1) * P],
                                             c.ident[:, :], start=False, stop=True)
                else:
                    src = r
                    if m == TAIL[-1]:
                        pe.wait_ge(rn_done, b.n + 1)
                        src = rn
                    else:
                        ob, ok = K(OUT)
                        pe.wait_ge(ob.free, ob.nth(b.n, ok) + 1)
                    pe.wait_ge(bk.free, bk.nth(b.n, k))
                    flat = src[:, :, :].rearrange("p q c -> p (q c)")
                    for i in range(2):
                        last = pe.transpose(out[:, i * P:(i + 1) * P], flat[:, i * P:(i + 1) * P], c.ident[:, :])
                last.then_inc(bk.full, 1)

            run(pe, {"early": early, "score": score, "turn": turn, "stream": stream, "tail": tail})

        @block.scalar
        def _(act):
            act.wait_ge(set_up, 4 if l1 else 3)

            def early(b, f):
                p = b.k % 2
                bk, k = F(f)
                if f in V_JOBS:
                    return
                act.wait_ge(bk.full, bk.nth(b.n, k))
                if f == T:
                    if masked:
                        g, be = ("l3_ln2_g", "l3_ln2_b") if cross else ("l3_ln1_g", "l3_ln1_b")
                        for t in range(2):
                            last = act.activation(x_T[:, b.k % per, t * P:(t + 1) * P], bk.ap[:, t * P:(t + 1) * P], ACT.Identity,
                                                  bias=c.col(be, t), scale=c.col(g, t))
                    else:
                        n = 4 if l0 else 2
                        last = act.activation(x_T[:, b.k % per, 0:n * P], bk.ap[:, 0:n * P], ACT.Copy)
                elif l0:
                    act.activation(QK_parts[0][:, p, :], bk.ap[:, :], ACT.Copy)
                    last = act.activation(QK[:, p, :], bk.ap[:, :], ACT.Copy)
                elif l1:
                    dst, name = (QT[p], "l1_q_b") if f == Q_JOB else (KT[p], "l1_k_b")
                    high = (QT_parts if f == Q_JOB else KT_parts)[p][0]
                    n = z.nq if f == Q_JOB else z.nk
                    for t in range(2):
                        act.activation(high[:, t, :], bk.ap[:, t * n:(t + 1) * n], ACT.Identity,
                                       bias=c.col(name, t), scale=1.0)
                        last = act.activation(dst[:, t, :], bk.ap[:, t * n:(t + 1) * n], ACT.Identity,
                                              bias=c.col(name, t), scale=1.0)
                else:
                    for j, (dst, name) in enumerate(((QT[p], "l3_q_b"), (KT[p], "l3_k_b"))):
                        at = 2 * P * j
                        for t in range(2):
                            last = act.activation(dst[:, t, :], bk.ap[:, at + t * P:at + (t + 1) * P],
                                                  ACT.Identity, bias=c.col(name + ("2" if cross else "1"), t), scale=1.0)
                last.then_inc(bk.free, 1)

            def stream(b, n):
                if masked:
                    n -= 1
                if n not in range(z.turned_jobs):
                    return
                if l1 and n == 0:
                    act.activation(mask_step[:, :], mask_col[:, bass.ds(b.n, 1)], ACT.Copy).then_inc(mask_copied, 1)
                    act.wait_ge(mask_copied, b.n + 1)
                if masked:
                    act.wait_ge(shifts[n % 2].free, shifts[n % 2].nth(b.n, n // 2) + 1)
                    act.activation(PT[:, n % 3, :], t_shifted[:, n % 2, :], ACT.Exp).then_inc(probs_ready, 1)
                    return
                bk, k = turned[n % 2], n // 2
                act.wait_ge(bk.full, bk.nth(b.n, k))
                bias = mask_step[:, :] if l1 and n % z.kt == 0 else 0.0
                act.activation(PT[:, n % 3, :], bk.ap[:, :], ACT.Exp, bias=bias, scale=z.scale).then_inc(probs_ready, 1)
                act.wait_ge(probs_ready, b.times(z.turned_jobs, n + 1))
                act.sem_inc(bk.free, 1)

            def tail(b, m):
                bk, k = K(m)
                if m in TURN or m == OUT:
                    return
                act.wait_ge(bk.full, bk.nth(b.n, k))
                if m == CTX_T:
                    if l0:
                        last = act.activation(ctx_T[:, 0, :], bk.ap[:, 0:z.nq], ACT.Copy)
                    else:
                        name = "l1_v_b" if l1 else "l3_v_b2" if cross else "l3_v_b1"
                        for t in range(2):
                            last = act.activation(ctx_T[:, t, :], bk.ap[:, t * P:(t + 1) * P], ACT.Identity,
                                                  bias=c.col(name, t), scale=1.0)
                elif l0:
                    carry_wait(act, c)
                    if m == TAIL[-1]:
                        last = act.activation(c.nT_flat[:, bass.ds(b.n * 256, 256)], bk.ap[:, 0:256], ACT.Identity,
                                              bias=c.col("l0_ffn_b", 0), scale=c.col("l0_ffn_g", 0))
                    else:
                        last = act.activation(c.acc_flat[:, bass.ds(b.n * 256, 256)], bk.ap[:, 0:256], ACT.Copy)
                else:
                    carry_wait(act, c)
                    for t in range(2):
                        last = act.activation(c.nT[:, t, b.n, :], bk.ap[:, t * P:(t + 1) * P], ACT.Copy,
                                              scale=c.col("l1_post", t))
                last.then_inc(bk.free, 1)

            run(act, {"early": early, "stream": stream, "tail": tail})

        @block.vector
        def _(dve):
            if l1:
                dve.memset(mask_row[:, :, :], 0.0).then_inc(mask_row_ready, 1)
                dve.wait_ge(mask_row_ready, 1)
                dve.wait_ge(loaded, 32)
                dve.tensor_scalar(out=mask_row[0:1, :, 0:S], in0=mask_row_int[:, :, :], scalar1=0.0, scalar2=NEG,
                                  op0=ALU.is_equal, op1=ALU.mult).then_inc(mask_row_ready, 1)
            dve.wait_ge(set_up, 4 if l1 else 3)

            def begin(b, part):
                if l1:
                    return
                p = b.k % 2
                tiles = [x_in[:, p, t, :] for t in range(4)] if l0 else [c.x[:, b.n, :]]
                if part == 1:
                    if l0:
                        dve.wait_ge(x_ready, b.n + 1)
                    for t, x in enumerate(tiles):
                        last = dve.bn_stats(stats[:, t, :], x)
                    last.then_inc(stats_done, 1)
                    dve.wait_ge(stats_done, b.n + 1)
                    dve.memset(c.waiter[:, :], 0.0)
                    for t in range(len(tiles)):
                        last = dve.bn_aggr(mean_var[:, t, :], stats[:, t, :])
                    last.then_inc(var_done, 1)
                if part == 2:
                    dve.wait_ge(rstd_done, b.n + 1)
                    for t, x in enumerate(tiles):
                        out = xn[:, t, :] if l0 else xn[:, 0:2, :].rearrange("p t c -> p (t c)")
                        last = dve.tensor_scalar(out=out, in0=x, scalar1=mean_var[:, t, 0:1], scalar2=rstd[:, t, :],
                                                 op0=ALU.subtract, op1=ALU.mult)
                    last.then_inc(xn_done, 1)

            def early(b, f):
                p = b.k % 2
                if f not in V_JOBS:
                    return
                bk, k = F(f)
                dve.wait_ge(bk.full, bk.nth(b.n, k))
                for t in range(2 if l0 else 1):
                    kt = t if l0 else f - V_JOBS[0]
                    src = bk.ap[:, t * width:(t + 1) * width].rearrange("p (h d) -> p h d", h=H)
                    last = dve.tensor_copy(V[:, p, kt, :, 0:z.dh], src)
                last.then_inc(bk.free, 1)

            def blocks(b, _):
                p = b.k % 2
                q = QT_parts[p][0].bitcast(F32) if split else QT[p]
                for t in range(1 if masked else z.ct):
                    q_to_blocks(dve, b, t, q_blocks_ready[0], q_blocks, q, q_evacuated(b))

            def maximum(b, j, src):
                per_tile = H // z.hk
                q, h = j // per_tile, j % per_tile * z.hk
                return dve.tensor_reduce(neg_max[:, q, h:h + z.hk], src.rearrange("p (h k) -> p h k", h=z.hk), AX,
                                         ALU.max, negate=True)

            def score(b, j):
                bk, k = F(z.early_jobs + j)
                dve.wait_ge(bk.full, bk.nth(b.n, k))
                if not masked:
                    maximum(b, j, bk.ap[:, :]).then_inc(bk.free, 1)
                    return
                p = b.k % 2 if cross else 0
                if cross:
                    dve.wait_ge(mask_made, b.times(MASK_OPS, MASK_OPS))
                dve.tensor_tensor(out=by_head(s_masked[:, j % 2, :]), in0=by_head(bk.ap[:, :]),
                                  in1=all_heads(mask_mul[:, p, 0, :]), op=ALU.mult).then_inc(bk.free, 1)
                if j > 0:
                    dve.wait_ge(s_ready, b.times(4, j))
                    maximum(b, j - 1, s_biased[:, (j - 1) % 2, :])

            def parts(b, _):
                if masked:
                    dve.wait_ge(s_ready, b.times(4, 4))
                    maximum(b, 3, s_biased[:, 1, :]).then_inc(max_done, 1)
                    dve.wait_ge(max_done, b.times(3, 1))
                else:
                    for j in (z.score_jobs - 2, z.score_jobs - 1):
                        bk, k = F(z.early_jobs + j)
                        dve.wait_ge(bk.free, bk.nth(b.n, k) + 1)
                    dve.sem_inc(max_done, 1)
                dve.tensor_copy(neg_max_bf[:, :, 0:H], neg_max[:, :, :]).then_inc(max_done, 1)
                dve.wait_ge(max_done, b.times(3, 2))
                dve.tensor_tensor(out=neg_max_bf[:, :, H:2 * H], in0=neg_max[:, :, :], in1=neg_max_bf[:, :, 0:H],
                                  op=ALU.subtract).then_inc(max_done, 1)

            def turn(b, _):
                bk, k = F(N_JOB)
                dve.wait_ge(bk.full, bk.nth(b.n, k))
                dve.tensor_copy(neg_max_T[:, b.k % 2, :], bk.ap[:, :].bitcast(BF16)[:, 0:z.nq]).then_inc(bk.free, 1)

            def shift(b, n):
                bk, k = shifts[n % 2], n // 2
                dve.wait_ge(bk.full, bk.nth(b.n, k))
                tb = turned[n % 2]
                dve.wait_ge(tb.free, tb.nth(b.n, k) + 1)
                if n >= 2:
                    dve.wait_ge(probs_ready, b.times(4, n - 1))
                dve.tensor_tensor(out=t_shifted[:, n % 2, :], in0=t_masked[:, n % 3, :], in1=bk.ap[:, :],
                                  op=ALU.add).then_inc(bk.free, 1)

            def stream(b, n):
                if masked:
                    if n < z.turned_jobs:
                        p = b.k % 2 if cross else 0
                        bk, k = turned[n % 2], n // 2
                        dve.wait_ge(bk.full, bk.nth(b.n, k))
                        dve.tensor_tensor(out=by_head(t_masked[:, n % 3, :]), in0=by_head(bk.ap[:, :]),
                                          in1=all_heads(mask_mul[:, p, 1, :]), op=ALU.mult).then_inc(bk.free, 1)
                    if 1 <= n <= z.turned_jobs:
                        shift(b, n - 1)
                for i, cb in enumerate(context):
                    if n == (z.turned_jobs * (i + 1)) // len(context) + lag - 1:
                        dve.wait_ge(cb.full, b.n + 1)
                        per = 4 // len(context)
                        dve.tensor_copy(ctx_den[:, i * per:(i + 1) * per, :].rearrange("p g q -> p (g q)"),
                                        cb.ap[:, 0:per * z.nq]).then_inc(cb.free, 1)

            def tail(b, m):
                p = b.k % 2
                bk, k = K(m)
                if m in TURN:
                    q = m - TURN[0]
                    dve.wait_ge(bk.full, bk.nth(b.n, k))
                    slots = bk.ap[:, :].rearrange("p (h s) -> p h s", h=H)
                    dve.reciprocal(rden[:, q, :, :], slots[:, :, z.dh:z.dh + 1]).then_inc(rden_done, 1)
                    dve.wait_ge(rden_done, b.times(z.qt, q + 1))
                    dve.tensor_tensor(out=ctx_q[:, q, :, :], in0=slots[:, :, 0:z.dh],
                                      in1=rden[:, q, :, :].to_broadcast([P, H, z.dh]), op=ALU.mult).then_inc(bk.free, 1)
                elif m == OUT:
                    dve.wait_ge(bk.full, bk.nth(b.n, k))
                    if not l0:
                        dve.wait_ge(res_ready, b.n + 1)
                    if masked:
                        dve.tensor_tensor(out=c.x[:, b.n, :], in0=res[:, p, :], in1=bk.ap[:, 0:D], op=ALU.add)\
                            .then_inc(bk.free, 1)
                        return
                    flat = r[:, :, :].rearrange("p q c -> p (q c)")
                    if l0:
                        dve.tensor_copy(flat, bk.ap[:, 0:256]).then_inc(bk.free, 1)
                    else:
                        dve.tensor_tensor(out=flat, in0=res[:, p, :], in1=bk.ap[:, 0:256], op=ALU.add)\
                            .then_inc(bk.free, 1)
                    dve.wait_ge(bk.free, bk.nth(b.n, k) + 1)
                    if l0:
                        for q in range(z.qt):
                            last = dve.bn_stats(stats_b[:, q, :], r[:, q, :])
                        last.then_inc(stats_b_done, 1)
                        dve.wait_ge(stats_b_done, b.n + 1)
                        dve.memset(c.waiter[:, :], 0.0)
                        for q in range(z.qt):
                            last = dve.bn_aggr(mean_var_b[:, q, :], stats_b[:, q, :])
                        last.then_inc(var_b_done, 1)
                        dve.wait_ge(rstd_b_done, b.n + 1)
                        for q in range(z.qt):
                            last = dve.tensor_scalar(out=rn[:, q, :], in0=r[:, q, :], scalar1=mean_var_b[:, q, 0:1],
                                                     scalar2=rstd_b[:, q, :], op0=ALU.subtract, op1=ALU.mult)
                        last.then_inc(rn_done, 1)
                    else:
                        dve.tensor_tensor_reduce(out=rn[:, 0, :], in0=r[:, 0, :], in1=r[:, 0, :], scale=1.0 / D,
                                                 scalar=0.0, op0=ALU.mult, op1=ALU.add,
                                                 accum_out=mean_var_b[:, 0, 1:2]).then_inc(var_b_done, 1)
                        dve.wait_ge(rstd_b_done, b.n + 1)
                        dve.tensor_scalar(out=rn[:, 0, :], in0=r[:, 0, :], scalar1=rstd_b[:, 0, :], scalar2=None,
                                          op0=ALU.mult).then_inc(rn_done, 1)

            run(dve, {"begin": begin, "early": early, "blocks": blocks, "score": score, "parts": parts,
                                          "turn": turn, "stream": stream, "tail": tail})


def wide_heads(c, a):
    nc = c.nc
    G = 4
    T = G * S
    scale = float(P) ** -0.5
    steps = H * G
    with ExitStack() as ctx:
        def sb(n, shape, dt=F32):
            return ctx.enter_context(nc.sbuf_tensor(f"l2h{a}_{n}", shape, dt))

        sems = []

        def sem(n):
            sems.append(ctx.enter_context(nc.semaphore(f"l2h{a}_{n}")))
            return sems[-1]

        weights = sb("weights", [P, 2, 4, D])
        QT = sb("QT", [P, 2, T])
        KT = sb("KT", [P, 2, T])
        V = sb("V", [P, 2, G, P + 1])
        max_s = sb("max_s", [P, G])
        max_all = sb("max_all", [P, G])
        shift = sb("shift", [P, P], BF16)
        extra_arg = sb("extra_arg", [P, 2, G])
        extra_prob = sb("extra_prob", [P, 2, G])
        shift_T = sb("shift_T", [P, 2, P], BF16)
        PT = sb("PT", [P, T])
        den = sb("den", [P, G])
        rden = sb("rden", [P, G])
        ctx_q = sb("ctx_q", [P, G, P])
        ctx_T = sb("ctx_T", [P, T])
        w_parts = [sb(f"w_{n}", [P, 2, 3, D], F32R) for n in ("high", "low")]
        ctx_T_parts = [sb(f"ctx_T_{n}", [P, T], F32R) for n in ("high", "low")]
        head_vectors = sb("head_vectors", [P, 2, 4, 1])
        banks = [ctx.enter_context(nc.psum_tensor(f"l2h{a}_psum{i}", [P, BANK], F32)) for i in range(8)]

        def bank(n, what, jobs):
            return Bank(banks[n], sem(f"{what}_full"), sem(f"{what}_free"), jobs)

        q_bank = bank(0, "q", 1)
        k_bank = bank(1, "k", 1)
        v_bank = bank(2, "v", 1)
        s_bank = bank(3, "s", 2)
        t_bank = bank(4, "t", 1)
        pv_bank = [bank(5, "pv0", 2), bank(6, "pv1", 1)]
        o_bank = [bank(7, "o0", 1), bank(0, "o1", 1)]

        weights_loaded = [sem(f"weights_loaded{p}") for p in range(2)]
        set_up = sem("set_up")
        max_done = sem("max_done")
        extra_ready = sem("extra_ready")
        vectors_ready = sem("vectors_ready")
        high_ready = sem("high_ready")
        low_ready = sem("low_ready")
        ctx_low_ready = sem("ctx_low_ready")
        probs_ready = sem("probs_ready")
        den_done = sem("den_done")
        ctx.callback(clear_semaphores, nc, sems)
        block = ctx.enter_context(nc.Block())
        OPS = 6

        def head(s):
            return s.i * 2 + s.k // G

        @block.sync
        def _(sync):
            for bk in [q_bank, k_bank, v_bank, s_bank, t_bank, o_bank[0]] + pv_bank:
                sync.sem_inc(bk.free, 1)
            sync.sem_inc(o_bank[1].free, 3)

            def load(h, p):
                sync.dma_start(weights[:, p, :, :], c.dram[f"l2_heads{a}"][h].rearrange("w p n -> p w n"))\
                    .then_inc(weights_loaded[p], 16)

            for p in range(2):
                load(p, p)
            with sync.Fori(1, H // 2) as i:
                for p in range(2):
                    sync.wait_ge(o_bank[1].full, ((i - 1) * 2 + p + 1) * G)
                    load(i * 2 + p, p)

        @block.gpsimd
        def _(pool):
            pool.memset(shift[:, :], 0.0).then_inc(set_up, 1)
            pool.memset(V[:, :, :, P:P + 1], 1.0).then_inc(set_up, 1)

            def split_weights(h, i, p):
                pool.wait_ge(weights_loaded[p], i * 16 + 16)
                for at, which in ((slice(0, 2), slice(0, 2)), (slice(2, 3), slice(3, 4))):
                    raw, high = weights[:, p, which, :], w_parts[0][:, p, at, :]
                    one = c.one[:, :].unsqueeze(2).to_broadcast([P, at.stop - at.start, D])
                    pool.tensor_tensor(out=high, in0=raw, in1=one, op=ALU.mult).then_inc(high_ready, 1)
                pool.wait_ge(high_ready, h * 2 + 2)
                for at, which in ((slice(0, 2), slice(0, 2)), (slice(2, 3), slice(3, 4))):
                    raw, high = weights[:, p, which, :], w_parts[0][:, p, at, :]
                    pool.tensor_tensor(out=w_parts[1][:, p, at, :], in0=raw, in1=high.bitcast(F32), op=ALU.subtract)\
                        .then_inc(low_ready, 1)

            split_weights(0, 0, 0)

            def period(fr, _, bk):
                if bk is not None:
                    pool.wait_ge(pv_bank[0].free, pv_bank[0].nth(bk.n, 1) + 1)
                    pool.tensor_tensor(out=ctx_T_parts[1][:, :], in0=ctx_T[:, :],
                                       in1=ctx_T_parts[0][:, :].bitcast(F32), op=ALU.subtract)\
                        .then_inc(ctx_low_ready, 1)
                if fr is not None and fr.k % G == G - 1 and not (isinstance(fr.n, int) and fr.n == steps - 1):
                    ahead = fr.k // G + 1
                    split_weights(fr.i * 2 + ahead, fr.i + ahead // 2, ahead % 2)

            pipelined3(pool, steps, 8, period)

        @block.tensor
        def _(pe):
            pe.wait_ge(set_up, 2)

            def front_w(s, which):
                return weights[:, (s.k // G) % 2, which, :].rearrange("p (t n) -> p t n", t=2)

            def q_or_k(s, which):
                if which == 0 and s.k % G == 0:
                    pe.wait_ge(low_ready, head(s) * 2 + 2)
                g = s.k % G
                bk = (q_bank, k_bank)[which]
                p = (s.k // G) % 2
                src = (c.n_parts, c.ctx_parts)[which]
                pe.wait_ge(bk.free, bk.nth(s.n, 0))
                if which == 0:
                    pe.wait_ge(o_bank[1].free, s.n + 1)
                for t in range(2):
                    last = product(pe, bk.ap[:, :], [part[:, p, which, t * P:(t + 1) * P] for part in w_parts],
                                   [part[:, t, g * G:(g + 1) * G, :] for part in src], start=(t == 0), stop=(t == 1))
                last.then_inc(bk.full, 1)

            def values(s):
                g = s.k % G
                pe.wait_ge(v_bank.free, s.n + 1)
                for i in range(G):
                    for t in range(2):
                        last = pe.matmul(v_bank.ap[:, i * P:(i + 1) * P], c.ctx_T[:, t, g * G + i, :],
                                         front_w(s, 2)[:, t, :], start=(t == 0), stop=(t == 1))
                last.then_inc(v_bank.full, 1)

            def scores(s):
                p = s.k % 2
                pe.wait_ge(q_bank.free, s.n + 2)
                pe.wait_ge(k_bank.free, k_bank.nth(s.n, 0) + 1)
                pe.wait_ge(s_bank.free, s_bank.nth(s.n, 0))
                for i in range(G):
                    cols = slice(i * S, (i + 1) * S)
                    last = pe.matmul(s_bank.ap[:, cols], upper_half(QT[:, p, cols]), upper_half(KT[:, p, cols]),
                                     start=True, stop=True)
                last.then_inc(s_bank.full, 1)

            def turn_shift(s):
                pe.wait_ge(max_done, s.times(OPS, 3))
                pe.wait_ge(s_bank.free, s_bank.nth(s.n, 1))
                pe.transpose(s_bank.ap[:, :].bitcast(BF16)[:, 0:P], shift[:, :], c.ident_bf[:, :])\
                    .then_inc(s_bank.full, 1)

            def scores_T(s):
                p = s.k % 2
                pe.wait_ge(s_bank.free, s_bank.nth(s.n, 1) + 1)
                pe.wait_ge(t_bank.free, t_bank.nth(s.n, 0))
                for i in range(G):
                    cols = slice(i * S, (i + 1) * S)
                    pe.matmul(t_bank.ap[:, cols], KT[:, p, cols], QT[:, p, cols], start=True, stop=False)
                    last = pe.matmul(t_bank.ap[:, cols], c.select4[:, i:i + 1].to_broadcast([P, P]), shift_T[:, p, :],
                                     start=False, stop=True)
                last.then_inc(t_bank.full, 1)

            def context(s):
                p = s.k % 2
                pe.wait_ge(v_bank.free, s.n + 2)
                pe.wait_ge(t_bank.free, t_bank.nth(s.n, 0) + 1)
                for i in range(G):
                    bk = pv_bank[i // 2]
                    if i % 2 == 0:
                        pe.wait_ge(bk.free, bk.nth(s.n, 0))
                    last = pe.matmul(bk.ap[:, (i % 2) * (P + 1):(i % 2 + 1) * (P + 1)], PT[:, i * S:(i + 1) * S],
                                     V[:, p, i, :], start=True, stop=True)
                    if i % 2 == 1:
                        last.then_inc(bk.full, 1)

            def turn_context(s):
                for bk in pv_bank:
                    pe.wait_ge(bk.free, bk.nth(s.n, 0) + 1)
                for i in range(G):
                    last = pe.transpose(pv_bank[0].ap[:, i * P:(i + 1) * P], ctx_q[:, i, :], c.ident[:, :])
                last.then_inc(pv_bank[0].full, 1)

            def output(s, t):
                wo = [part[:, (s.k // G) % 2, 2, t * P:(t + 1) * P] for part in w_parts]
                bk = o_bank[t]
                if t == 0:
                    pe.wait_ge(ctx_low_ready, s.n + 1)
                    pe.wait_ge(bk.free, s.n + 1)
                product(pe, bk.ap[:, :], wo, [part[:, :] for part in ctx_T_parts], start=True, stop=True)\
                    .then_inc(bk.full, 1)

            def period(fr, mid, bk):
                if bk is not None:
                    turn_context(bk)
                if mid is not None:
                    scores_T(mid)
                if fr is not None:
                    q_or_k(fr, 0)
                    q_or_k(fr, 1)
                if mid is not None:
                    context(mid)
                if bk is not None:
                    output(bk, 0)
                    if fr is not None:
                        pe.wait_ge(q_bank.free, fr.n + 2)
                    pe.wait_ge(o_bank[1].free, bk.n + 3)
                    output(bk, 1)
                if fr is not None:
                    scores(fr)
                    values(fr)
                    turn_shift(fr)

            pipelined3(pe, steps, 8, period)

        @block.scalar
        def _(act):
            def vectors(s):
                at = COL_AT[f"l2_bq{a}"][0]
                act.activation(head_vectors[:, (s.k // G) % 2, :, :],
                               c.cols[:, at:at + 4 * H].rearrange("p (v h) -> p v h", v=4)[:, :, bass.ds(head(s), 1)],
                               ACT.Copy).then_inc(vectors_ready, 1)
                act.wait_ge(vectors_ready, head(s) + 1)

            def vector(s, which):
                return head_vectors[:, (s.k // G) % 2, which, :]

            def q_or_k(s, which):
                bk = (q_bank, k_bank)[which]
                dst = (QT, KT)[which][:, s.k % 2, :]
                act.wait_ge(bk.full, bk.nth(s.n, 0))
                act.activation(dst, bk.ap[:, :], ACT.Identity, bias=vector(s, which),
                               scale=1.0).then_inc(bk.free, 1)

            def probs(s):
                act.wait_ge(t_bank.full, t_bank.nth(s.n, 0))
                act.activation(PT[:, :], t_bank.ap[:, :], ACT.Exp, scale=scale).then_inc(t_bank.free, 1)

            def extra(s):
                act.wait_ge(max_done, s.times(OPS, OPS))
                act.activation(extra_prob[:, s.k % 2, :], extra_arg[:, s.k % 2, :], ACT.Exp, scale=scale)\
                    .then_inc(extra_ready, 1)

            def context(s):
                act.wait_ge(pv_bank[0].full, pv_bank[0].nth(s.n, 1))
                act.activation(ctx_T_parts[0][:, :], pv_bank[0].ap[:, :], ACT.Identity, bias=vector(s, 3), scale=1.0)
                act.activation(ctx_T[:, :], pv_bank[0].ap[:, :], ACT.Identity, bias=vector(s, 3), scale=1.0)\
                    .then_inc(pv_bank[0].free, 1)

            def period(fr, mid, bk):
                if bk is not None:
                    context(bk)
                if mid is not None:
                    probs(mid)
                if fr is not None:
                    if fr.k % G == 0:
                        vectors(fr)
                    q_or_k(fr, 0)
                    q_or_k(fr, 1)
                    extra(fr)

            pipelined3(act, steps, 8, period)

        @block.vector
        def _(dve):
            dve.wait_ge(set_up, 2)

            def values(s):
                dve.wait_ge(v_bank.full, s.n + 1)
                bias = c.value_bias[:, bass.ds(head(s) * P, P)].unsqueeze(1).to_broadcast([P, G, P])
                dve.tensor_tensor(out=V[:, s.k % 2, :, 0:P], in0=v_bank.ap[:, :].rearrange("p (i d) -> p i d", i=G),
                                  in1=bias, op=ALU.add).then_inc(v_bank.free, 1)

            def maxima(s):
                g, p = s.k % G, s.k % 2
                extra = c.extra[:, head(s), g * G:(g + 1) * G]
                dve.wait_ge(s_bank.full, s_bank.nth(s.n, 0))
                dve.tensor_reduce(max_s[:, :], s_bank.ap[:, :].rearrange("p (i k) -> p i k", i=G), AX, ALU.max)\
                    .then_inc(s_bank.free, 1)
                dve.wait_ge(s_bank.free, s_bank.nth(s.n, 0) + 1)
                dve.tensor_tensor(out=max_all[:, :], in0=max_s[:, :], in1=extra, op=ALU.max).then_inc(max_done, 1)
                dve.wait_ge(max_done, s.times(OPS, 1))
                dve.tensor_scalar(out=shift[:, 0:G], in0=max_all[:, :], scalar1=-1.0, scalar2=None, op0=ALU.mult)\
                    .then_inc(max_done, 1)
                dve.wait_ge(max_done, s.times(OPS, 2))
                dve.scalar_tensor_tensor(out=shift[:, G:2 * G], in0=max_all[:, :], scalar=-1.0, in1=shift[:, 0:G],
                                         op0=ALU.mult, op1=ALU.subtract).then_inc(max_done, 1)
                dve.tensor_tensor(out=extra_arg[:, p, :], in0=extra, in1=shift[:, 0:G], op=ALU.add)\
                    .then_inc(max_done, 1)
                dve.wait_ge(max_done, s.times(OPS, 4))
                dve.tensor_tensor(out=extra_arg[:, p, :], in0=extra_arg[:, p, :], in1=shift[:, G:2 * G], op=ALU.add)\
                    .then_inc(max_done, 1)
                dve.wait_ge(max_done, s.times(OPS, 5))
                dve.sem_inc(max_done, 1)

            def turned_shift(s):
                dve.wait_ge(s_bank.full, s_bank.nth(s.n, 1))
                dve.tensor_copy(shift_T[:, s.k % 2, :], s_bank.ap[:, :].bitcast(BF16)[:, 0:P]).then_inc(s_bank.free, 1)

            def context(s):
                p = s.k % 2
                dve.wait_ge(extra_ready, s.n + 1)
                for j, bk in enumerate(pv_bank):
                    two = slice(2 * j, 2 * j + 2)
                    pv = bk.ap[:, 0:2 * (P + 1)].rearrange("p (i d) -> p i d", i=2)
                    dve.wait_ge(bk.full, bk.nth(s.n, 0))
                    dve.tensor_tensor(out=den[:, two].unsqueeze(2), in0=extra_prob[:, p, two].unsqueeze(2),
                                      in1=pv[:, :, P:P + 1], op=ALU.add).then_inc(den_done, 1)
                    dve.wait_ge(den_done, s.times(4, 2 * j + 1))
                    dve.reciprocal(rden[:, two], den[:, two]).then_inc(den_done, 1)
                    dve.wait_ge(den_done, s.times(4, 2 * j + 2))
                    dve.tensor_tensor(out=ctx_q[:, two, :], in0=pv[:, :, 0:P],
                                      in1=rden[:, two].unsqueeze(2).to_broadcast([P, 2, P]), op=ALU.mult)\
                        .then_inc(bk.free, 1)

            def output(s, t):
                g = s.k % G
                acc = c.acc[:, t, g * G:(g + 1) * G, :].rearrange("p b s -> p (b s)")
                dve.wait_ge(o_bank[t].full, s.n + 1)
                dve.tensor_tensor(out=acc, in0=acc, in1=o_bank[t].ap[:, :], op=ALU.add).then_inc(o_bank[t].free, 1)

            def period(fr, mid, bk):
                if mid is not None:
                    context(mid)
                if fr is not None:
                    maxima(fr)
                    turned_shift(fr)
                if bk is not None:
                    output(bk, 0)
                    output(bk, 1)
                if fr is not None:
                    values(fr)

            pipelined3(dve, steps, 8, period)


def build(nc, dram, out):
    c = Chip()
    c.nc, c.dram, c.out = nc, dram, out
    with ExitStack() as ctx:
        def sb(n, shape, dt=F32):
            return ctx.enter_context(nc.sbuf_tensor(n, shape, dt))

        c.x_flat = sb("x", [P, B * D])
        c.x = c.x_flat[:, :].rearrange("p (b d) -> p b d", b=B)
        c.nT_flat = sb("nT", [P, 2 * B * S])
        c.nT = c.nT_flat[:, :].rearrange("p (t b s) -> p t b s", t=2, b=B)
        c.acc_flat = sb("acc", [P, 2 * B * S])
        c.acc = c.acc_flat[:, :].rearrange("p (t b s) -> p t b s", t=2, b=B)
        c.cols = sb("cols", [P, N_COLS])
        c.rows = sb("rows", [P, N_ROWS])
        c.ident = sb("ident", [P, P])
        c.ident_bf = sb("ident_bf", [P, P], BF16)
        c.ones_bf = sb("ones_bf", [P, P], BF16)
        c.minus_half = sb("minus_half", [P, 4])
        c.epsilons = sb("epsilons", [P, 2])
        c.quarter = sb("quarter", [P, 1])
        c.one = sb("one", [P, 1])
        c.waiter = sb("waiter", [P, 1])
        c.waiter_pool = sb("waiter_pool", [P, 8])
        c.waiter_act = sb("waiter_act", [P, 8])
        c.carried = 0
        c.shapes = sb("shapes", [P, 2 * H + H + 4])
        c.select = sb("select", [P, H + 4], BF16)
        c.select16 = c.select[:, 0:H]
        c.select4 = c.select[:, H:H + 4]

        def col(name, t):
            at, n = COL_AT[name]
            return c.cols[:, at + t:at + t + 1]

        def row(name):
            return c.rows[:, ROW_AT[name]:ROW_AT[name] + ROW_LEN[name]]

        def pair(name):
            return c.rows[:, ROW_AT[name]:ROW_AT[name] + 2 * S].rearrange("p (s c) -> p s c", s=2).unsqueeze(2)\
                .to_broadcast([P, 2, 2, S])

        def head_mask(dim):
            return c.shapes[:, 0:H] if dim == 8 else c.shapes[:, H:2 * H]

        c.col, c.row, c.pair, c.head_mask = col, row, pair, head_mask
        c.w = {}
        c.lasting = lambda n: ctx.enter_context(nc.semaphore(n))
        c.l1_loaded = c.lasting("l1_weights_loaded")
        c.l2_loaded = c.lasting("l2_loaded")
        c.l3_loaded = c.lasting("l3_weights_loaded")

        def load_layer2(sync):
            load_weights(sync, c, WEIGHTS_2, c.l2_loaded)
            for t in range(2):
                tile = dram["ctx_T"][:, t * P:(t + 1) * P, :].rearrange("b p s -> p b s")
                sync.dma_start(c.ctx_T[:, t, :, :], tile).then_inc(c.l2_loaded, 16)

        with ExitStack() as early:
            for name in WEIGHTS_01:
                c.w[name] = early.enter_context(nc.sbuf_tensor(name, list(WEIGHTS_01[name]), F32))
            with nc.sbuf_tensor("pos", [P, 4, P], F32) as pos:
                c.pos = pos
                load_constants(c)
                narrow_attention(c, LAYER0)
            mlp(c, "l0_mlp", c.w["l0_w1"], "l0_b1", c.w["l0_w2"], ACT.Gelu, P, 2 * P, "channels")
            narrow_attention(c, LAYER1)
            for name in WEIGHTS_2:
                c.w[name] = ctx.enter_context(nc.sbuf_tensor(name, list(WEIGHTS_2[name]), F32, side="right"))
            c.ctx_T_flat = ctx.enter_context(nc.sbuf_tensor("ctx_T_all", [P, 2 * B * S], F32, side="right"))
            c.ctx_T = c.ctx_T_flat[:, :].rearrange("p (t b s) -> p t b s", t=2, b=B)
            mlp(c, "l1_mlp", c.w["l1_w1"], "l1_b1", c.w["l1_w2"], ACT.Gelu_apprx_tanh, D, FF, "l1_b2", load_layer2)
        with ExitStack() as late:
            with ExitStack() as two:
                shape = [P, 2, B, S]
                c.ctx_parts = [two.enter_context(nc.sbuf_tensor(f"ctx_{n}", shape, F32R)) for n in ("high", "low")]
                c.n_parts = [two.enter_context(nc.sbuf_tensor(f"n_{n}", shape, F32R)) for n in ("high", "low")]
                c.extra = two.enter_context(nc.sbuf_tensor("extra", [P, H, B], F32))
                c.value_bias = two.enter_context(nc.sbuf_tensor("value_bias", [P, H * P], F32))
                for a in (1, 2):
                    norm_transposed(c, f"l2_norm{a}", f"l2_ln{a}_g", f"l2_ln{a}_b",
                                    add="l2_bo1" if a == 2 else None, ahead_of=a)
                    wide_heads(c, a)
                norm_transposed(c, "l2_norm3", "l2_lnm_g", "l2_lnm_b", add="l2_bo2")
            for name in WEIGHTS_3:
                c.w[name] = late.enter_context(nc.sbuf_tensor(name, list(WEIGHTS_3[name]), F32))
            mlp(c, "l2_mlp", c.w["l2_w1"], "l2_b1", c.w["l2_w2"], ACT.Gelu, D, FF, "l2_b2",
                lambda sync: load_weights(sync, c, WEIGHTS_3, c.l3_loaded))
            narrow_attention(c, LAYER3_SELF)
            narrow_attention(c, LAYER3_CROSS)
            norm_transposed(c, "l3_norm3", "l3_ln3_g", "l3_ln3_b")
            mlp(c, "l3_mlp", c.w["l3_w1"], "l3_b1", c.w["l3_w2"], ACT.Gelu_apprx_tanh, D, FF, "l3_b2")


WEIGHTS_01 = {
    "l0_wq": (P, 1, P), "l0_wk": (P, 1, P), "l0_wv": (P, 1, P), "l0_wo": (P, 1, P),
    "l0_w1": (P, 1, 2 * P), "l0_w2": (P, 2, P),
    "l1_wq": (P, 2, D), "l1_wk": (P, 2, D), "l1_wv": (P, 2, D), "l1_wo": (P, 2, D),
    "l1_w1": (P, 2, FF), "l1_w2": (P, 8, D),
}
LAYER1_WEIGHTS = [name for name in WEIGHTS_01 if name.startswith("l1")]
WEIGHTS_2 = {"l2_w1": (P, 2, FF), "l2_w2": (P, 8, D)}
WEIGHTS_3 = {
    "l3_wq": (P, 2, D), "l3_wk": (P, 2, D), "l3_wv": (P, 2, D), "l3_wao": (P, 2, D),
    "l3_wqc": (P, 2, D), "l3_wkc": (P, 2, D), "l3_wvc": (P, 2, D), "l3_wco": (P, 2, D),
    "l3_w1": (P, 2, FF), "l3_w2": (P, 8, D),
}


def positions():
    pos = np.arange(2 * P, dtype=np.float32)[:, None]
    div = np.exp(np.arange(0, P, 2, dtype=np.float32) * np.float32(-np.log(10000.0) / P)).astype(np.float32)
    ang = (pos * div).astype(np.float32)
    pe = np.zeros((2 * P, P), np.float32)
    pe[:, 0::2], pe[:, 1::2] = np.sin(ang), np.cos(ang)
    return pe


def laid_out(i):
    g = {k: np.asarray(v) for k, v in i.items()}
    a = {}
    a["x_T"] = g["x"].transpose(0, 2, 1)
    a["ctx_T"] = g["ctx_2048"].transpose(0, 2, 1)
    a["mask"] = g["mask_BxS2_ik0"]
    a["mask_T"] = g["mask_BxS2_ik0"].T
    m = g["mask_1x1xSxS2_fc1"][0, 0]
    a["self_mask"] = np.stack([m, m.T])
    m = g["mask_Bx1xSxS2_ff1"][:, 0]
    a["cross_mask"] = np.stack([m, m.transpose(0, 2, 1)], 1)

    def tiles(w):
        return w.reshape(-1, P, w.shape[1]).transpose(1, 0, 2)

    kv_w = g["L1_xattn_kv_w"].reshape(D, D, 2)
    kv_b = g["L1_xattn_kv_b"].reshape(D, 2)
    qkv, kvc = g["L3_xattn_w_qkv"], g["L3_xattn_w_kv"]
    b_qkv, b_kvc = g["L3_xattn_b_qkv"], g["L3_xattn_b_kv"]
    w = {
        "l0_wq": g["L0_xattn_Wq"], "l0_wk": g["L0_xattn_Wk"], "l0_wv": g["L0_xattn_Wv"], "l0_wo": g["L0_xattn_Wo"],
        "l0_w1": g["L0_xattn_W1"], "l0_w2": g["L0_xattn_W2"],
        "l1_wq": g["L1_xattn_q_w"], "l1_wk": kv_w[:, :, 0], "l1_wv": kv_w[:, :, 1], "l1_wo": g["L1_xattn_out_w"],
        "l1_w1": g["L1_xattn_mlp_w1"], "l1_w2": g["L1_xattn_mlp_w2"],
        "l2_w1": g["L2_xattn_w_fc1"], "l2_w2": g["L2_xattn_w_fc2"],
        "l3_wq": qkv[:, 0:D], "l3_wk": qkv[:, D:2 * D], "l3_wv": qkv[:, 2 * D:], "l3_wao": g["L3_xattn_w_ao"],
        "l3_wqc": g["L3_xattn_w_q"], "l3_wkc": kvc[:, 0:D], "l3_wvc": kvc[:, D:], "l3_wco": g["L3_xattn_w_co"],
        "l3_w1": g["L3_xattn_w1"], "l3_w2": g["L3_xattn_w2"],
    }
    for name, x in w.items():
        a[name] = tiles(x)
    vec = {
        "l0_ffn_g": g["L0_xattn_ffn_ln_g"], "l0_ffn_b": g["L0_xattn_ffn_ln_b"], "l0_b1": g["L0_xattn_b1"],
        "l0_b2": g["L0_xattn_b2"],
        "l1_q_b": g["L1_xattn_q_b"], "l1_k_b": kv_b[:, 0], "l1_v_b": kv_b[:, 1], "l1_post": g["L1_xattn_postnorm_w"],
        "l1_b1": g["L1_xattn_mlp_b1"],
        "l2_lnm_g": g["L2_xattn_ln_mlp_scale"], "l2_lnm_b": g["L2_xattn_ln_mlp_offset"], "l2_b1": g["L2_xattn_b_fc1"],
        "l3_ln1_g": g["L3_xattn_ln1_s"], "l3_ln1_b": g["L3_xattn_ln1_b"],
        "l3_q_b1": b_qkv[0:D], "l3_k_b1": b_qkv[D:2 * D], "l3_v_b1": b_qkv[2 * D:],
        "l3_ln2_g": g["L3_xattn_ln2_s"], "l3_ln2_b": g["L3_xattn_ln2_b"],
        "l3_q_b2": g["L3_xattn_b_q"], "l3_k_b2": b_kvc[0:D], "l3_v_b2": b_kvc[D:],
        "l3_ln3_g": g["L3_xattn_ln3_s"], "l3_ln3_b": g["L3_xattn_ln3_b"], "l3_b1": g["L3_xattn_b1"],
    }
    for n in (1, 2):
        vec[f"l2_ln{n}_g"] = g[f"L2_xattn_ln{n}_scale"]
        vec[f"l2_ln{n}_b"] = g[f"L2_xattn_ln{n}_offset"]
        for v in ("bq", "bk", "bias_k", "bias_v", "bo"):
            vec[f"l2_{v}{n}"] = g[f"L2_xattn_{v}{n}"].reshape(-1)
        a[f"l2_wq_T{n}"] = g[f"L2_xattn_wq{n}"].reshape(D, H, P).transpose(2, 1, 0)
        a[f"l2_rows{n}"] = np.stack([g[f"L2_xattn_{v}{n}"].reshape(-1) for v in ("bv", "bias_v")])
        by_head = [g[f"L2_xattn_w{v}{n}"].reshape(2, P, H, P).transpose(2, 1, 0, 3).reshape(H, P, D) for v in "qkv"]
        a[f"l2_heads{n}"] = np.stack(by_head + [g[f"L2_xattn_wo{n}"].reshape(H, P, D)], 1)
    a["cols"] = np.concatenate([vec[name].reshape(n, P) for name, n in COLUMNS]).T
    rows = {
        "l0_q_g": g["L0_xattn_ln_q_g"], "l0_kv_g": g["L0_xattn_ln_kv_g"],
        "l0_q_b": g["L0_xattn_ln_q_b"], "l0_kv_b": g["L0_xattn_ln_kv_b"],
        "l1_out_b": g["L1_xattn_out_b"], "l1_b2": g["L1_xattn_mlp_b2"], "l2_b2": g["L2_xattn_b_fc2"],
        "l3_ao_b": g["L3_xattn_b_ao"], "l3_co_b": g["L3_xattn_b_co"], "l3_b2": g["L3_xattn_b2"],
    }
    a["rows"] = np.concatenate([rows[name] for name in ROWS])
    pe = positions().reshape(2, P, P).transpose(1, 0, 2)
    a["pos"] = np.concatenate([pe, pe], 1)
    p, h = np.arange(P)[:, None], np.arange(H)[None, :]
    n4 = np.arange(4)[None, :]
    a["shapes"] = np.concatenate([p // 8 == h, p // 16 == h % 8, (p < 32) & (p % 16 == h), (p < 8) & (p % 4 == n4)],
                                 1).astype(np.float32)
    return {k: np.ascontiguousarray(v) for k, v in a.items()}


def kernel(**inputs):
    import concourse.bacc as bacc
    from concourse.bass_utils import run_bass_kernel_spmd

    nc = bacc.Bacc("TRN2", target_bir_lowering=False, num_devices=1)
    arrays = laid_out(inputs)
    dram = {k: nc.dram_tensor(f"in_{k}", v.shape, mybir.dt.from_np(v.dtype), kind="ExternalInput").ap()
            for k, v in arrays.items()}
    out = nc.dram_tensor("out", (B, S, D), F32, kind="ExternalOutput").ap()
    build(nc, dram, out)
    result = run_bass_kernel_spmd(nc, [{f"in_{k}": v for k, v in arrays.items()}], core_ids=[0])
    return result.results[0]["out"]
```
